# Optimizing a Trainium2 kernel written in Bass

```python
import numpy as np
import jax
import jax.numpy as jnp

def _softmax(x, axis=-1):
    return jax.nn.softmax(x, axis=axis)
def _gelu(x):
    return jax.nn.gelu(x, approximate=True)
def _silu(x):
    return jax.nn.silu(x)
def _sigmoid(x):
    return jax.nn.sigmoid(x)
def _layernorm(x, axis=-1, eps=1e-5):
    m = jnp.mean(x, axis=axis, keepdims=True)
    v = jnp.var(x, axis=axis, keepdims=True)
    return (x - m) / jnp.sqrt(v + eps)
def _scatter_add(tgt, idx, src, axis=0):
    return tgt.at[idx].add(src)
def _segment_sum(src, seg, n):
    return jax.ops.segment_sum(src, seg, n)

kernel_name = 'mk_conv_preact_d4_conv_nchw64_23991b'

def setup_inputs(seed: int = 0):
    np.random.seed(seed)
    _w = jnp.asarray
    def _rec_inputs():
        import jax
        import jax.numpy as jnp
        _gk = jax.random.key(seed)
        x = -7.109e-05 + 0.9999 * jax.random.normal(jax.random.fold_in(_gk, 1), (8, 64, 256, 256), jnp.float32)
        return x
    x = _rec_inputs()
    def _L0_conv_setup():
        import jax, jax.numpy as jnp
        import numpy as np
        IN_C, OUT_C, MX, MY = (64, 64, 32, 32)
        B, H, W = (16, 256, 256)
        key = jax.random.key(seed)
        k1, k2, k3 = jax.random.split(key, 3)
        scale = 1.0 / (IN_C * OUT_C)
        x = jax.random.normal(k1, (B, IN_C, H, W), dtype=jnp.float32)
        weight_real = scale * jax.random.normal(k2, (IN_C, OUT_C, MX, MY), dtype=jnp.float32)
        weight_imag = scale * jax.random.normal(k3, (IN_C, OUT_C, MX, MY), dtype=jnp.float32)
        return {'x': x, 'weight_real': weight_real, 'weight_imag': weight_imag}
    _L0_conv_all = _L0_conv_setup()
    _L0_conv_in = {k: v for k, v in _L0_conv_all.items() if k in ('weight_real', 'weight_imag', )}
    del _L0_conv_all

    def _L1_conv_setup():
        import jax, jax.numpy as jnp
        import numpy as np
        from jax import lax
        GROUPS = 4
        DILATIONS = (1, 6, 12, 18)
        PADDINGS = (1, 6, 12, 18)
        key = jax.random.key(seed)
        k1, k2, k3 = jax.random.split(key, 3)
        x = jax.random.normal(k1, (8, 64, 320, 320), dtype=jnp.float32)
        weight = jax.random.normal(k2, (64, 16, 3, 3), dtype=jnp.float32) * 0.05
        bias = jax.random.normal(k3, (64,), dtype=jnp.float32) * 0.05
        return {'x': x, 'weight': weight, 'bias': bias}
    _L1_conv_all = _L1_conv_setup()
    _L1_conv_in = {k: v for k, v in _L1_conv_all.items() if k in ('weight', 'bias', )}
    del _L1_conv_all

    def _L2_conv_setup():
        import jax, jax.numpy as jnp
        from jax import lax
        import numpy as np
        B, C, H, W = (16, 64, 256, 256)
        K = 7
        key = jax.random.key(seed)
        kx, kk = jax.random.split(key)
        x = jax.random.normal(kx, (B, C, H, W), dtype=jnp.float32)
        kernel = jax.random.normal(kk, (K, K), dtype=jnp.float32)
        return {'x': x, 'kernel': kernel}
    _L2_conv_all = _L2_conv_setup()
    _L2_conv_in = {k: v for k, v in _L2_conv_all.items() if k in ('kernel', )}
    del _L2_conv_all

    def _L3_conv_setup():
        import jax, jax.numpy as jnp
        from jax import lax
        import numpy as np
        PATCH = 8
        key = jax.random.key(seed)
        ks = jax.random.split(key, 5)
        dim, hidden = (64, 192)
        c2 = hidden * 2
        x = jax.random.normal(ks[0], (4, dim, 256, 256), dtype=jnp.float32)
        w_in = jax.random.normal(ks[1], (c2, dim), dtype=jnp.float32) * (1.0 / np.sqrt(dim))
        w_dw = jax.random.normal(ks[2], (c2, 1, 3, 3), dtype=jnp.float32) * (1.0 / 3.0)
        fft_filter = jnp.ones((c2, 1, 1, PATCH, PATCH // 2 + 1), dtype=jnp.float32)
        w_out = jax.random.normal(ks[3], (dim, hidden), dtype=jnp.float32) * (1.0 / np.sqrt(hidden))
        return {'x': x, 'w_in': w_in, 'w_dw': w_dw, 'fft_filter': fft_filter, 'w_out': w_out}
    _L3_conv_all = _L3_conv_setup()
    _L3_conv_in = {k: v for k, v in _L3_conv_all.items() if k in ('w_in', 'w_dw', 'fft_filter', 'w_out', )}
    del _L3_conv_all

    return {
        "x": x,
        "L0_conv_weight_real": _L0_conv_in["weight_real"],
        "L0_conv_weight_imag": _L0_conv_in["weight_imag"],
        "L1_conv_weight": _L1_conv_in["weight"],
        "L1_conv_bias": _L1_conv_in["bias"],
        "L2_conv_kernel": _L2_conv_in["kernel"],
        "L3_conv_w_in": _L3_conv_in["w_in"],
        "L3_conv_w_dw": _L3_conv_in["w_dw"],
        "L3_conv_fft_filter": _L3_conv_in["fft_filter"],
        "L3_conv_w_out": _L3_conv_in["w_out"],
    }

def reference(x, L0_conv_weight_real, L0_conv_weight_imag, L1_conv_weight, L1_conv_bias, L2_conv_kernel, L3_conv_w_in, L3_conv_w_dw, L3_conv_fft_filter, L3_conv_w_out):
    import jax
    import jax.numpy as jnp
    def _L0_conv_ref(x, weight_real, weight_imag):
        import jax, jax.numpy as jnp
        import numpy as np
        IN_C, OUT_C, MX, MY = (64, 64, 32, 32)
        B, H, W = (16, 256, 256)
        Bv, C, Hv, Wv = x.shape
        x_ft = jnp.fft.rfft2(x, norm='ortho')
        mx = min(MX, Hv)
        my = min(MY, Wv // 2 + 1)
        x_crop = x_ft[:, :, :mx, :my]
        w = (weight_real[:, :, :mx, :my] + 1j * weight_imag[:, :, :mx, :my]).astype(jnp.complex64)
        out_modes = jnp.einsum('bixy,ioxy->boxy', x_crop, w)
        out_ft = jnp.zeros((Bv, OUT_C, Hv, Wv // 2 + 1), dtype=jnp.complex64)
        out_ft = out_ft.at[:, :, :mx, :my].set(out_modes)
        return jnp.fft.irfft2(out_ft, s=(Hv, Wv), norm='ortho')

    def _L1_conv_ref(x, weight, bias):
        import jax, jax.numpy as jnp
        import numpy as np
        from jax import lax
        GROUPS = 4
        DILATIONS = (1, 6, 12, 18)
        PADDINGS = (1, 6, 12, 18)
        b, c, h, w = x.shape
        out_ch = weight.shape[0]
        xg = x.reshape(b, GROUPS, c // GROUPS, h, w)
        wg = weight.reshape(GROUPS, out_ch // GROUPS, weight.shape[1], 3, 3)
        dn = lax.conv_dimension_numbers(xg[:, 0].shape, wg[0].shape, ('NCHW', 'OIHW', 'NCHW'))
        outs = []
        for g in range(GROUPS):
            p, d = (PADDINGS[g], DILATIONS[g])
            outs.append(lax.conv_general_dilated(xg[:, g], wg[g], window_strides=(1, 1), padding=[(p, p), (p, p)], rhs_dilation=(d, d), dimension_numbers=dn))
        out = jnp.concatenate(outs, axis=1)
        return out + bias[None, :, None, None]

    def _L2_conv_ref(x, kernel):
        import jax, jax.numpy as jnp
        from jax import lax
        import numpy as np
        B, C, H, W = (16, 64, 256, 256)
        K = 7
        c = x.shape[1]
        kflip = jnp.flip(kernel, axis=(0, 1))
        w = jnp.tile(kflip[None, None], (c, 1, 1, 1))
        y = lax.conv_general_dilated(x, w, window_strides=(1, 1), padding='SAME', feature_group_count=c, dimension_numbers=('NCHW', 'OIHW', 'NCHW'))
        return y * jnp.tanh(jax.nn.softplus(y))

    def _L3_conv_ref(x, w_in, w_dw, fft_filter, w_out):
        import jax, jax.numpy as jnp
        from jax import lax
        import numpy as np
        PATCH = 8
        p = PATCH
        x = jnp.einsum('bchw,oc->bohw', x, w_in)
        B, C, H, W = x.shape
        xp = x.reshape(B, C, H // p, p, W // p, p).transpose(0, 1, 2, 4, 3, 5)
        xf = jnp.fft.rfft2(xp) * fft_filter
        xp = jnp.fft.irfft2(xf, s=(p, p))
        x = xp.transpose(0, 1, 2, 4, 3, 5).reshape(B, C, H, W)
        x = lax.conv_general_dilated(x, w_dw, window_strides=(1, 1), padding=[(1, 1), (1, 1)], feature_group_count=C)
        x1, x2 = jnp.split(x, 2, axis=1)
        x = jax.nn.gelu(x1, approximate=False) * x2
        return jnp.einsum('bchw,oc->bohw', x, w_out)

    def _gn(v, G=32, eps=1e-5):
        B_, C_, H_, W_ = v.shape
        g = v.reshape(B_, G, C_ // G, H_, W_)
        m = jnp.mean(g, axis=(2, 3, 4), keepdims=True)
        s = jnp.var(g, axis=(2, 3, 4), keepdims=True)
        return ((g - m) / jnp.sqrt(s + eps)).reshape(v.shape)

    def _ln_c(v, eps=1e-6):
        m = jnp.mean(v, axis=1, keepdims=True)
        s = jnp.var(v, axis=1, keepdims=True)
        return (v - m) / jnp.sqrt(s + eps)

    def _ln_t(v, eps=1e-5):
        m = jnp.mean(v, axis=-1, keepdims=True)
        s = jnp.var(v, axis=-1, keepdims=True)
        return (v - m) / jnp.sqrt(s + eps)

    def _to_tokens(v):
        B_, C_, H_, W_ = v.shape
        return v.reshape(B_, C_, H_ * W_).transpose(0, 2, 1)
    def _from_tokens(t, like):
        B_, C_, H_, W_ = like.shape
        return t.transpose(0, 2, 1).reshape(B_, C_, H_, W_)

    x = x + _L0_conv_ref(_gn(x), L0_conv_weight_real, L0_conv_weight_imag)
    x = x + _L1_conv_ref(_gn(x), L1_conv_weight, L1_conv_bias)
    x = x + _L2_conv_ref(_gn(x), L2_conv_kernel)
    x = x + _L3_conv_ref(_gn(x), L3_conv_w_in, L3_conv_w_dw, L3_conv_fft_filter, L3_conv_w_out)
    return x


_drawn_inputs = setup_inputs


def setup_inputs(seed=0):
    import zlib

    import numpy as np

    out = dict(_drawn_inputs(seed))
    spreads = {'L3_conv_fft_filter': (1.0, 0.2)}
    factors = {'L0_conv_weight_real': 64.0, 'L0_conv_weight_imag': 64.0}
    for name, (base, spread) in spreads.items():
        noise = np.random.default_rng([zlib.crc32(name.encode()), seed]).standard_normal(out[name].shape)
        drawn = base * np.exp(spread * noise) if base else spread * noise
        out[name] = jnp.asarray(drawn.astype(out[name].dtype))
    for name, factor in factors.items():
        out[name] = (out[name] * factor).astype(out[name].dtype)
    return out
```

```python
import numpy as np
import concourse.bass as bass
from concourse import mybir
from contextlib import ExitStack

FP32 = mybir.dt.float32
ALU = mybir.AluOpType
ACT = mybir.ActivationFunctionType

C, H, W = 64, 256, 256
P = 128
GROUPS = 32
MODES = 32
EPS = 1e-5
BANK = 512
CT = 8
NT = C // CT


class Stage:

    def __init__(self, nc, name):
        self.nc, self.name, self.stack = nc, name, ExitStack()

    def __enter__(self):
        self.stack.__enter__()
        return self

    def __exit__(self, *exc):
        return self.stack.__exit__(*exc)

    def sbuf(self, name, shape):
        return self.stack.enter_context(self.nc.sbuf_tensor(f"{self.name}_{name}", shape, FP32))

    def psum(self, name, shape):
        return self.stack.enter_context(self.nc.psum_tensor(f"{self.name}_{name}", shape, FP32))

    def sem(self, name):
        return self.stack.enter_context(self.nc.semaphore(f"{self.name}_{name}"))

    def block(self):
        return self.stack.enter_context(self.nc.Block())


def finish_statistics(nc, name, moments, n, averager, stores):
    with Stage(nc, name) as s:
        avg = s.sbuf("avg", [P, P])
        mean = s.sbuf("mean", [P, n])
        spread = s.sbuf("spread", [P, n])
        var = s.sbuf("var", [P, n])
        root = s.sbuf("root", [P, n])
        rstd = s.sbuf("rstd", [P, n])
        result = s.sbuf("result", [P, n, 2])
        mean_ps = s.psum("mean_ps", [P, BANK])
        var_ps = s.psum("var_ps", [P, BANK])
        avg_loaded = s.sem("avg_loaded")
        averaged = s.sem("averaged")
        step = s.sem("step")
        spread_ready = s.sem("spread_ready")
        var_ready = s.sem("var_ready")
        root_ready = s.sem("root_ready")
        result_ready = s.sem("result_ready")
        stored = s.sem("stored")
        pairs = stores(result)
        block = s.block()

        @block.sync
        def _(sp):
            sp.dma_start(avg[:, :], averager).then_inc(avg_loaded, 16)
            sp.wait_ge(result_ready, 1)
            for dst, src in pairs:
                sp.dma_start(dst, src).then_inc(stored, 16)
            sp.wait_ge(stored, 16 * len(pairs))

        @block.tensor
        def _(pe):
            pe.wait_ge(avg_loaded, 16)
            nc.tensor.matmul(mean_ps[:, 0:n], avg[:, :], moments[:, :, 0], start=True, stop=True).then_inc(averaged, 1)
            pe.wait_ge(spread_ready, 1)
            nc.tensor.matmul(var_ps[:, 0:n], avg[:, :], spread[:, :], start=True, stop=True).then_inc(averaged, 1)

        @block.scalar
        def _(act):
            act.wait_ge(var_ready, 1)
            nc.scalar.activation(root[:, :], var[:, :], ACT.Sqrt).then_inc(root_ready, 1)

        @block.vector
        def _(dve):
            done = [0]

            def chained(instruction):
                done[0] += 1
                instruction.then_inc(step, 1)
                dve.wait_ge(step, done[0])

            dve.wait_ge(averaged, 1)
            chained(nc.vector.tensor_copy(mean[:, :], mean_ps[:, 0:n]))
            chained(nc.vector.tensor_tensor(spread[:, :], moments[:, :, 0], mean[:, :], ALU.subtract))
            chained(nc.vector.tensor_tensor(spread[:, :], spread[:, :], spread[:, :], ALU.mult))
            nc.vector.tensor_tensor(spread[:, :], spread[:, :], moments[:, :, 1], ALU.add).then_inc(spread_ready, 1)
            dve.wait_ge(averaged, 2)
            nc.vector.tensor_scalar(var[:, :], var_ps[:, 0:n], EPS, None, ALU.add).then_inc(var_ready, 1)
            dve.wait_ge(root_ready, 1)
            chained(nc.vector.reciprocal(rstd[:, :], root[:, :]))
            chained(nc.vector.tensor_tensor(root[:, :], rstd[:, :], rstd[:, :], ALU.mult))
            chained(nc.vector.tensor_tensor(root[:, :], root[:, :], var[:, :], ALU.mult))
            chained(nc.vector.tensor_scalar(root[:, :], root[:, :], -0.5, 1.5, ALU.mult, ALU.add))
            chained(nc.vector.tensor_tensor(result[:, :, 0], rstd[:, :], root[:, :], ALU.mult))
            nc.vector.scalar_tensor_tensor(result[:, :, 1], mean[:, :], -1.0, result[:, :, 0],
                                           ALU.mult, ALU.mult).then_inc(result_ready, 1)


def row_layout_stores(stats_dram, B):
    def stores(result):
        src = result[0:1, :, :].rearrange("p (b g) k -> p b g k", b=B)
        dst = stats_dram.rearrange("b (g t) k -> t b g k", t=2)
        return [(dst[t:t + 1, b, :, :], src[:, b, :, :]) for t in range(2) for b in range(B)]
    return stores


def spectral_forward(nc, x, consts, moments, modes_in, B):
    K2 = 2 * MODES
    with Stage(nc, "fwd") as s:
        x_tile = [s.sbuf(f"x{i}", [P, 2, CT, W]) for i in range(2)]
        f_rows = s.sbuf("f_rows", [P, 2, K2])
        f_cols = s.sbuf("f_cols", [P, 2, 2, K2])
        col_modes = s.sbuf("col_modes", [P, 2, K2, C])
        stats = [s.sbuf(f"stats{i}", [P, CT // 2, 2, 6]) for i in range(2)]
        image_moments = s.sbuf("image_moments", [P, GROUPS, 2])
        rows_ps = [s.psum(f"rows_ps{i}", [P, 2, CT, K2]) for i in range(2)]
        QN = 4
        KQ = MODES // QN
        modes_ps = [s.psum(f"modes_ps{i}", [C, KQ, K2]) for i in range(QN)]
        consts_loaded = s.sem("consts_loaded")
        x_loaded = [s.sem(f"x_loaded{i}") for i in range(2)]
        x_transformed = s.sem("x_transformed")
        x_measured = s.sem("x_measured")
        cols_ready = s.sem("cols_ready")
        modes_done = s.sem("modes_done")
        modes_free = s.sem("modes_free")
        may_aggregate = s.sem("may_aggregate")
        aggregated = s.sem("aggregated")
        block = s.block()

        @block.sync
        def _(sp):
            sp.dma_start(f_rows[:, :, :], consts["f_rows"]).then_inc(consts_loaded, 16)
            sp.dma_start(f_cols[:, :, :, :], consts["f_cols"]).then_inc(consts_loaded, 16)

            def load(b, t):
                for half in range(2):
                    src = x[b, t * CT:(t + 1) * CT, half * P:(half + 1) * P, :].rearrange("c h w -> h c w")
                    sp.dma_start(x_tile[t % 2][:, half, :, :], src).then_inc(x_loaded[t % 2], 16)

            with sp.Fori(0, B) as b:
                for t in range(NT):
                    sp.wait_ge(x_transformed, b * NT + t + 1)
                    sp.wait_ge(x_measured, b * NT + t + 1)
                    load(b, t)

        @block.tensor
        def _(pe):
            nc.tensor.sem_inc(x_transformed, 2)
            pe.wait_ge(consts_loaded, 32)
            with pe.Fori(0, B) as b:
                for t in range(NT):
                    pe.wait_ge(x_loaded[t % 2], b * (32 * NT // 2) + 32 * (t // 2 + 1))
                    pe.wait_ge(cols_ready, b * NT + t + 1)
                    for half_w in range(2):
                        for c in range(CT):
                            for half in range(2):
                                last = nc.tensor.matmul(
                                    rows_ps[t % 2][:, half_w, c, :],
                                    x_tile[t % 2][:, half, c, half_w * P:(half_w + 1) * P],
                                    f_rows[:, half, :], start=(half == 0), stop=(half == 1))
                    last.then_inc(x_transformed, 1)
                pe.wait_ge(cols_ready, b * NT + NT + 2)
                for q in range(QN):
                    pe.wait_ge(modes_free, b * QN + q + 1)
                    for k in range(KQ):
                        kx = q * KQ + k
                        n = 0
                        for half_w in range(2):
                            for part in range(2):
                                last = nc.tensor.matmul(
                                    modes_ps[q][:, k, :], col_modes[:, half_w, part * MODES + kx, :],
                                    f_cols[:, half_w, part, :], start=(n == 0), stop=(n == 3))
                                n += 1
                    last.then_inc(modes_done, 1)
            

        @block.scalar
        def _(act):
            nc.scalar.sem_inc(cols_ready, 2)
            with act.Fori(0, B) as b:
                act.wait_ge(modes_done, b * QN)
                for t in range(NT):
                    act.wait_ge(x_transformed, b * NT + t + 3)
                    for half_w in range(2):
                        last = nc.scalar.activation(
                            col_modes[:, half_w, :, t * CT:(t + 1) * CT].rearrange("p k c -> p c k"),
                            rows_ps[t % 2][:, half_w, :, :], ACT.Copy)
                    last.then_inc(cols_ready, 1)

        @block.vector
        def _(dve):
            nc.vector.sem_inc(x_measured, 2)
            nc.vector.sem_inc(modes_free, QN)
            mo = moments[:, :, :].rearrange("p (b g) k -> p b g k", b=B)
            with dve.Fori(0, B) as b:
                for t in range(NT):
                    dve.wait_ge(x_loaded[t % 2], b * (32 * NT // 2) + 32 * (t // 2 + 1))
                    for j in range(CT // 2):
                        for half in range(2):
                            last = nc.vector.bn_stats(stats[t % 2][:, j, half, :],
                                                      x_tile[t % 2][:, half, 2 * j:2 * j + 2, :])
                    last.then_inc(x_measured, 1)
                    dve.wait_ge(x_measured, b * NT + t + 3)
                    nc.vector.sem_inc(may_aggregate, 1)
                    for j in range(CT // 2):
                        last = nc.vector.bn_aggr(image_moments[:, t * CT // 2 + j, :], stats[t % 2][:, j, :, :])
                last.then_inc(aggregated, 1)
                dve.wait_ge(aggregated, b + 1)
                nc.vector.tensor_copy(mo[:, b, :, :], image_moments[:, :, :])
                for q in range(QN):
                    dve.wait_ge(modes_done, b * QN + q + 1)
                    re = modes_ps[q][:, :, 0:MODES]
                    im = modes_ps[q][:, :, MODES:K2]
                    dst = modes_in[:, q * KQ:(q + 1) * KQ, :, :]
                    nc.vector.tensor_copy(dst[0:C, :, :, b], re)
                    nc.vector.tensor_scalar(dst[C:P, :, :, b], im, -1.0, None, ALU.mult)
                    nc.vector.tensor_copy(dst[0:C, :, :, B + b], im)
                    nc.vector.tensor_copy(dst[C:P, :, :, B + b], re).then_inc(modes_free, 1)


def spectral_mix(nc, w_real, w_imag, stats_dram, modes_in, modes_out, B):
    MC = 4 * MODES
    NCH = MODES * MODES // MC
    MB = BANK // C
    NB = MC // MB
    with Stage(nc, "mix") as s:
        norm = s.sbuf("norm", [P, B, 2])
        scale = s.sbuf("scale", [P, 2, B])
        shift = s.sbuf("shift", [P, B])
        w = [s.sbuf(f"w{i}", [P, C, MC]) for i in range(2)]
        chunk = [s.sbuf(f"chunk{i}", [P, MC, 2 * B]) for i in range(2)]
        mixed = s.sbuf("mixed", [2 * B, MC, C])
        mixed_ps = [s.psum(f"mixed_ps{i}", [2 * B, MB, C]) for i in range(8)]
        norm_loaded = s.sem("norm_loaded")
        w_loaded = [s.sem(f"w_loaded{i}") for i in range(2)]
        step = s.sem("step")
        normalised = s.sem("normalised")
        chunk_ready = s.sem("chunk_ready")
        chunk_mixed = s.sem("chunk_mixed")
        bank_mixed = s.sem("bank_mixed")
        bank_free = s.sem("bank_free")
        may_store = s.sem("may_store")
        out_stored = s.sem("out_stored")
        block = s.block()
        flat_in = modes_in[:, :, :, :].rearrange("p x y n -> p (x y) n")

        @block.sync
        def _(sp):
            for half in range(2):
                sp.dma_start(norm[half * C:(half + 1) * C, :, :],
                             stats_dram.rearrange("b c k -> c b k")).then_inc(norm_loaded, 16)
            with sp.Fori(0, NCH // 2) as pair:
                for i in range(2):
                    sp.wait_ge(chunk_mixed, pair * 2 + i + 1)
                    for half, src in enumerate((w_real, w_imag)):
                        sp.dma_start(w[i][half * C:(half + 1) * C, :, :],
                                     src.rearrange("c o x y -> c o (x y)")[:, :, bass.ds((pair * 2 + i) * MC, MC)]
                                     ).then_inc(w_loaded[i], 16)

        @block.gpsimd
        def _(pool):
            with pool.Fori(0, NCH) as ch:
                pool.wait_ge(bank_free, ch * NB + NB + 8)
                nc.gpsimd.sem_inc(may_store, 1)
                pool.dma_start(modes_out[:, bass.ds(ch * MC, MC), :], mixed[:, :, :]).then_inc(out_stored, 16)
            pool.wait_ge(out_stored, 16 * NCH)

        @block.scalar
        def _(act):
            act.wait_ge(normalised, 1)
            with act.Fori(0, NCH // 2) as pair:
                for i in range(2):
                    act.wait_ge(chunk_mixed, pair * 2 + i + 1)
                    nc.scalar.activation(chunk[i][:, :, :], flat_in[:, bass.ds((pair * 2 + i) * MC, MC), :],
                                         ACT.Copy).then_inc(chunk_ready, 1)

        @block.tensor
        def _(pe):
            nc.tensor.sem_inc(chunk_mixed, 2)
            with pe.Fori(0, NCH // 2) as pair:
                for i in range(2):
                    pe.wait_ge(chunk_ready, pair * 2 + i + 1)
                    pe.wait_ge(w_loaded[i], pair * 32 + 32)
                    for k in range(NB):
                        pe.wait_ge(bank_free, pair * (2 * NB) + i * NB + k + 1)
                        for j in range(MB):
                            m = k * MB + j
                            last = nc.tensor.matmul(mixed_ps[k % 8][:, j, :], chunk[i][:, m, :], w[i][:, :, m],
                                                    start=True, stop=True)
                        if k < NB - 1:
                            last.then_inc(bank_mixed, 1)
                    last.then_inc(bank_mixed, 1)
                    pe.wait_ge(bank_mixed, pair * (2 * NB) + (i + 1) * NB)
                    nc.tensor.sem_inc(chunk_mixed, 1)

        @block.vector
        def _(dve):
            done = [0]

            def chained(instruction):
                done[0] += 1
                instruction.then_inc(step, 1)
                dve.wait_ge(step, done[0])

            nc.vector.sem_inc(bank_free, 8)
            dve.wait_ge(norm_loaded, 32)
            nc.vector.tensor_copy(scale[:, 0, :], norm[:, :, 0])
            chained(nc.vector.tensor_copy(scale[:, 1, :], norm[:, :, 0]))
            chained(nc.vector.tensor_scalar(shift[:, :], norm[:, :, 1], float(H * W) ** 0.5, None, ALU.mult))
            flat_scale = scale[:, :, :].rearrange("p k b -> p (k b)")
            chained(nc.vector.tensor_tensor(
                flat_in, flat_in, flat_scale.unsqueeze(1).to_broadcast([P, MODES * MODES, 2 * B]), ALU.mult))
            nc.vector.tensor_tensor(flat_in[0:C, 0, 0:B], flat_in[0:C, 0, 0:B], shift[0:C, :], ALU.add)
            nc.vector.tensor_tensor(flat_in[C:P, 0, B:2 * B], flat_in[C:P, 0, B:2 * B], shift[C:P, :],
                                    ALU.add).then_inc(normalised, 1)
            with dve.Fori(0, NCH) as ch:
                dve.wait_ge(out_stored, ch * 16)
                for k in range(NB):
                    dve.wait_ge(bank_mixed, ch * NB + k + 1)
                    nc.vector.tensor_copy(mixed[:, k * MB:(k + 1) * MB, :], mixed_ps[k % 8][:, :, :]
                                          ).then_inc(bank_free, 1)


def spectral_inverse(nc, x, y, consts, modes_out, moments, B):
    K2 = 2 * MODES
    NX = 3
    with Stage(nc, "inv") as s:
        x_tile = [s.sbuf(f"x{i}", [P, 2, CT, W]) for i in range(4)]
        g_cols = s.sbuf("g_cols", [P, W])
        g_rows = s.sbuf("g_rows", [P, 2, P])
        modes = [s.sbuf(f"modes{i}", [P, 2, MODES, C]) for i in range(2)]
        rows = [s.sbuf(f"rows{i}", [P, CT, W]) for i in range(2)]
        stats = [s.sbuf(f"stats{i}", [P, CT // 2, 2, 6]) for i in range(2)]
        image_moments = s.sbuf("image_moments", [P, GROUPS, 2])
        HT = CT // 2
        rows_ps = [s.psum(f"rows_ps{i}", [K2, HT, W]) for i in range(2)]
        y_ps = [s.psum(f"y_ps{i}", [P, 2, W]) for i in range(4)]
        consts_loaded = s.sem("consts_loaded")
        x_loaded = [s.sem(f"x_loaded{i}") for i in range(4)]
        y_stored = [s.sem(f"y_stored{i}") for i in range(4)]
        modes_loaded = [s.sem(f"modes_loaded{i}") for i in range(2)]
        modes_ready = s.sem("modes_ready")
        modes_used = s.sem("modes_used")
        rows_done = s.sem("rows_done")
        rows_ready = s.sem("rows_ready")
        y_done = s.sem("y_done")
        y_added = s.sem("y_added")
        measured = s.sem("measured")
        may_aggregate = s.sem("may_aggregate")
        aggregated = s.sem("aggregated")
        cleared = s.sem("cleared")
        may_store = s.sem("may_store")
        block = s.block()

        def rows_of(t, b, i, dram):
            return dram[b * 2 + i, t * CT:(t + 1) * CT, :, :].rearrange("c (f h) w -> f h c w", f=2)

        @block.sync
        def _(sp):
            sp.dma_start(g_cols[:, :], consts["g_cols"]).then_inc(consts_loaded, 16)
            sp.dma_start(g_rows[:, :, :], consts["g_rows"]).then_inc(consts_loaded, 16)
            with sp.Fori(0, B // 2) as pair:
                for i in range(2):
                    sp.wait_ge(modes_used, pair * 2 + i + 1)
                    for top in range(2):
                        for part in range(2):
                            src = modes_out.rearrange("(r b) (x y) o -> r b y x o", r=2, y=MODES)
                            sp.dma_start(modes[i][top * MODES:(top + 1) * MODES, part, :, :],
                                         src[part ^ top, pair * 2 + i]).then_inc(modes_loaded[i], 16)
                    for t in range(NT):
                        n = (i * NT + t) % 4
                        sp.wait_ge(y_stored[n], pair * (32 * NT // 2) + 32 * ((i * NT + t) // 4))
                        for half in range(2):
                            sp.dma_start(x_tile[n][:, half, :, :], rows_of(t, pair, i, x)[half]
                                         ).then_inc(x_loaded[n], 16)

        @block.gpsimd
        def _(pool):
            with pool.Fori(0, B // 2) as pair:
                for m in range(2 * NT):
                    i, t = divmod(m, NT)
                    pool.wait_ge(measured, pair * (2 * NT) + m + 1)
                    nc.gpsimd.sem_inc(may_store, 1)
                    for half in range(2):
                        pool.dma_start(rows_of(t, pair, i, y)[half], x_tile[m % 4][:, half, :, :]
                                       ).then_inc(y_stored[m % 4], 16)
            for n in range(4):
                pool.wait_ge(y_stored[n], 32 * (B * NT // 4))

        @block.tensor
        def _(pe):
            nc.tensor.sem_inc(modes_used, 2)
            pe.wait_ge(consts_loaded, 32)
            pe.wait_ge(cleared, 1)
            with pe.Fori(0, B // 2) as pair:
                for m in range(2 * NT):
                    i, t = divmod(m, NT)
                    if t == 0:
                        pe.wait_ge(modes_ready, pair * 2 + i + 1)
                    for part in range(2):
                        pe.wait_ge(rows_ready, pair * (4 * NT) + 2 * m + part + 1)
                        for c in range(HT):
                            last = nc.tensor.matmul(
                                rows_ps[part][:, c, :],
                                modes[i][:, :, :, t * CT + part * HT + c].rearrange("p r k -> p (r k)"),
                                g_cols[:, :], start=True, stop=True)
                        last.then_inc(rows_done, 1)
                    if t == NT - 1:
                        pe.wait_ge(rows_done, pair * (4 * NT) + 2 * m + 2)
                        nc.tensor.sem_inc(modes_used, 1)
                    for part in range(2):
                        pe.wait_ge(rows_ready, pair * (4 * NT) + 2 * m + part + 3)
                        for j in range(HT // 2):
                            for half in range(2):
                                u = part * HT + j * 2 + half
                                pe.wait_ge(y_added, pair * (16 * NT) + 8 * m + u + 1)
                                c0 = part * HT + 2 * j
                                nc.tensor.matmul(y_ps[u % 4][:, :, :], g_rows[:, half, :],
                                                 rows[m % 2][:, c0:c0 + 2, :],
                                                 start=True, stop=True).then_inc(y_done, 1)

        @block.scalar
        def _(act):
            nc.scalar.sem_inc(rows_ready, 2)
            with act.Fori(0, B // 2) as pair:
                for m in range(2 * NT):
                    i, t = divmod(m, NT)
                    if t == 0:
                        act.wait_ge(modes_loaded[i], pair * 64 + 64)
                        nc.scalar.activation(modes[i][MODES:K2, 1, :, :], modes[i][MODES:K2, 1, :, :],
                                             ACT.Copy, scale=-1.0).then_inc(modes_ready, 1)
                    for part in range(2):
                        act.wait_ge(rows_done, pair * (4 * NT) + 2 * m + part + 1)
                        nc.scalar.activation(rows[m % 2][0:K2, part * HT:(part + 1) * HT, :], rows_ps[part][:, :, :],
                                             ACT.Copy).then_inc(rows_ready, 1)

        @block.vector
        def _(dve):
            for i in range(2):
                nc.vector.memset(modes[i][K2:P, :, :, :], 0.0)
                last = nc.vector.memset(rows[i][K2:P, :, :], 0.0)
            last.then_inc(cleared, 1)
            nc.vector.sem_inc(y_added, 4)
            mo = moments[:, :, :].rearrange("p (b i g) k -> p b i g k", b=B // 2, i=2)
            with dve.Fori(0, B // 2) as pair:
                for m in range(2 * NT):
                    i, t = divmod(m, NT)
                    n = m % 4
                    dve.wait_ge(x_loaded[n], pair * (32 * NT // 2) + 32 * (m // 4) + 32)
                    for j in range(CT // 2):
                        for half in range(2):
                            u = 2 * j + half
                            here = x_tile[n][:, half, 2 * j:2 * j + 2, :]
                            dve.wait_ge(y_done, pair * (16 * NT) + 8 * m + u + 1)
                            nc.vector.tensor_tensor(here, y_ps[u % 4][:, :, :], here, ALU.add).then_inc(y_added, 1)
                            if u >= 1:
                                pj, ph = divmod(u - 1, 2)
                                dve.wait_ge(y_added, pair * (16 * NT) + 8 * m + u + 4)
                                nc.vector.bn_stats(stats[m % 2][:, pj, ph, :],
                                                   x_tile[n][:, ph, 2 * pj:2 * pj + 2, :])
                    dve.wait_ge(y_added, pair * (16 * NT) + 8 * m + 8 + 4)
                    nc.vector.bn_stats(stats[m % 2][:, CT // 2 - 1, 1, :],
                                       x_tile[n][:, 1, CT - 2:CT, :]).then_inc(measured, 1)
                    dve.wait_ge(measured, pair * (2 * NT) + m + 1)
                    nc.vector.sem_inc(may_aggregate, 1)
                    for j in range(CT // 2):
                        last = nc.vector.bn_aggr(image_moments[:, t * CT // 2 + j, :], stats[m % 2][:, j, :, :])
                    if t == NT - 1:
                        last.then_inc(aggregated, 1)
                        dve.wait_ge(aggregated, pair * 2 + i + 1)
                        nc.vector.tensor_copy(mo[:, pair, i, :, :], image_moments[:, :, :])


def constants():
    k = np.arange(MODES)
    h = np.arange(H)
    ang = 2 * np.pi * np.outer(h, k) / H
    root = np.sqrt(float(H))
    cos, sin = np.cos(ang) / root, np.sin(ang) / root
    double = np.where(k == 0, 1.0, 2.0)
    f_rows = np.concatenate([cos, -sin], 1).reshape(2, P, 2 * MODES).transpose(1, 0, 2)
    f_cols = np.stack([np.concatenate([cos, -sin], 1), np.concatenate([sin, cos], 1)], 1)
    f_cols = f_cols.reshape(2, P, 2, 2 * MODES).transpose(1, 0, 2, 3)
    g_cols = np.concatenate([(cos * double).T, -(sin * double).T], 0)
    g_rows = np.concatenate([cos.T, -sin.T], 0).reshape(2 * MODES, 2, P)
    zeros = P - 2 * MODES
    g_cols = np.pad(g_cols, ((0, zeros), (0, 0)))
    g_rows = np.pad(g_rows, ((0, zeros), (0, 0), (0, 0)))
    out = {"f_rows": f_rows, "f_cols": f_cols, "g_cols": g_cols, "g_rows": g_rows,
           "average_all": np.full((P, P), 1.0 / P)}
    return {n: np.ascontiguousarray(v, dtype=np.float32) for n, v in out.items()}


def pair_constants():
    CG, SL = 16, 8
    p = np.arange(P)
    pair = (p % CG) // 2
    masks = np.ones((P, 2))
    masks[:CG, 0] = 0.0
    masks[-CG:, 1] = 0.0
    out = {"average_pairs": (pair[:, None] == pair[None, :]) / (2.0 * SL), "slab_masks": masks}
    return {n: np.ascontiguousarray(v, dtype=np.float32) for n, v in out.items()}


def channel_layout_stores(stats_dram, B):
    def stores(result):
        src = result[0:16, :, :].rearrange("c (b q) k -> c b q k", b=B)
        dst = stats_dram.rearrange("b (q c) k -> c b q k", c=16)
        return [(dst[:, b, :, :], src[:, b, :, :]) for b in range(B)]
    return stores


def dilated_conv(nc, x, y, taps_dram, bias_dram, stats_dram, slab_masks, moments, B):
    DIL = (1, 6, 12, 18)
    NG, CG = len(DIL), C // len(DIL)
    SL = P // CG
    SR = H // SL
    RC = BANK // W
    NCHUNK = SR // RC
    CB = 4
    halo = [max(DIL[i::2]) for i in range(2)]
    with Stage(nc, "dil") as s:
        tile = [s.sbuf(f"tile{i}", [P, SR + 2 * halo[i], W + 2 * halo[i]]) for i in range(2)]
        out = [s.sbuf(f"out{i}", [P, CB * RC, W]) for i in range(2)]
        taps = s.sbuf("taps", [P, NG, 9, P])
        bias = s.sbuf("bias", [P, NG])
        masks = s.sbuf("masks", [P, 2])
        norm = [s.sbuf(f"norm{i}", [P, 2]) for i in range(2)]
        norm_halo = [s.sbuf(f"norm_halo{i}", [P, 2, 2]) for i in range(2)]
        stats = s.sbuf("stats", [P, NCHUNK, 6])
        group_moments = s.sbuf("group_moments", [P, NG, 2])
        ps = [s.psum(f"ps{i}", [P, RC, W]) for i in range(8)]
        cleared = s.sem("cleared")
        consts_loaded = s.sem("consts_loaded")
        tile_loaded = [s.sem(f"tile_loaded{i}") for i in range(2)]
        scales_ready = s.sem("scales_ready")
        tile_ready = s.sem("tile_ready")
        tile_used = s.sem("tile_used")
        chunk_done = s.sem("chunk_done")
        chunk_added = s.sem("chunk_added")
        out_loaded = [s.sem(f"out_loaded{i}") for i in range(2)]
        out_ready = s.sem("out_ready")
        out_stored = [s.sem(f"out_stored{i}") for i in range(2)]
        may_copy = s.sem("may_copy")
        may_aggregate = s.sem("may_aggregate")
        aggregated = s.sem("aggregated")
        block = s.block()
        NBLK = NCHUNK // CB

        def load_tile(sp, b, g):
            i, d = g % 2, DIL[g]
            hl = halo[i]
            cs = slice(g * CG, (g + 1) * CG)
            for s0, s1, up, down in ((0, 1, 0, d), (1, SL - 1, d, d), (SL - 1, SL, d, 0)):
                for sl in range(s0, s1):
                    r0, r1 = sl * SR - up, (sl + 1) * SR + down
                    sp.dma_start(tile[i][sl * CG:(sl + 1) * CG, hl - up:hl + SR + down, hl:hl + W],
                                 x[b, cs, r0:r1, :]).then_inc(tile_loaded[i], 16)
            for sl in range(SL):
                sp.dma_start(norm[i][sl * CG:(sl + 1) * CG, :], stats_dram[b, cs, :]).then_inc(tile_loaded[i], 16)
        TL = 16 * (2 * SL)

        def block_rows(b, g, k, dram):
            v = dram[b, g * CG:(g + 1) * CG, :, :].rearrange("c (s r) w -> s c r w", s=SL)
            return v[:, :, k * CB * RC:(k + 1) * CB * RC, :]

        @block.sync
        def _(sp):
            sp.wait_ge(cleared, 3)
            for sl in range(SL):
                sl_p = slice(sl * CG, (sl + 1) * CG)
                sp.dma_start(taps[sl_p, :, :, sl_p], taps_dram).then_inc(consts_loaded, 16)
                sp.dma_start(bias[sl_p, :], bias_dram).then_inc(consts_loaded, 16)
            sp.dma_start(masks[:, :], slab_masks).then_inc(consts_loaded, 16)
            with sp.Fori(0, B) as b:
                for g in range(NG):
                    sp.wait_ge(tile_used, b * NG + g + 1)
                    load_tile(sp, b, g)

        @block.gpsimd
        def _(pool):
            for i in range(2):
                nc.gpsimd.memset(tile[i][:, :, :], 0.0).then_inc(cleared, 1)
            with pool.Fori(0, B) as b:
                for g in range(NG):
                    for k in range(NBLK):
                        n = (g * NBLK + k) % 2
                        m = b * (NG * NBLK // 2) + (g * NBLK + k) // 2
                        pool.wait_ge(out_stored[n], m * (16 * SL))
                        nc.gpsimd.sem_inc(may_copy, 1)
                        for sl in range(SL):
                            pool.dma_start(out[n][sl * CG:(sl + 1) * CG, :, :], block_rows(b, g, k, x)[sl]
                                           ).then_inc(out_loaded[n], 16)
                        pool.wait_ge(out_ready, b * (NG * NBLK) + g * NBLK + k + 1)
                        nc.gpsimd.sem_inc(may_copy, 1)
                        for sl in range(SL):
                            pool.dma_start(block_rows(b, g, k, y)[sl], out[n][sl * CG:(sl + 1) * CG, :, :]
                                           ).then_inc(out_stored[n], 16)
            for n in range(2):
                pool.wait_ge(out_stored[n], B * NG * NBLK // 2 * (16 * SL))

        @block.scalar
        def _(act):
            act.wait_ge(consts_loaded, 16 * (2 * SL + 1))
            with act.Fori(0, B) as b:
                for g in range(NG):
                    i, d = g % 2, DIL[g]
                    hl = halo[i]
                    act.wait_ge(tile_loaded[i], b * (TL * NG // 2) + TL * (g // 2 + 1))
                    for m in range(2):
                        last = nc.scalar.activation(norm_halo[i][:, m, :], norm[i][:, :], ACT.Copy,
                                                    scale=masks[:, m:m + 1])
                    last.then_inc(scales_ready, 1)
                    act.wait_ge(scales_ready, b * NG + g + 1)
                    cols = slice(hl, hl + W)
                    for rows, sc in ((slice(hl - d, hl), norm_halo[i][:, 0, :]),
                                     (slice(hl, hl + SR), norm[i][:, :]),
                                     (slice(hl + SR, hl + SR + d), norm_halo[i][:, 1, :])):
                        last = nc.scalar.activation(tile[i][:, rows, cols], tile[i][:, rows, cols], ACT.Identity,
                                                    scale=sc[:, 0:1], bias=sc[:, 1:2])
                    last.then_inc(tile_ready, 1)

        @block.tensor
        def _(pe):
            nc.tensor.sem_inc(tile_used, 2)
            pe.wait_ge(consts_loaded, 16 * (2 * SL + 1))
            with pe.Fori(0, B) as b:
                for g in range(NG):
                    i, d = g % 2, DIL[g]
                    hl = halo[i]
                    pe.wait_ge(tile_ready, b * NG + g + 1)
                    for k in range(NCHUNK):
                        pe.wait_ge(chunk_added, b * (NG * NCHUNK) + g * NCHUNK + k + 1)
                        for t in range(9):
                            r0 = hl + k * RC + (t // 3 - 1) * d
                            c0 = hl + (t % 3 - 1) * d
                            last = nc.tensor.matmul(ps[k % 8][:, :, :], taps[:, g, t, :],
                                                    tile[i][:, r0:r0 + RC, c0:c0 + W],
                                                    start=(t == 0), stop=(t == 8))
                        last.then_inc(chunk_done, 1)
                    pe.wait_ge(chunk_done, b * (NG * NCHUNK) + (g + 1) * NCHUNK)
                    nc.tensor.sem_inc(tile_used, 1)

        @block.vector
        def _(dve):
            nc.vector.memset(taps[:, :, :, :], 0.0).then_inc(cleared, 1)
            nc.vector.sem_inc(chunk_added, 8)
            dve.wait_ge(consts_loaded, 16 * (2 * SL + 1))
            mo = moments[:, :, :].rearrange("p (b q) k -> p b q k", b=B)

            with dve.Fori(0, B) as b:
                for g in range(NG):
                    for k in range(NCHUNK):
                        blk, j = divmod(k, CB)
                        n = (g * NBLK + blk) % 2
                        m = b * (NG * NBLK // 2) + (g * NBLK + blk) // 2
                        if j == 0:
                            dve.wait_ge(out_loaded[n], m * (16 * SL) + 16 * SL)
                        done = b * (NG * NCHUNK) + g * NCHUNK + k
                        dve.wait_ge(chunk_done, done + 1)
                        here = out[n][:, j * RC:(j + 1) * RC, :]
                        nc.vector.scalar_tensor_tensor(here, ps[k % 8][:, :, :], bias[:, g:g + 1], here,
                                                       ALU.add, ALU.add).then_inc(chunk_added, 1)
                        dve.wait_ge(chunk_added, done + 9)
                        last = nc.vector.bn_stats(stats[:, k, :], here)
                        if j == CB - 1:
                            last.then_inc(out_ready, 1)
                    dve.wait_ge(out_ready, b * (NG * NBLK) + (g + 1) * NBLK)
                    nc.vector.sem_inc(may_aggregate, 1)
                    nc.vector.bn_aggr(group_moments[:, g, :], stats[:, :, :]).then_inc(aggregated, 1)
                    if g == NG - 1:
                        dve.wait_ge(aggregated, b * NG + NG)
                        nc.vector.tensor_copy(mo[:, b, :, :], group_moments[:, :, :])


KS = 7
KR = KS // 2


def depthwise_mish(nc, x, y, consts, kernel_all, kernel_halo, stats_dram, moments, B):
    NS, NU = 4, 4
    UC = CT // 2
    HALO = (0, 32)
    with Stage(nc, "dw") as s:
        x_tile = [s.sbuf(f"x{i}", [P, 2, CT, W]) for i in range(NS)]
        norm = [s.sbuf(f"norm{i}", [P, CT, 2]) for i in range(NS)]
        padded = [s.sbuf(f"padded{i}", [P, 2, CT, W + 2 * KR]) for i in range(2)]
        edge = [s.sbuf(f"edge{i}", [P, CT, W]) for i in range(2)]
        band = s.sbuf("band", [P, KS, P])
        band_edge = s.sbuf("band_edge", [P, 2, P])
        k_all = s.sbuf("k_all", [P, KS * KS])
        k_halo = s.sbuf("k_halo", [P, KS])
        place = s.sbuf("place", [P, KS, P])
        place_halo = s.sbuf("place_halo", [P, 2, KS, P])
        capped = [s.sbuf(f"capped{i}", [P, UC, W]) for i in range(2)]
        power = [s.sbuf(f"power{i}", [P, UC, W]) for i in range(2)]
        denom = s.sbuf("denom", [P, UC, W])
        numer = s.sbuf("numer", [P, UC, W])
        stats = s.sbuf("stats", [P, CT // 2, 2, 6])
        image_moments = s.sbuf("image_moments", [P, GROUPS, 2])
        ps = [s.psum(f"ps{i}", [P, UC, W]) for i in range(NU)]
        consts_loaded = s.sem("consts_loaded")
        cleared = s.sem("cleared")
        bands_ready = s.sem("bands_ready")
        step = s.sem("step")
        x_loaded = [s.sem(f"x_loaded{i}") for i in range(NS)]
        y_stored = [s.sem(f"y_stored{i}") for i in range(NS)]
        normalised = s.sem("normalised")
        edges_loaded = [s.sem(f"edges_loaded{i}") for i in range(2)]
        padded_used = s.sem("padded_used")
        conv_done = s.sem("conv_done")
        cap_ready = s.sem("cap_ready")
        exp_ready = s.sem("exp_ready")
        chain = s.sem("chain")
        unit_free = s.sem("unit_free")
        y_ready = s.sem("y_ready")
        may_aggregate = s.sem("may_aggregate")
        aggregated = s.sem("aggregated")
        summed = s.sem("summed")
        may_copy = s.sem("may_copy")
        may_normalise = s.sem("may_normalise")
        CH = 4
        XL = 16 * 3
        block = s.block()

        def rows_of(dram, b, t):
            return dram[b, t * CT:(t + 1) * CT, :, :].rearrange("c (f h) w -> f h c w", f=2)

        def images(eng, image):
            if B > 1:
                with eng.Fori(0, B - 1) as b:
                    image(b, False)
            image(B - 1, True)

        @block.sync
        def _(sp):
            for dst, src in ((k_all[:, :], kernel_all), (place[:, :, :], consts["place"]),
                             (place_halo[:, :, :, :], consts["place_halo"]), (k_halo[:, :], kernel_halo)):
                sp.dma_start(dst, src).then_inc(consts_loaded, 16)

            def load(b, t, first=False):
                n = t % NS
                if not first:
                    sp.wait_ge(y_stored[n], b * (32 * NT // NS) + 32 * (t // NS))
                for half in range(2):
                    sp.dma_start(x_tile[n][:, half, :, :], rows_of(x, b, t)[half]).then_inc(x_loaded[n], 16)
                sp.dma_start(norm[n][:, :, :], stats_dram[b, t * CT:(t + 1) * CT, :].partition_broadcast(P)
                             ).then_inc(x_loaded[n], 16)

            AHEAD = NS - 1
            for t in range(AHEAD):
                load(0, t, True)

            def image(b, last):
                for t in range(NT):
                    sp.wait_ge(y_ready, b * NT + t + 1)
                    for half in range(2):
                        sp.dma_start(rows_of(y, b, t)[half], x_tile[t % NS][:, half, :, :]
                                     ).then_inc(y_stored[t % NS], 16)
                    nt = t + AHEAD
                    if nt < NT:
                        load(b, nt) if not (isinstance(b, int) and b == 0 and nt < NS) else load(b, nt, True)
                    elif not last:
                        load(b + 1, nt - NT)

            images(sp, image)
            for n in range(NS):
                sp.wait_ge(y_stored[n], 32 * (B * NT // NS))

        @block.gpsimd
        def _(pool):
            for i in range(2):
                nc.gpsimd.memset(padded[i][:, :, :, :], 0.0)
                nc.gpsimd.memset(edge[i][:, :, :], 0.0).then_inc(cleared, 1)
            pool.wait_ge(cleared, 2)
            with pool.Fori(0, B) as b:
                for t in range(NT):
                    i = t % 2
                    pool.wait_ge(normalised, b * NT + t + 1)
                    nc.gpsimd.sem_inc(may_copy, 1)
                    for kw in range(KS):
                        p0 = HALO[0] + KR * kw
                        pool.dma_start(edge[i][p0:p0 + KR, :, :], padded[i][0:KR, 1, :, kw:kw + W]
                                       ).then_inc(edges_loaded[i], 16)
                        p1 = HALO[1] + KR * kw
                        pool.dma_start(edge[i][p1:p1 + KR, :, :], padded[i][P - KR:P, 0, :, kw:kw + W]
                                       ).then_inc(edges_loaded[i], 16)

        @block.scalar
        def _(act):
            act.wait_ge(cleared, 2)

            def exps(n0, t, units):
                for u in units:
                    act.wait_ge(cap_ready, n0 * NU + t * NU + u + 1)
                    nc.scalar.activation(power[u % 2][:, :, :], capped[u % 2][:, :, :], ACT.Exp).then_inc(exp_ready, 1)

            def normalise(b, t):
                i, n = t % 2, t % NS
                act.wait_ge(x_loaded[n], b * (XL * NT // NS) + XL * (t // NS) + XL)
                act.wait_ge(padded_used, b * NT + t + 1)
                nc.scalar.sem_inc(may_normalise, 1)
                for j in range(CT // 2):
                    for half in range(2):
                        last = nc.scalar.activation(
                            padded[i][:, half, 2 * j:2 * j + 2, KR:KR + W], x_tile[n][:, half, 2 * j:2 * j + 2, :],
                            ACT.Identity, scale=norm[n][:, 2 * j, 0:1], bias=norm[n][:, 2 * j, 1:2])
                last.then_inc(normalised, 1)

            normalise(0, 0)

            def image(b, last):
                for t in range(NT):
                    exps(b * NT, t, (0,))
                    if t < NT - 1:
                        normalise(b, t + 1)
                    elif not last:
                        normalise(b + 1, 0)
                    exps(b * NT, t, (1, 2, 3))

            images(act, image)

        @block.tensor
        def _(pe):
            nc.tensor.sem_inc(padded_used, 2)
            pe.wait_ge(bands_ready, 1)
            with pe.Fori(0, B) as b:
                for t in range(NT):
                    i = t % 2
                    pe.wait_ge(normalised, b * NT + t + 1)
                    pe.wait_ge(edges_loaded[i], b * (16 * 2 * KS * NT // 2) + 16 * 2 * KS * (t // 2 + 1))
                    for u in range(NU):
                        part, half = divmod(u, 2)
                        pe.wait_ge(unit_free, b * (NT * NU) + t * NU + u + 1)
                        for j in range(UC // 2):
                            c0 = part * UC + 2 * j
                            for kw in range(KS):
                                nc.tensor.matmul(ps[u][:, 2 * j:2 * j + 2, :], band[:, kw, :],
                                                 padded[i][:, half, c0:c0 + 2, kw:kw + W],
                                                 start=(kw == 0), stop=False)
                            last = nc.tensor.matmul(ps[u][:, 2 * j:2 * j + 2, :], band_edge[:, half, :],
                                                    edge[i][:, c0:c0 + 2, :], start=False, stop=True)
                        last.then_inc(conv_done, 1)
                    pe.wait_ge(conv_done, b * (NT * NU) + (t + 1) * NU)
                    nc.tensor.sem_inc(padded_used, 1)

        @block.vector
        def _(dve):
            done = [0]

            def chained(instruction):
                done[0] += 1
                instruction.then_inc(step, 1)
                dve.wait_ge(step, done[0])

            dve.wait_ge(consts_loaded, 64)
            for a in range(KS):
                for kw in range(KS):
                    w = k_all[:, a * KS + kw:a * KS + kw + 1]
                    if a == 0:
                        last = nc.vector.tensor_scalar(band[:, kw, :], place[:, a, :], w, None, ALU.mult)
                    else:
                        last = nc.vector.scalar_tensor_tensor(band[:, kw, :], place[:, a, :], w, band[:, kw, :],
                                                              ALU.mult, ALU.add)
                for half in range(2):
                    w = k_halo[:, a:a + 1]
                    src = place_halo[:, half, a, :]
                    if a == 0:
                        last = nc.vector.tensor_scalar(band_edge[:, half, :], src, w, None, ALU.mult)
                    else:
                        last = nc.vector.scalar_tensor_tensor(band_edge[:, half, :], src, w, band_edge[:, half, :],
                                                              ALU.mult, ALU.add)
                if a < KS - 1:
                    chained(last)
            last.then_inc(bands_ready, 1)
            nc.vector.sem_inc(unit_free, NU)
            mo = moments[:, :, :].rearrange("p (b g) k -> p b g k", b=B)
            with dve.Fori(0, B) as b:
                for t in range(NT):
                    n = t % NS
                    for u in range(NU):
                        part, half = divmod(u, 2)
                        at = b * (NT * NU) + t * NU + u
                        c0 = part * UC
                        here = x_tile[n][:, half, c0:c0 + UC, :]
                        dve.wait_ge(conv_done, at + 1)
                        nc.vector.tensor_scalar(capped[u % 2][:, :, :], ps[u][:, :, :], 20.0, None, ALU.min
                                                ).then_inc(cap_ready, 1)
                        dve.wait_ge(exp_ready, at + 1)
                        e = power[u % 2][:, :, :]
                        nc.vector.scalar_tensor_tensor(numer[:, :, :], e, 2.0, e, ALU.add, ALU.mult).then_inc(chain, 1)
                        dve.wait_ge(chain, at * CH + 1)
                        nc.vector.tensor_scalar(denom[:, :, :], numer[:, :, :], 2.0, None, ALU.add).then_inc(chain, 1)
                        nc.vector.tensor_tensor(numer[:, :, :], ps[u][:, :, :], numer[:, :, :], ALU.mult
                                                ).then_inc(unit_free, 1)
                        dve.wait_ge(chain, at * CH + 2)
                        nc.vector.reciprocal(denom[:, :, :], denom[:, :, :]).then_inc(chain, 1)
                        dve.wait_ge(chain, at * CH + 3)
                        dve.wait_ge(unit_free, at + 1 + NU)
                        nc.vector.tensor_tensor(numer[:, :, :], numer[:, :, :], denom[:, :, :], ALU.mult
                                                ).then_inc(chain, 1)
                        dve.wait_ge(chain, at * CH + 4)
                        nc.vector.tensor_tensor(here, here, numer[:, :, :], ALU.add).then_inc(summed, 1)
                        dve.wait_ge(summed, at + 1)
                        for j in range(UC // 2):
                            last = nc.vector.bn_stats(stats[:, part * UC // 2 + j, half, :],
                                                      x_tile[n][:, half, c0 + 2 * j:c0 + 2 * j + 2, :])
                    last.then_inc(y_ready, 1)
                    dve.wait_ge(y_ready, b * NT + t + 1)
                    nc.vector.sem_inc(may_aggregate, 1)
                    for j in range(CT // 2):
                        last = nc.vector.bn_aggr(image_moments[:, t * CT // 2 + j, :], stats[:, j, :, :])
                last.then_inc(aggregated, 1)
                dve.wait_ge(aggregated, b + 1)
                nc.vector.tensor_copy(mo[:, b, :, :], image_moments[:, :, :])


def mish_constants():
    src, dst = np.arange(P)[:, None], np.arange(P)[None, :]
    place = np.stack([(src - dst + KR == a) for a in range(KS)], 1)
    halo = np.zeros((P, 2, KS, P))
    for kw in range(KS):
        for r in range(KR):
            for a in range(KS):
                halo[KR * kw + r, 0, a] = (P + r - np.arange(P) + KR == a)
                halo[32 + KR * kw + r, 1, a] = (r - np.arange(P) == a)
    return {n: np.ascontiguousarray(v, dtype=np.float32) for n, v in (("place", place), ("place_halo", halo))}


def mish_kernels(kernel):
    turned = kernel[::-1, ::-1]
    k_all = np.broadcast_to(turned.reshape(1, KS * KS), (P, KS * KS))
    k_halo = np.zeros((P, KS), kernel.dtype)
    for first in (0, 32):
        k_halo[first:first + KR * KS] = np.repeat(turned.T, KR, axis=0)
    return np.ascontiguousarray(k_all), k_halo


PATCH = 8
CIN = 384


def patch_filter_block(nc, x, y, consts, w_in, w_dw, filt, w_out, stats_dram, B):
    S = H // PATCH
    NB = 4
    HW_ = W // 2
    NJ = HW_ // (2 * PATCH)
    BJ = NJ // 2
    CTS = CIN // P
    RU = 4
    NPE = 2
    TAPS = [(0, 0), (0, 2), (2, 0), (2, 2), (0, 1), (2, 1), (1, 0), (1, 2), (1, 1)]
    UNITS = [(0, 0), (0, 1), (0, 2), (1, 2), (1, 0), (1, 1)]
    NUN = len(UNITS)
    NV = len(TAPS) - NPE
    with Stage(nc, "l3") as s:
        x_tile = [s.sbuf(f"x{i}", [P, PATCH, HW_]) for i in range(NB)]
        normed = s.sbuf("normed", [P, NJ, PATCH, 2 * PATCH])
        grid = [s.sbuf(f"grid{i}", [P, CTS, PATCH + 2, W + 2]) for i in range(NB)]
        turned = s.sbuf("turned", [P, BJ, P])
        spectrum = s.sbuf("spectrum", [P, BJ, P])
        wide = s.sbuf("wide", [P, 2, BJ, CIN])
        acc = [[s.sbuf(f"acc{r}{c}", [P, RU, W]) for c in range(CTS)] for r in range(2)]
        gated = [s.sbuf(f"gated{r}", [P, RU, W]) for r in range(2)]
        norm = s.sbuf("norm", [P, B, 2])
        ident = s.sbuf("ident", [P, P])
        to_freq = s.sbuf("to_freq", [P, P])
        to_pixel = s.sbuf("to_pixel", [P, P])
        gain = s.sbuf("gain", [P, CIN])
        w_in_s = s.sbuf("w_in", [P, 2, CIN])
        w_dw_s = s.sbuf("w_dw", [P, CTS, 9])
        diag = s.sbuf("diag", [P, CTS, NPE, P])
        w_out_s = s.sbuf("w_out", [P, 2, C])
        spread = x_tile[0][0:40, 0, 0:P]
        filt_s = x_tile[1][0:40, 0:3, :]
        ps_turn = s.psum("ps_turn", [P, BJ, P])
        ps_out = s.psum("ps_out", [P, RU, HW_])
        ps_wide = [s.psum(f"ps_wide{i}", [P, BANK]) for i in range(2)]
        ps_grid = [s.psum(f"ps_grid{i}", [P, BJ, PATCH, 2 * PATCH]) for i in range(2)]
        ps_taps = s.psum("ps_taps", [P, RU, W])
        consts_loaded = s.sem("consts_loaded")
        cleared = s.sem("cleared")
        gain_done = s.sem("gain_done")
        gain_ready = s.sem("gain_ready")
        x_loaded = [s.sem(f"x_loaded{i}") for i in range(NB)]
        y_stored = [s.sem(f"y_stored{i}") for i in range(NB)]
        may_copy = s.sem("may_copy")
        may_normalise = s.sem("may_normalise")
        normed_ready = s.sem("normed_ready")
        turned_done = s.sem("turned_done")
        turned_ready = s.sem("turned_ready")
        spectrum_done = s.sem("spectrum_done")
        spectrum_ready = s.sem("spectrum_ready")
        wide_done = s.sem("wide_done")
        wide_ready = s.sem("wide_ready")
        grid_done = s.sem("grid_done")
        grid_ready = s.sem("grid_ready")
        halo_ready = s.sem("halo_ready")
        taps_done = s.sem("taps_done")
        taps_read = s.sem("taps_read")
        chain = s.sem("chain")
        unit_ready = s.sem("unit_ready")
        gelu_ready = s.sem("gelu_ready")
        gate_ready = s.sem("gate_ready")
        out_done = s.sem("out_done")
        y_ready = s.sem("y_ready")
        block = s.block()
        UNIT0 = NB * NUN
        NSMALL = 10

        def strips_of(dram, b, q):
            v = dram[b].rearrange("c (q r) (f w) -> q f c r w", r=PATCH, f=2)
            return v[q]

        def steps(eng, step):
            step(None, (0, 0, 0))
            step(None, (0, 1, 1))

            def image(b, last):
                with eng.Fori(0, S // NB - 1) as j:
                    for i in range(NB):
                        step((b, j * NB + i, i), (b, j * NB + i + 2, (i + 2) % NB))
                for i in range(NB):
                    q = S - NB + i
                    if q + 2 < S:
                        ahead = (b, q + 2, (i + 2) % NB)
                    else:
                        ahead = None if last else (b + 1, q + 2 - S, (i + 2) % NB)
                    step((b, q, i), ahead)

            if B > 1:
                with eng.Fori(0, B - 1) as b:
                    image(b, False)
            image(B - 1, True)

        def edge(q, value):
            return isinstance(q, int) and q == value

        @block.sync
        def _(sp):
            small = [(spread, consts["spread"]), (filt_s.rearrange("p a b -> p (a b)"), filt),
                     (ident[:, :], consts["ident"]), (to_freq[:, :], consts["to_freq"]),
                     (to_pixel[:, :], consts["to_pixel"]), (w_dw_s[:, :, :], w_dw)]
            sp.wait_ge(cleared, 2)
            for half in range(2):
                hp = slice(half * C, (half + 1) * C)
                small += [(norm[hp, :, :], stats_dram.rearrange("b c k -> c b k")), (w_in_s[hp, half, :], w_in)]
            small += [(w_out_s[:, 0, :], w_out[0:P, :]), (w_out_s[C:P, 1, :], w_out[P:P + C, :])]
            for dst, src in small:
                sp.dma_start(dst, src).then_inc(consts_loaded, 16)
            assert len(small) == NSMALL + 2

            def load(b, q, i, first=False):
                if not first:
                    sp.wait_ge(y_stored[i], b * (32 * S // NB) + q // NB * 32)
                for half in range(2):
                    sp.dma_start(x_tile[i][half * C:(half + 1) * C, :, :], strips_of(x, b, q)[half]
                                 ).then_inc(x_loaded[i], 16)

            sp.wait_ge(gain_ready, 1)
            for i in range(NB):
                load(0, i, i, True)

            def store(b, q, i):
                sp.wait_ge(y_ready, b * (2 * S) + q * 2 + 3)
                for half in range(2):
                    sp.dma_start(strips_of(y, b, q)[half], x_tile[i][half * C:(half + 1) * C, :, :]
                                 ).then_inc(y_stored[i], 16)

            def image(b, last):
                with sp.Fori(0, S // NB - 1) as j:
                    for i in range(NB):
                        store(b, j * NB + i, i)
                        load(b, j * NB + NB + i, i)
                for i in range(NB):
                    store(b, S - NB + i, i)
                    if not last:
                        load(b + 1, i, i)

            if B > 1:
                with sp.Fori(0, B - 1) as b:
                    image(b, False)
            image(B - 1, True)
            for i in range(NB):
                sp.wait_ge(y_stored[i], 32 * (B * S // NB))

        @block.gpsimd
        def _(pool):
            for r in range(2):
                nc.gpsimd.memset(gated[r][:, :, :], 0.0)
            for i in range(NB):
                nc.gpsimd.memset(grid[i][:, :, :, 0:1], 0.0)
                last = nc.gpsimd.memset(grid[i][:, :, :, W + 1:W + 2], 0.0)
            last.then_inc(cleared, 1)

            def step(conv, idft):
                if idft is None:
                    return
                b, q, i = idft
                n = b * S + q
                pool.wait_ge(grid_ready, n * (4 * CTS) + 4 * CTS + 2)
                nc.gpsimd.sem_inc(may_copy, 1)
                before = (i - 1) % NB
                if edge(q, 0):
                    last = nc.gpsimd.memset(grid[i][:, :, 0, 1:W + 1], 0.0)
                else:
                    nc.gpsimd.tensor_copy(grid[i][:, :, 0, 1:W + 1], grid[before][:, :, PATCH, 1:W + 1])
                    last = nc.gpsimd.tensor_copy(grid[before][:, :, PATCH + 1, 1:W + 1], grid[i][:, :, 1, 1:W + 1])
                if edge(q, S - 1):
                    last = nc.gpsimd.memset(grid[i][:, :, PATCH + 1, 1:W + 1], 0.0)
                last.then_inc(halo_ready, 1)

            steps(pool, step)

        @block.scalar
        def _(act):
            nc.scalar.sem_inc(grid_ready, 2)
            act.wait_ge(consts_loaded, 16 * (NSMALL + 2))

            def step(conv, idft):
                if idft:
                    b, q, i = idft
                    n = b * S + q

                def normalise():
                    act.wait_ge(x_loaded[i], b * (32 * S // NB) + q // NB * 32 + 32)
                    act.wait_ge(turned_done, n * 2)
                    nc.scalar.sem_inc(may_normalise, 1)
                    nc.scalar.activation(normed[:, :, :, :].rearrange("p j r c -> p r j c"),
                                         x_tile[i][:, :, :].rearrange("p r (j c) -> p r j c", j=NJ),
                                         ACT.Identity, scale=norm[:, b, 0:1], bias=norm[:, b, 1:2]
                                         ).then_inc(normed_ready, 1)

                def turn_copy(k):
                    act.wait_ge(turned_done, n * 2 + k + 1)
                    nc.scalar.activation(turned[:, :, :], ps_turn[:, :, :], ACT.Copy).then_inc(turned_ready, 1)

                def spectrum_copy(k):
                    act.wait_ge(spectrum_done, n * 2 + k + 1)
                    nc.scalar.activation(spectrum[:, :, :], ps_turn[:, :, :], ACT.Copy).then_inc(spectrum_ready, 1)

                def grid_copies(k):
                    if k == 0:
                        act.wait_ge(unit_ready, n * NUN + NUN)
                    for g in range(2 * CTS):
                        half, ct = divmod(g, CTS)
                        act.wait_ge(grid_done, n * (4 * CTS) + k * 2 * CTS + g + 1)
                        c0 = 1 + half * HW_ + k * BJ * 2 * PATCH
                        dst = grid[i][:, ct, 1:PATCH + 1, c0:c0 + BJ * 2 * PATCH]
                        nc.scalar.activation(dst.rearrange("p r (j c) -> p r j c", j=BJ),
                                             ps_grid[g % 2][:, :, :, :].rearrange("p j r c -> p r j c"),
                                             ACT.Copy).then_inc(grid_ready, 1)

                def gelu(u):
                    cb, cq, _ = conv
                    r, ct = UNITS[u]
                    act.wait_ge(unit_ready, cb * (S * NUN) + cq * NUN + u + 1 + UNIT0)
                    if ct == 0:
                        nc.scalar.activation(acc[r][0][:, :, :], acc[r][0][:, :, :], ACT.Gelu).then_inc(gelu_ready, 1)
                    else:
                        nc.scalar.activation(gated[r][C:P, :, :], acc[r][2][0:C, :, :], ACT.Gelu
                                             ).then_inc(gelu_ready, 1)

                if idft:
                    normalise()
                    turn_copy(0)
                    spectrum_copy(0)
                if conv:
                    gelu(0)
                if idft:
                    turn_copy(1)
                if conv:
                    gelu(2)
                if idft:
                    spectrum_copy(1)
                    grid_copies(0)
                if conv:
                    gelu(3)
                    gelu(4)
                if idft:
                    grid_copies(1)

            steps(act, step)

        @block.tensor
        def _(pe):
            pe.wait_ge(consts_loaded, 16 * (NSMALL + 2))
            nc.tensor.matmul(ps_wide[0][:, 0:CIN], spread, filt_s.rearrange("p a b -> p (a b)"), start=True, stop=True
                             ).then_inc(gain_done, 1)
            pe.wait_ge(gain_ready, 1)

            def step(conv, idft):
                if idft:
                    b, q, i = idft
                    n = b * S + q
                if conv:
                    cb, cq, ci = conv
                    at = cb * S + cq

                def turn(k):
                    pe.wait_ge(normed_ready, n + 1)
                    pe.wait_ge(spectrum_ready, n * 2 + k)
                    for j in range(BJ):
                        last = nc.tensor.matmul(ps_turn[:, j, :],
                                                normed[:, k * BJ + j, :, :].rearrange("p r c -> p (r c)"),
                                                ident[:, :], start=True, stop=True)
                    last.then_inc(turned_done, 1)

                def transform(k):
                    pe.wait_ge(turned_ready, n * 2 + k + 1)
                    for j in range(BJ):
                        last = nc.tensor.matmul(ps_turn[:, j, :], turned[:, j, :], to_freq[:, :],
                                                start=True, stop=True)
                    last.then_inc(spectrum_done, 1)

                def project(k, m0, m1):
                    pe.wait_ge(spectrum_ready, n * 2 + k + 1)
                    for m in range(m0, m1):
                        half, j = divmod(m, BJ)
                        pe.wait_ge(wide_ready, n * (4 * BJ) + k * 2 * BJ + m + 1)
                        nc.tensor.matmul(ps_wide[m % 2][:, 0:CIN], spectrum[:, j, :], w_in_s[:, half, :],
                                         start=True, stop=True).then_inc(wide_done, 1)

                def invert(k):
                    for g in range(2 * CTS):
                        half, ct = divmod(g, CTS)
                        pe.wait_ge(wide_ready, n * (4 * BJ) + k * 2 * BJ + (half + 1) * BJ + 2)
                        pe.wait_ge(grid_ready, n * (4 * CTS) + k * 2 * CTS + g + 1)
                        for j in range(BJ):
                            last = nc.tensor.matmul(ps_grid[g % 2][:, j, :, :], wide[:, half, j, ct * P:(ct + 1) * P],
                                                    to_pixel[:, :], start=True, stop=True)
                        last.then_inc(grid_done, 1)

                def taps(u):
                    r, ct = UNITS[u]
                    if u == 0:
                        pe.wait_ge(halo_ready, at + (1 if edge(cq, S - 1) else 2))
                    pe.wait_ge(taps_read, at * NUN + u + 1)
                    for h in range(RU // 2):
                        for m, (kh, kw) in enumerate(TAPS[:NPE]):
                            r0 = r * RU + 2 * h + kh
                            last = nc.tensor.matmul(ps_taps[:, 2 * h:2 * h + 2, :], diag[:, ct, m, :],
                                                    grid[ci][:, ct, r0:r0 + 2, kw:kw + W],
                                                    start=(m == 0), stop=(m == NPE - 1))
                    last.then_inc(taps_done, 1)

                def output(r):
                    pe.wait_ge(gate_ready, at * 4 + 2 * r + 2)
                    pe.wait_ge(y_ready, at * 2 + r + 1)
                    for half in range(2):
                        cols = slice(half * HW_, (half + 1) * HW_)
                        dst = ps_out[half * C:(half + 1) * C, :, :]
                        nc.tensor.matmul(dst, w_out_s[:, 1, :], gated[r][:, :, cols], start=True, stop=False)
                        last = nc.tensor.matmul(dst, w_out_s[:, 0, :], acc[r][1][:, :, cols], start=False, stop=True)
                    last.then_inc(out_done, 1)

                if conv:
                    taps(0)
                if idft:
                    turn(0)
                if conv:
                    taps(1)
                if idft:
                    transform(0)
                if conv:
                    taps(2)
                if idft:
                    project(0, 0, BJ)
                    turn(1)
                if conv:
                    taps(3)
                if idft:
                    project(0, BJ, 2 * BJ)
                    transform(1)
                if conv:
                    taps(4)
                    output(0)
                if idft:
                    invert(0)
                    project(1, 0, BJ)
                if conv:
                    taps(5)
                if idft:
                    project(1, BJ, BJ + 2)
                if conv:
                    output(1)
                if idft:
                    project(1, BJ + 2, 2 * BJ)
                    invert(1)

            steps(pe, step)

        @block.vector
        def _(dve):
            nc.vector.memset(w_in_s[:, :, :], 0.0)
            nc.vector.memset(w_out_s[:, :, :], 0.0).then_inc(cleared, 1)
            dve.wait_ge(consts_loaded, 16 * (NSMALL + 2))
            for ct in range(CTS):
                for m, (kh, kw) in enumerate(TAPS[:NPE]):
                    k = kh * 3 + kw
                    nc.vector.tensor_scalar(diag[:, ct, m, :], ident[:, :], w_dw_s[:, ct, k:k + 1], None, ALU.mult)
            dve.wait_ge(gain_done, 1)
            nc.vector.tensor_copy(gain[:, :], ps_wide[0][:, 0:CIN]).then_inc(gain_ready, 1)
            nc.vector.sem_inc(wide_ready, 2)
            nc.vector.sem_inc(taps_read, 1)
            nc.vector.sem_inc(unit_ready, UNIT0)
            nc.vector.sem_inc(y_ready, 1)
            dve.wait_ge(gain_ready, 1)

            def step(conv, idft):
                if idft:
                    b, q, i = idft
                    n = b * S + q
                if conv:
                    cb, cq, ci = conv
                    at = cb * S + cq

                def widen(k, m):
                    half, j = divmod(m, BJ)
                    dve.wait_ge(wide_done, n * (4 * BJ) + k * 2 * BJ + m + 1)
                    nc.vector.tensor_tensor(wide[:, half, j, :], ps_wide[m % 2][:, 0:CIN], gain[:, :], ALU.mult
                                            ).then_inc(wide_ready, 1)

                def unit(u, extras=()):
                    r, ct = UNITS[u]
                    extras = list(extras)
                    for t, (kh, kw) in enumerate(TAPS[NPE:]):
                        src = grid[ci][:, ct, r * RU + kh:r * RU + kh + RU, kw:kw + W]
                        w = w_dw_s[:, ct, kh * 3 + kw:kh * 3 + kw + 1]
                        if t == 0:
                            dve.wait_ge(taps_done, at * NUN + u + 1)
                            nc.vector.scalar_tensor_tensor(acc[r][ct][:, :, :], src, w, ps_taps[:, :, :],
                                                           ALU.mult, ALU.add).then_inc(taps_read, 1)
                            dve.wait_ge(taps_read, at * NUN + u + 2)
                        else:
                            this = nc.vector.scalar_tensor_tensor(acc[r][ct][:, :, :], src, w, acc[r][ct][:, :, :],
                                                                  ALU.mult, ALU.add)
                            if t < NV - 1:
                                this.then_inc(chain, 1)
                            else:
                                this.then_inc(unit_ready, 1)
                        if t >= 1 and extras:
                            extras.pop(0)()
                        if 0 < t < NV - 1:
                            dve.wait_ge(chain, (at * NUN + u) * (NV - 2) + t)
                    for extra in extras:
                        extra()

                def gate(k, u_b):
                    r, ct = UNITS[u_b]
                    dve.wait_ge(unit_ready, at * NUN + u_b + 1 + UNIT0)
                    dve.wait_ge(gelu_ready, at * 4 + k + 1)
                    if ct == 1:
                        a, dst = acc[r][0][:, :, :], acc[r][1][:, :, :]
                        last = nc.vector.tensor_tensor(dst, dst, a, ALU.mult)
                    else:
                        a, dst = acc[r][2][C:P, :, :], gated[r][C:P, :, :]
                        last = nc.vector.tensor_tensor(dst, dst, a, ALU.mult)
                    last.then_inc(gate_ready, 1)

                def add_x(r):
                    dve.wait_ge(out_done, at * 2 + r + 1)
                    here = x_tile[ci][:, r * RU:(r + 1) * RU, :]
                    nc.vector.tensor_tensor(here, ps_out[:, :, :], here, ALU.add).then_inc(y_ready, 1)

                def widens(k, m0, m1):
                    return [lambda m=m: widen(k, m) for m in range(m0, m1)] if idft else []

                if not conv:
                    for k in range(2):
                        for extra in widens(k, 0, 2 * BJ):
                            extra()
                    return
                unit(0)
                unit(1)
                gate(0, 1)
                unit(2, widens(0, 0, BJ))
                unit(3, widens(0, BJ, 2 * BJ) + [lambda: gate(1, 2)])
                unit(4, widens(1, 0, BJ) + [lambda: gate(2, 3)])
                unit(5, [lambda: None, lambda: None, lambda: add_x(0)])
                gate(3, 5)
                for extra in widens(1, BJ, BJ + 2):
                    extra()
                add_x(1)
                for extra in widens(1, BJ + 2, 2 * BJ):
                    extra()

            steps(dve, step)


def patch_constants():
    n = PATCH
    r, c = np.meshgrid(np.arange(n), np.arange(n), indexing="ij")
    basis, spread = [], []
    for kx, ky in [(kx, ky) for ky in range(n // 2 + 1) for kx in range(n)]:
        own = ky in (0, n // 2)
        mirror = (-kx) % n
        if own and mirror < kx:
            continue
        ang = 2 * np.pi * (kx * r + ky * c) / n
        gain = np.zeros((n, n // 2 + 1))
        gain[kx, ky] += 0.5 if own else 1.0
        gain[mirror, ky] += 0.5 if own else 0.0
        for f in [np.cos(ang)] + ([] if own and mirror == kx else [np.sin(ang)]):
            basis.append((f / np.linalg.norm(f)).ravel())
            spread.append(gain.ravel())
    basis = np.array(basis)
    assert basis.shape == (n * n, n * n) and np.allclose(basis @ basis.T, np.eye(n * n))
    to_freq = np.zeros((n, 2, n, 2, n * n))
    for patch in range(2):
        to_freq[:, patch, :, patch, :] = basis.T.reshape(n, n, n * n)
    to_freq = to_freq.reshape(P, P)
    out = {"ident": np.eye(P), "to_freq": to_freq, "to_pixel": to_freq.T,
           "spread": np.tile(np.array(spread).T, (1, 2))}
    return {k: np.ascontiguousarray(v, dtype=np.float32) for k, v in out.items()}


def channel_order():
    h = CIN // 2
    return np.r_[0:P, h:h + P, P:h, h + P:CIN]


def projection_layouts(w_in, w_dw, filt, w_out):
    order = channel_order()
    w_in = np.ascontiguousarray(w_in[order].T)
    w_dw = np.ascontiguousarray(w_dw.reshape(CIN, 9)[order].reshape(CIN // P, P, 9).transpose(1, 0, 2))
    filt = np.ascontiguousarray(filt.reshape(CIN, 40)[order].T)
    return w_in, w_dw, filt, np.ascontiguousarray(w_out.T)


def build(nc, B, x, w_real, w_imag, dil_taps, dil_bias, kernel_all, kernel_halo, w_in, w_dw, filt, w_out, consts, y):
    def scratch(name, shape):
        return nc.dram_tensor(name, shape, FP32, kind="Internal").ap()

    shape = [B, C, H, W]
    x1, x2, x3 = (scratch(f"x{i}", shape) for i in (1, 2, 3))
    stats = [scratch(f"norm{i}", [B, C, 2]) for i in range(4)]
    modes_mixed = scratch("modes_mixed", [2 * B, MODES * MODES, C])
    with Stage(nc, "layer0a") as s:
        moments = s.sbuf("moments", [P, B * GROUPS, 2])
        modes_in = s.sbuf("modes_in", [P, MODES, MODES, 2 * B])
        spectral_forward(nc, x, consts, moments, modes_in, B)
        finish_statistics(nc, "norm0", moments, B * GROUPS, consts["average_all"], row_layout_stores(stats[0], B))
        spectral_mix(nc, w_real, w_imag, stats[0], modes_in, modes_mixed, B)
    with Stage(nc, "layer0b") as s:
        moments = s.sbuf("moments", [P, B * GROUPS, 2])
        spectral_inverse(nc, x, x1, consts, modes_mixed, moments, B)
        finish_statistics(nc, "norm1", moments, B * GROUPS, consts["average_all"], row_layout_stores(stats[1], B))
    with Stage(nc, "layer1") as s:
        moments = s.sbuf("moments", [P, B * 4, 2])
        dilated_conv(nc, x1, x2, dil_taps, dil_bias, stats[1], consts["slab_masks"], moments, B)
        finish_statistics(nc, "norm2", moments, B * 4, consts["average_pairs"], channel_layout_stores(stats[2], B))
    with Stage(nc, "layer2") as s:
        moments = s.sbuf("moments", [P, B * GROUPS, 2])
        depthwise_mish(nc, x2, x3, consts, kernel_all, kernel_halo, stats[2], moments, B)
        finish_statistics(nc, "norm3", moments, B * GROUPS, consts["average_all"], row_layout_stores(stats[3], B))
    patch_filter_block(nc, x3, y, consts, w_in, w_dw, filt, w_out, stats[3], B)


def kernel(x, L0_conv_weight_real, L0_conv_weight_imag, L1_conv_weight, L1_conv_bias, L2_conv_kernel,
           L3_conv_w_in, L3_conv_w_dw, L3_conv_fft_filter, L3_conv_w_out):
    import concourse.bacc as bacc
    from concourse.bass_utils import run_bass_kernel_spmd

    B = x.shape[0]
    consts = {**constants(), **pair_constants(), **mish_constants(), **patch_constants()}
    kernel_all, kernel_halo = mish_kernels(np.asarray(L2_conv_kernel))
    w_in, w_dw, filt, w_out = projection_layouts(*map(np.asarray, (L3_conv_w_in, L3_conv_w_dw, L3_conv_fft_filter,
                                                                  L3_conv_w_out)))
    arrays = {
        "x": np.asarray(x), "w_real": np.asarray(L0_conv_weight_real), "w_imag": np.asarray(L0_conv_weight_imag),
        "dil_taps": np.asarray(L1_conv_weight).reshape(4, 16, 16, 9).transpose(2, 0, 3, 1),
        "dil_bias": np.asarray(L1_conv_bias).reshape(4, 16).T,
        "kernel_all": kernel_all, "kernel_halo": kernel_halo,
        "w_in": w_in, "w_dw": w_dw, "filt": filt, "w_out": w_out,
    }
    arrays = {f"in_{k}": np.ascontiguousarray(v) for k, v in arrays.items()}
    tables = {f"const_{k}": v for k, v in consts.items()}
    nc = bacc.Bacc("TRN2", target_bir_lowering=False, num_devices=1)

    def declare(name, a):
        return nc.dram_tensor(name, a.shape, mybir.dt.from_np(a.dtype), kind="ExternalInput").ap()

    ins = {k[3:]: declare(k, v) for k, v in arrays.items()}
    const_aps = {k[6:]: declare(k, v) for k, v in tables.items()}
    y = nc.dram_tensor("out_y", [B, C, H, W], FP32, kind="ExternalOutput").ap()
    build(nc, B, consts=const_aps, y=y, **ins)
    r = run_bass_kernel_spmd(nc, [{**arrays, **tables}], core_ids=[0])
    return r.results[0]["out_y"]
```

```python
import numpy as np
import concourse.bass as bass
from concourse import mybir
from contextlib import ExitStack

FP32 = mybir.dt.float32
ALU = mybir.AluOpType
ACT = mybir.ActivationFunctionType

C, H, W = 64, 256, 256
P = 128
GROUPS = 32
MODES = 32
EPS = 1e-5
BANK = 512
CT = 8
NT = C // CT


class Stage:

    def __init__(self, nc, name):
        self.nc, self.name, self.stack = nc, name, ExitStack()

    def __enter__(self):
        self.stack.__enter__()
        return self

    def __exit__(self, *exc):
        return self.stack.__exit__(*exc)

    def sbuf(self, name, shape):
        return self.stack.enter_context(self.nc.sbuf_tensor(f"{self.name}_{name}", shape, FP32))

    def psum(self, name, shape):
        return self.stack.enter_context(self.nc.psum_tensor(f"{self.name}_{name}", shape, FP32))

    def sem(self, name):
        return self.stack.enter_context(self.nc.semaphore(f"{self.name}_{name}"))

    def block(self):
        return self.stack.enter_context(self.nc.Block())


def finish_statistics(nc, name, moments, n, averager, stores):
    with Stage(nc, name) as s:
        avg = s.sbuf("avg", [P, P])
        mean = s.sbuf("mean", [P, n])
        spread = s.sbuf("spread", [P, n])
        var = s.sbuf("var", [P, n])
        root = s.sbuf("root", [P, n])
        rstd = s.sbuf("rstd", [P, n])
        result = s.sbuf("result", [P, n, 2])
        mean_ps = s.psum("mean_ps", [P, BANK])
        var_ps = s.psum("var_ps", [P, BANK])
        avg_loaded = s.sem("avg_loaded")
        averaged = s.sem("averaged")
        step = s.sem("step")
        spread_ready = s.sem("spread_ready")
        var_ready = s.sem("var_ready")
        root_ready = s.sem("root_ready")
        result_ready = s.sem("result_ready")
        stored = s.sem("stored")
        pairs = stores(result)
        block = s.block()

        @block.sync
        def _(sp):
            sp.dma_start(avg[:, :], averager).then_inc(avg_loaded, 16)
            sp.wait_ge(result_ready, 1)
            for dst, src in pairs:
                sp.dma_start(dst, src).then_inc(stored, 16)
            sp.wait_ge(stored, 16 * len(pairs))

        @block.tensor
        def _(pe):
            pe.wait_ge(avg_loaded, 16)
            nc.tensor.matmul(mean_ps[:, 0:n], avg[:, :], moments[:, :, 0], start=True, stop=True).then_inc(averaged, 1)
            pe.wait_ge(spread_ready, 1)
            nc.tensor.matmul(var_ps[:, 0:n], avg[:, :], spread[:, :], start=True, stop=True).then_inc(averaged, 1)

        @block.scalar
        def _(act):
            act.wait_ge(var_ready, 1)
            nc.scalar.activation(root[:, :], var[:, :], ACT.Sqrt).then_inc(root_ready, 1)

        @block.vector
        def _(dve):
            done = [0]

            def chained(instruction):
                done[0] += 1
                instruction.then_inc(step, 1)
                dve.wait_ge(step, done[0])

            dve.wait_ge(averaged, 1)
            chained(nc.vector.tensor_copy(mean[:, :], mean_ps[:, 0:n]))
            chained(nc.vector.tensor_tensor(spread[:, :], moments[:, :, 0], mean[:, :], ALU.subtract))
            chained(nc.vector.tensor_tensor(spread[:, :], spread[:, :], spread[:, :], ALU.mult))
            nc.vector.tensor_tensor(spread[:, :], spread[:, :], moments[:, :, 1], ALU.add).then_inc(spread_ready, 1)
            dve.wait_ge(averaged, 2)
            nc.vector.tensor_scalar(var[:, :], var_ps[:, 0:n], EPS, None, ALU.add).then_inc(var_ready, 1)
            dve.wait_ge(root_ready, 1)
            chained(nc.vector.reciprocal(rstd[:, :], root[:, :]))
            chained(nc.vector.tensor_tensor(root[:, :], rstd[:, :], rstd[:, :], ALU.mult))
            chained(nc.vector.tensor_tensor(root[:, :], root[:, :], var[:, :], ALU.mult))
            chained(nc.vector.tensor_scalar(root[:, :], root[:, :], -0.5, 1.5, ALU.mult, ALU.add))
            chained(nc.vector.tensor_tensor(result[:, :, 0], rstd[:, :], root[:, :], ALU.mult))
            nc.vector.scalar_tensor_tensor(result[:, :, 1], mean[:, :], -1.0, result[:, :, 0],
                                           ALU.mult, ALU.mult).then_inc(result_ready, 1)


def row_layout_stores(stats_dram, B):
    def stores(result):
        src = result[0:1, :, :].rearrange("p (b g) k -> p b g k", b=B)
        dst = stats_dram.rearrange("b (g t) k -> t b g k", t=2)
        return [(dst[t:t + 1, b, :, :], src[:, b, :, :]) for t in range(2) for b in range(B)]
    return stores


def spectral_forward(nc, x, consts, moments, modes_in, B):
    K2 = 2 * MODES
    with Stage(nc, "fwd") as s:
        x_tile = [s.sbuf(f"x{i}", [P, 2, CT, W]) for i in range(2)]
        f_rows = s.sbuf("f_rows", [P, 2, K2])
        f_cols = s.sbuf("f_cols", [P, 2, 2, K2])
        col_modes = s.sbuf("col_modes", [P, 2, K2, C])
        stats = [s.sbuf(f"stats{i}", [P, CT // 2, 2, 6]) for i in range(2)]
        image_moments = s.sbuf("image_moments", [P, GROUPS, 2])
        rows_ps = [s.psum(f"rows_ps{i}", [P, 2, CT, K2]) for i in range(2)]
        QN = 4
        KQ = MODES // QN
        modes_ps = [s.psum(f"modes_ps{i}", [C, KQ, K2]) for i in range(QN)]
        consts_loaded = s.sem("consts_loaded")
        x_loaded = [s.sem(f"x_loaded{i}") for i in range(2)]
        x_transformed = s.sem("x_transformed")
        x_measured = s.sem("x_measured")
        cols_ready = s.sem("cols_ready")
        modes_done = s.sem("modes_done")
        modes_free = s.sem("modes_free")
        may_aggregate = s.sem("may_aggregate")
        aggregated = s.sem("aggregated")
        block = s.block()

        @block.sync
        def _(sp):
            sp.dma_start(f_rows[:, :, :], consts["f_rows"]).then_inc(consts_loaded, 16)
            sp.dma_start(f_cols[:, :, :, :], consts["f_cols"]).then_inc(consts_loaded, 16)

            def load(b, t):
                for half in range(2):
                    src = x[b, t * CT:(t + 1) * CT, half * P:(half + 1) * P, :].rearrange("c h w -> h c w")
                    sp.dma_start(x_tile[t % 2][:, half, :, :], src).then_inc(x_loaded[t % 2], 16)

            with sp.Fori(0, B) as b:
                for t in range(NT):
                    sp.wait_ge(x_transformed, b * NT + t + 1)
                    sp.wait_ge(x_measured, b * NT + t + 1)
                    load(b, t)

        @block.tensor
        def _(pe):
            nc.tensor.sem_inc(x_transformed, 2)
            pe.wait_ge(consts_loaded, 32)
            with pe.Fori(0, B) as b:
                for t in range(NT):
                    pe.wait_ge(x_loaded[t % 2], b * (32 * NT // 2) + 32 * (t // 2 + 1))
                    pe.wait_ge(cols_ready, b * NT + t + 1)
                    for half_w in range(2):
                        for c in range(CT):
                            for half in range(2):
                                last = nc.tensor.matmul(
                                    rows_ps[t % 2][:, half_w, c, :],
                                    x_tile[t % 2][:, half, c, half_w * P:(half_w + 1) * P],
                                    f_rows[:, half, :], start=(half == 0), stop=(half == 1))
                    last.then_inc(x_transformed, 1)
                pe.wait_ge(cols_ready, b * NT + NT + 2)
                for q in range(QN):
                    pe.wait_ge(modes_free, b * QN + q + 1)
                    for k in range(KQ):
                        kx = q * KQ + k
                        n = 0
                        for half_w in range(2):
                            for part in range(2):
                                last = nc.tensor.matmul(
                                    modes_ps[q][:, k, :], col_modes[:, half_w, part * MODES + kx, :],
                                    f_cols[:, half_w, part, :], start=(n == 0), stop=(n == 3))
                                n += 1
                    last.then_inc(modes_done, 1)
            

        @block.scalar
        def _(act):
            nc.scalar.sem_inc(cols_ready, 2)
            with act.Fori(0, B) as b:
                act.wait_ge(modes_done, b * QN)
                for t in range(NT):
                    act.wait_ge(x_transformed, b * NT + t + 3)
                    for half_w in range(2):
                        last = nc.scalar.activation(
                            col_modes[:, half_w, :, t * CT:(t + 1) * CT].rearrange("p k c -> p c k"),
                            rows_ps[t % 2][:, half_w, :, :], ACT.Copy)
                    last.then_inc(cols_ready, 1)

        @block.vector
        def _(dve):
            nc.vector.sem_inc(x_measured, 2)
            nc.vector.sem_inc(modes_free, QN)
            mo = moments[:, :, :].rearrange("p (b g) k -> p b g k", b=B)
            with dve.Fori(0, B) as b:
                for t in range(NT):
                    dve.wait_ge(x_loaded[t % 2], b * (32 * NT // 2) + 32 * (t // 2 + 1))
                    for j in range(CT // 2):
                        for half in range(2):
                            last = nc.vector.bn_stats(stats[t % 2][:, j, half, :],
                                                      x_tile[t % 2][:, half, 2 * j:2 * j + 2, :])
                    last.then_inc(x_measured, 1)
                    dve.wait_ge(x_measured, b * NT + t + 3)
                    nc.vector.sem_inc(may_aggregate, 1)
                    for j in range(CT // 2):
                        last = nc.vector.bn_aggr(image_moments[:, t * CT // 2 + j, :], stats[t % 2][:, j, :, :])
                last.then_inc(aggregated, 1)
                dve.wait_ge(aggregated, b + 1)
                nc.vector.tensor_copy(mo[:, b, :, :], image_moments[:, :, :])
                for q in range(QN):
                    dve.wait_ge(modes_done, b * QN + q + 1)
                    re = modes_ps[q][:, :, 0:MODES]
                    im = modes_ps[q][:, :, MODES:K2]
                    dst = modes_in[:, q * KQ:(q + 1) * KQ, :, :]
                    nc.vector.tensor_copy(dst[0:C, :, :, b], re)
                    nc.vector.tensor_scalar(dst[C:P, :, :, b], im, -1.0, None, ALU.mult)
                    nc.vector.tensor_copy(dst[0:C, :, :, B + b], im)
                    nc.vector.tensor_copy(dst[C:P, :, :, B + b], re).then_inc(modes_free, 1)


def spectral_mix(nc, w_real, w_imag, stats_dram, modes_in, modes_out, B):
    MC = 4 * MODES
    NCH = MODES * MODES // MC
    MB = BANK // C
    NB = MC // MB
    with Stage(nc, "mix") as s:
        norm = s.sbuf("norm", [P, B, 2])
        scale = s.sbuf("scale", [P, 2, B])
        shift = s.sbuf("shift", [P, B])
        w = [s.sbuf(f"w{i}", [P, C, MC]) for i in range(2)]
        chunk = [s.sbuf(f"chunk{i}", [P, MC, 2 * B]) for i in range(2)]
        mixed = s.sbuf("mixed", [2 * B, MC, C])
        mixed_ps = [s.psum(f"mixed_ps{i}", [2 * B, MB, C]) for i in range(8)]
        norm_loaded = s.sem("norm_loaded")
        w_loaded = [s.sem(f"w_loaded{i}") for i in range(2)]
        step = s.sem("step")
        normalised = s.sem("normalised")
        chunk_ready = s.sem("chunk_ready")
        chunk_mixed = s.sem("chunk_mixed")
        bank_mixed = s.sem("bank_mixed")
        bank_free = s.sem("bank_free")
        may_store = s.sem("may_store")
        out_stored = s.sem("out_stored")
        block = s.block()
        flat_in = modes_in[:, :, :, :].rearrange("p x y n -> p (x y) n")

        @block.sync
        def _(sp):
            for half in range(2):
                sp.dma_start(norm[half * C:(half + 1) * C, :, :],
                             stats_dram.rearrange("b c k -> c b k")).then_inc(norm_loaded, 16)
            with sp.Fori(0, NCH // 2) as pair:
                for i in range(2):
                    sp.wait_ge(chunk_mixed, pair * 2 + i + 1)
                    for half, src in enumerate((w_real, w_imag)):
                        sp.dma_start(w[i][half * C:(half + 1) * C, :, :],
                                     src.rearrange("c o x y -> c o (x y)")[:, :, bass.ds((pair * 2 + i) * MC, MC)]
                                     ).then_inc(w_loaded[i], 16)

        @block.gpsimd
        def _(pool):
            with pool.Fori(0, NCH) as ch:
                pool.wait_ge(bank_free, ch * NB + NB + 8)
                nc.gpsimd.sem_inc(may_store, 1)
                pool.dma_start(modes_out[:, bass.ds(ch * MC, MC), :], mixed[:, :, :]).then_inc(out_stored, 16)
            pool.wait_ge(out_stored, 16 * NCH)

        @block.scalar
        def _(act):
            act.wait_ge(normalised, 1)
            with act.Fori(0, NCH // 2) as pair:
                for i in range(2):
                    act.wait_ge(chunk_mixed, pair * 2 + i + 1)
                    nc.scalar.activation(chunk[i][:, :, :], flat_in[:, bass.ds((pair * 2 + i) * MC, MC), :],
                                         ACT.Copy).then_inc(chunk_ready, 1)

        @block.tensor
        def _(pe):
            nc.tensor.sem_inc(chunk_mixed, 2)
            with pe.Fori(0, NCH // 2) as pair:
                for i in range(2):
                    pe.wait_ge(chunk_ready, pair * 2 + i + 1)
                    pe.wait_ge(w_loaded[i], pair * 32 + 32)
                    for k in range(NB):
                        pe.wait_ge(bank_free, pair * (2 * NB) + i * NB + k + 1)
                        for j in range(MB):
                            m = k * MB + j
                            last = nc.tensor.matmul(mixed_ps[k % 8][:, j, :], chunk[i][:, m, :], w[i][:, :, m],
                                                    start=True, stop=True)
                        if k < NB - 1:
                            last.then_inc(bank_mixed, 1)
                    last.then_inc(bank_mixed, 1)
                    pe.wait_ge(bank_mixed, pair * (2 * NB) + (i + 1) * NB)
                    nc.tensor.sem_inc(chunk_mixed, 1)

        @block.vector
        def _(dve):
            done = [0]

            def chained(instruction):
                done[0] += 1
                instruction.then_inc(step, 1)
                dve.wait_ge(step, done[0])

            nc.vector.sem_inc(bank_free, 8)
            dve.wait_ge(norm_loaded, 32)
            nc.vector.tensor_copy(scale[:, 0, :], norm[:, :, 0])
            chained(nc.vector.tensor_copy(scale[:, 1, :], norm[:, :, 0]))
            chained(nc.vector.tensor_scalar(shift[:, :], norm[:, :, 1], float(H * W) ** 0.5, None, ALU.mult))
            flat_scale = scale[:, :, :].rearrange("p k b -> p (k b)")
            chained(nc.vector.tensor_tensor(
                flat_in, flat_in, flat_scale.unsqueeze(1).to_broadcast([P, MODES * MODES, 2 * B]), ALU.mult))
            nc.vector.tensor_tensor(flat_in[0:C, 0, 0:B], flat_in[0:C, 0, 0:B], shift[0:C, :], ALU.add)
            nc.vector.tensor_tensor(flat_in[C:P, 0, B:2 * B], flat_in[C:P, 0, B:2 * B], shift[C:P, :],
                                    ALU.add).then_inc(normalised, 1)
            with dve.Fori(0, NCH) as ch:
                dve.wait_ge(out_stored, ch * 16)
                for k in range(NB):
                    dve.wait_ge(bank_mixed, ch * NB + k + 1)
                    nc.vector.tensor_copy(mixed[:, k * MB:(k + 1) * MB, :], mixed_ps[k % 8][:, :, :]
                                          ).then_inc(bank_free, 1)


def spectral_inverse(nc, x, y, consts, modes_out, moments, B):
    K2 = 2 * MODES
    NX = 3
    with Stage(nc, "inv") as s:
        x_tile = [s.sbuf(f"x{i}", [P, 2, CT, W]) for i in range(4)]
        g_cols = s.sbuf("g_cols", [P, W])
        g_rows = s.sbuf("g_rows", [P, 2, P])
        modes = [s.sbuf(f"modes{i}", [P, 2, MODES, C]) for i in range(2)]
        rows = [s.sbuf(f"rows{i}", [P, CT, W]) for i in range(2)]
        stats = [s.sbuf(f"stats{i}", [P, CT // 2, 2, 6]) for i in range(2)]
        image_moments = s.sbuf("image_moments", [P, GROUPS, 2])
        HT = CT // 2
        rows_ps = [s.psum(f"rows_ps{i}", [K2, HT, W]) for i in range(2)]
        y_ps = [s.psum(f"y_ps{i}", [P, 2, W]) for i in range(4)]
        consts_loaded = s.sem("consts_loaded")
        x_loaded = [s.sem(f"x_loaded{i}") for i in range(4)]
        y_stored = [s.sem(f"y_stored{i}") for i in range(4)]
        modes_loaded = [s.sem(f"modes_loaded{i}") for i in range(2)]
        modes_ready = s.sem("modes_ready")
        modes_used = s.sem("modes_used")
        rows_done = s.sem("rows_done")
        rows_ready = s.sem("rows_ready")
        y_done = s.sem("y_done")
        y_added = s.sem("y_added")
        measured = s.sem("measured")
        may_aggregate = s.sem("may_aggregate")
        aggregated = s.sem("aggregated")
        cleared = s.sem("cleared")
        may_store = s.sem("may_store")
        block = s.block()

        def rows_of(t, b, i, dram):
            return dram[b * 2 + i, t * CT:(t + 1) * CT, :, :].rearrange("c (f h) w -> f h c w", f=2)

        @block.sync
        def _(sp):
            sp.dma_start(g_cols[:, :], consts["g_cols"]).then_inc(consts_loaded, 16)
            sp.dma_start(g_rows[:, :, :], consts["g_rows"]).then_inc(consts_loaded, 16)
            with sp.Fori(0, B // 2) as pair:
                for i in range(2):
                    sp.wait_ge(modes_used, pair * 2 + i + 1)
                    for top in range(2):
                        for part in range(2):
                            src = modes_out.rearrange("(r b) (x y) o -> r b y x o", r=2, y=MODES)
                            sp.dma_start(modes[i][top * MODES:(top + 1) * MODES, part, :, :],
                                         src[part ^ top, pair * 2 + i]).then_inc(modes_loaded[i], 16)
                    for t in range(NT):
                        n = (i * NT + t) % 4
                        sp.wait_ge(y_stored[n], pair * (32 * NT // 2) + 32 * ((i * NT + t) // 4))
                        for half in range(2):
                            sp.dma_start(x_tile[n][:, half, :, :], rows_of(t, pair, i, x)[half]
                                         ).then_inc(x_loaded[n], 16)

        @block.gpsimd
        def _(pool):
            with pool.Fori(0, B // 2) as pair:
                for m in range(2 * NT):
                    i, t = divmod(m, NT)
                    pool.wait_ge(measured, pair * (2 * NT) + m + 1)
                    nc.gpsimd.sem_inc(may_store, 1)
                    for half in range(2):
                        pool.dma_start(rows_of(t, pair, i, y)[half], x_tile[m % 4][:, half, :, :]
                                       ).then_inc(y_stored[m % 4], 16)
            for n in range(4):
                pool.wait_ge(y_stored[n], 32 * (B * NT // 4))

        @block.tensor
        def _(pe):
            nc.tensor.sem_inc(modes_used, 2)
            pe.wait_ge(consts_loaded, 32)
            pe.wait_ge(cleared, 1)
            with pe.Fori(0, B // 2) as pair:
                for m in range(2 * NT):
                    i, t = divmod(m, NT)
                    if t == 0:
                        pe.wait_ge(modes_ready, pair * 2 + i + 1)
                    for part in range(2):
                        pe.wait_ge(rows_ready, pair * (4 * NT) + 2 * m + part + 1)
                        for c in range(HT):
                            last = nc.tensor.matmul(
                                rows_ps[part][:, c, :],
                                modes[i][:, :, :, t * CT + part * HT + c].rearrange("p r k -> p (r k)"),
                                g_cols[:, :], start=True, stop=True)
                        last.then_inc(rows_done, 1)
                    if t == NT - 1:
                        pe.wait_ge(rows_done, pair * (4 * NT) + 2 * m + 2)
                        nc.tensor.sem_inc(modes_used, 1)
                    for part in range(2):
                        pe.wait_ge(rows_ready, pair * (4 * NT) + 2 * m + part + 3)
                        for j in range(HT // 2):
                            for half in range(2):
                                u = part * HT + j * 2 + half
                                pe.wait_ge(y_added, pair * (16 * NT) + 8 * m + u + 1)
                                c0 = part * HT + 2 * j
                                nc.tensor.matmul(y_ps[u % 4][:, :, :], g_rows[:, half, :],
                                                 rows[m % 2][:, c0:c0 + 2, :],
                                                 start=True, stop=True).then_inc(y_done, 1)

        @block.scalar
        def _(act):
            nc.scalar.sem_inc(rows_ready, 2)
            with act.Fori(0, B // 2) as pair:
                for m in range(2 * NT):
                    i, t = divmod(m, NT)
                    if t == 0:
                        act.wait_ge(modes_loaded[i], pair * 64 + 64)
                        nc.scalar.activation(modes[i][MODES:K2, 1, :, :], modes[i][MODES:K2, 1, :, :],
                                             ACT.Copy, scale=-1.0).then_inc(modes_ready, 1)
                    for part in range(2):
                        act.wait_ge(rows_done, pair * (4 * NT) + 2 * m + part + 1)
                        nc.scalar.activation(rows[m % 2][0:K2, part * HT:(part + 1) * HT, :], rows_ps[part][:, :, :],
                                             ACT.Copy).then_inc(rows_ready, 1)

        @block.vector
        def _(dve):
            for i in range(2):
                nc.vector.memset(modes[i][K2:P, :, :, :], 0.0)
                last = nc.vector.memset(rows[i][K2:P, :, :], 0.0)
            last.then_inc(cleared, 1)
            nc.vector.sem_inc(y_added, 4)
            mo = moments[:, :, :].rearrange("p (b i g) k -> p b i g k", b=B // 2, i=2)
            with dve.Fori(0, B // 2) as pair:
                for m in range(2 * NT):
                    i, t = divmod(m, NT)
                    n = m % 4
                    dve.wait_ge(x_loaded[n], pair * (32 * NT // 2) + 32 * (m // 4) + 32)
                    for j in range(CT // 2):
                        for half in range(2):
                            u = 2 * j + half
                            here = x_tile[n][:, half, 2 * j:2 * j + 2, :]
                            dve.wait_ge(y_done, pair * (16 * NT) + 8 * m + u + 1)
                            nc.vector.tensor_tensor(here, y_ps[u % 4][:, :, :], here, ALU.add).then_inc(y_added, 1)
                            if u >= 1:
                                pj, ph = divmod(u - 1, 2)
                                dve.wait_ge(y_added, pair * (16 * NT) + 8 * m + u + 4)
                                nc.vector.bn_stats(stats[m % 2][:, pj, ph, :],
                                                   x_tile[n][:, ph, 2 * pj:2 * pj + 2, :])
                    dve.wait_ge(y_added, pair * (16 * NT) + 8 * m + 8 + 4)
                    nc.vector.bn_stats(stats[m % 2][:, CT // 2 - 1, 1, :],
                                       x_tile[n][:, 1, CT - 2:CT, :]).then_inc(measured, 1)
                    dve.wait_ge(measured, pair * (2 * NT) + m + 1)
                    nc.vector.sem_inc(may_aggregate, 1)
                    for j in range(CT // 2):
                        last = nc.vector.bn_aggr(image_moments[:, t * CT // 2 + j, :], stats[m % 2][:, j, :, :])
                    if t == NT - 1:
                        last.then_inc(aggregated, 1)
                        dve.wait_ge(aggregated, pair * 2 + i + 1)
                        nc.vector.tensor_copy(mo[:, pair, i, :, :], image_moments[:, :, :])


def constants():
    k = np.arange(MODES)
    h = np.arange(H)
    ang = 2 * np.pi * np.outer(h, k) / H
    root = np.sqrt(float(H))
    cos, sin = np.cos(ang) / root, np.sin(ang) / root
    double = np.where(k == 0, 1.0, 2.0)
    f_rows = np.concatenate([cos, -sin], 1).reshape(2, P, 2 * MODES).transpose(1, 0, 2)
    f_cols = np.stack([np.concatenate([cos, -sin], 1), np.concatenate([sin, cos], 1)], 1)
    f_cols = f_cols.reshape(2, P, 2, 2 * MODES).transpose(1, 0, 2, 3)
    g_cols = np.concatenate([(cos * double).T, -(sin * double).T], 0)
    g_rows = np.concatenate([cos.T, -sin.T], 0).reshape(2 * MODES, 2, P)
    zeros = P - 2 * MODES
    g_cols = np.pad(g_cols, ((0, zeros), (0, 0)))
    g_rows = np.pad(g_rows, ((0, zeros), (0, 0), (0, 0)))
    out = {"f_rows": f_rows, "f_cols": f_cols, "g_cols": g_cols, "g_rows": g_rows,
           "average_all": np.full((P, P), 1.0 / P)}
    return {n: np.ascontiguousarray(v, dtype=np.float32) for n, v in out.items()}


def pair_constants():
    CG, SL = 16, 8
    p = np.arange(P)
    pair = (p % CG) // 2
    masks = np.ones((P, 2))
    masks[:CG, 0] = 0.0
    masks[-CG:, 1] = 0.0
    out = {"average_pairs": (pair[:, None] == pair[None, :]) / (2.0 * SL), "slab_masks": masks}
    return {n: np.ascontiguousarray(v, dtype=np.float32) for n, v in out.items()}


def channel_layout_stores(stats_dram, B):
    def stores(result):
        src = result[0:16, :, :].rearrange("c (b q) k -> c b q k", b=B)
        dst = stats_dram.rearrange("b (q c) k -> c b q k", c=16)
        return [(dst[:, b, :, :], src[:, b, :, :]) for b in range(B)]
    return stores


def dilated_conv(nc, x, y, taps_dram, bias_dram, stats_dram, slab_masks, moments, B):
    DIL = (1, 6, 12, 18)
    NG, CG = len(DIL), C // len(DIL)
    SL = P // CG
    SR = H // SL
    RC = BANK // W
    NCHUNK = SR // RC
    CB = 4
    halo = [max(DIL[i::2]) for i in range(2)]
    with Stage(nc, "dil") as s:
        tile = [s.sbuf(f"tile{i}", [P, SR + 2 * halo[i], W + 2 * halo[i]]) for i in range(2)]
        out = [s.sbuf(f"out{i}", [P, CB * RC, W]) for i in range(2)]
        taps = s.sbuf("taps", [P, NG, 9, P])
        bias = s.sbuf("bias", [P, NG])
        masks = s.sbuf("masks", [P, 2])
        norm = [s.sbuf(f"norm{i}", [P, 2]) for i in range(2)]
        norm_halo = [s.sbuf(f"norm_halo{i}", [P, 2, 2]) for i in range(2)]
        stats = s.sbuf("stats", [P, NCHUNK, 6])
        group_moments = s.sbuf("group_moments", [P, NG, 2])
        ps = [s.psum(f"ps{i}", [P, RC, W]) for i in range(8)]
        cleared = s.sem("cleared")
        consts_loaded = s.sem("consts_loaded")
        tile_loaded = [s.sem(f"tile_loaded{i}") for i in range(2)]
        scales_ready = s.sem("scales_ready")
        tile_ready = s.sem("tile_ready")
        tile_used = s.sem("tile_used")
        chunk_done = s.sem("chunk_done")
        chunk_added = s.sem("chunk_added")
        out_loaded = [s.sem(f"out_loaded{i}") for i in range(2)]
        out_ready = s.sem("out_ready")
        out_stored = [s.sem(f"out_stored{i}") for i in range(2)]
        may_copy = s.sem("may_copy")
        may_aggregate = s.sem("may_aggregate")
        aggregated = s.sem("aggregated")
        block = s.block()
        NBLK = NCHUNK // CB

        def load_tile(sp, b, g):
            i, d = g % 2, DIL[g]
            hl = halo[i]
            cs = slice(g * CG, (g + 1) * CG)
            for s0, s1, up, down in ((0, 1, 0, d), (1, SL - 1, d, d), (SL - 1, SL, d, 0)):
                for sl in range(s0, s1):
                    r0, r1 = sl * SR - up, (sl + 1) * SR + down
                    sp.dma_start(tile[i][sl * CG:(sl + 1) * CG, hl - up:hl + SR + down, hl:hl + W],
                                 x[b, cs, r0:r1, :]).then_inc(tile_loaded[i], 16)
            for sl in range(SL):
                sp.dma_start(norm[i][sl * CG:(sl + 1) * CG, :], stats_dram[b, cs, :]).then_inc(tile_loaded[i], 16)
        TL = 16 * (2 * SL)

        def block_rows(b, g, k, dram):
            v = dram[b, g * CG:(g + 1) * CG, :, :].rearrange("c (s r) w -> s c r w", s=SL)
            return v[:, :, k * CB * RC:(k + 1) * CB * RC, :]

        @block.sync
        def _(sp):
            sp.wait_ge(cleared, 3)
            for sl in range(SL):
                sl_p = slice(sl * CG, (sl + 1) * CG)
                sp.dma_start(taps[sl_p, :, :, sl_p], taps_dram).then_inc(consts_loaded, 16)
                sp.dma_start(bias[sl_p, :], bias_dram).then_inc(consts_loaded, 16)
            sp.dma_start(masks[:, :], slab_masks).then_inc(consts_loaded, 16)
            with sp.Fori(0, B) as b:
                for g in range(NG):
                    sp.wait_ge(tile_used, b * NG + g + 1)
                    load_tile(sp, b, g)

        @block.gpsimd
        def _(pool):
            for i in range(2):
                nc.gpsimd.memset(tile[i][:, :, :], 0.0).then_inc(cleared, 1)
            with pool.Fori(0, B) as b:
                for g in range(NG):
                    for k in range(NBLK):
                        n = (g * NBLK + k) % 2
                        m = b * (NG * NBLK // 2) + (g * NBLK + k) // 2
                        pool.wait_ge(out_stored[n], m * (16 * SL))
                        nc.gpsimd.sem_inc(may_copy, 1)
                        for sl in range(SL):
                            pool.dma_start(out[n][sl * CG:(sl + 1) * CG, :, :], block_rows(b, g, k, x)[sl]
                                           ).then_inc(out_loaded[n], 16)
                        pool.wait_ge(out_ready, b * (NG * NBLK) + g * NBLK + k + 1)
                        nc.gpsimd.sem_inc(may_copy, 1)
                        for sl in range(SL):
                            pool.dma_start(block_rows(b, g, k, y)[sl], out[n][sl * CG:(sl + 1) * CG, :, :]
                                           ).then_inc(out_stored[n], 16)
            for n in range(2):
                pool.wait_ge(out_stored[n], B * NG * NBLK // 2 * (16 * SL))

        @block.scalar
        def _(act):
            act.wait_ge(consts_loaded, 16 * (2 * SL + 1))
            with act.Fori(0, B) as b:
                for g in range(NG):
                    i, d = g % 2, DIL[g]
                    hl = halo[i]
                    act.wait_ge(tile_loaded[i], b * (TL * NG // 2) + TL * (g // 2 + 1))
                    for m in range(2):
                        last = nc.scalar.activation(norm_halo[i][:, m, :], norm[i][:, :], ACT.Copy,
                                                    scale=masks[:, m:m + 1])
                    last.then_inc(scales_ready, 1)
                    act.wait_ge(scales_ready, b * NG + g + 1)
                    cols = slice(hl, hl + W)
                    for rows, sc in ((slice(hl - d, hl), norm_halo[i][:, 0, :]),
                                     (slice(hl, hl + SR), norm[i][:, :]),
                                     (slice(hl + SR, hl + SR + d), norm_halo[i][:, 1, :])):
                        last = nc.scalar.activation(tile[i][:, rows, cols], tile[i][:, rows, cols], ACT.Identity,
                                                    scale=sc[:, 0:1], bias=sc[:, 1:2])
                    last.then_inc(tile_ready, 1)

        @block.tensor
        def _(pe):
            nc.tensor.sem_inc(tile_used, 2)
            pe.wait_ge(consts_loaded, 16 * (2 * SL + 1))
            with pe.Fori(0, B) as b:
                for g in range(NG):
                    i, d = g % 2, DIL[g]
                    hl = halo[i]
                    pe.wait_ge(tile_ready, b * NG + g + 1)
                    for k in range(NCHUNK):
                        pe.wait_ge(chunk_added, b * (NG * NCHUNK) + g * NCHUNK + k + 1)
                        for t in range(9):
                            r0 = hl + k * RC + (t // 3 - 1) * d
                            c0 = hl + (t % 3 - 1) * d
                            last = nc.tensor.matmul(ps[k % 8][:, :, :], taps[:, g, t, :],
                                                    tile[i][:, r0:r0 + RC, c0:c0 + W],
                                                    start=(t == 0), stop=(t == 8))
                        last.then_inc(chunk_done, 1)
                    pe.wait_ge(chunk_done, b * (NG * NCHUNK) + (g + 1) * NCHUNK)
                    nc.tensor.sem_inc(tile_used, 1)

        @block.vector
        def _(dve):
            nc.vector.memset(taps[:, :, :, :], 0.0).then_inc(cleared, 1)
            nc.vector.sem_inc(chunk_added, 8)
            dve.wait_ge(consts_loaded, 16 * (2 * SL + 1))
            mo = moments[:, :, :].rearrange("p (b q) k -> p b q k", b=B)

            with dve.Fori(0, B) as b:
                for g in range(NG):
                    for k in range(NCHUNK):
                        blk, j = divmod(k, CB)
                        n = (g * NBLK + blk) % 2
                        m = b * (NG * NBLK // 2) + (g * NBLK + blk) // 2
                        if j == 0:
                            dve.wait_ge(out_loaded[n], m * (16 * SL) + 16 * SL)
                        done = b * (NG * NCHUNK) + g * NCHUNK + k
                        dve.wait_ge(chunk_done, done + 1)
                        here = out[n][:, j * RC:(j + 1) * RC, :]
                        nc.vector.scalar_tensor_tensor(here, ps[k % 8][:, :, :], bias[:, g:g + 1], here,
                                                       ALU.add, ALU.add).then_inc(chunk_added, 1)
                        dve.wait_ge(chunk_added, done + 9)
                        last = nc.vector.bn_stats(stats[:, k, :], here)
                        if j == CB - 1:
                            last.then_inc(out_ready, 1)
                    dve.wait_ge(out_ready, b * (NG * NBLK) + (g + 1) * NBLK)
                    nc.vector.sem_inc(may_aggregate, 1)
                    nc.vector.bn_aggr(group_moments[:, g, :], stats[:, :, :]).then_inc(aggregated, 1)
                    if g == NG - 1:
                        dve.wait_ge(aggregated, b * NG + NG)
                        nc.vector.tensor_copy(mo[:, b, :, :], group_moments[:, :, :])


KS = 7
KR = KS // 2


def depthwise_mish(nc, x, y, consts, kernel_all, kernel_halo, stats_dram, moments, B):
    NS, NU = 4, 4
    UC = CT // 2
    HALO = (0, 32)
    with Stage(nc, "dw") as s:
        x_tile = [s.sbuf(f"x{i}", [P, 2, CT, W]) for i in range(NS)]
        norm = [s.sbuf(f"norm{i}", [P, CT, 2]) for i in range(NS)]
        padded = [s.sbuf(f"padded{i}", [P, 2, CT, W + 2 * KR]) for i in range(2)]
        edge = [s.sbuf(f"edge{i}", [P, CT, W]) for i in range(2)]
        band = s.sbuf("band", [P, KS, P])
        band_edge = s.sbuf("band_edge", [P, 2, P])
        k_all = s.sbuf("k_all", [P, KS * KS])
        k_halo = s.sbuf("k_halo", [P, KS])
        place = s.sbuf("place", [P, KS, P])
        place_halo = s.sbuf("place_halo", [P, 2, KS, P])
        capped = [s.sbuf(f"capped{i}", [P, UC, W]) for i in range(2)]
        power = [s.sbuf(f"power{i}", [P, UC, W]) for i in range(2)]
        denom = s.sbuf("denom", [P, UC, W])
        numer = s.sbuf("numer", [P, UC, W])
        stats = s.sbuf("stats", [P, CT // 2, 2, 6])
        image_moments = s.sbuf("image_moments", [P, GROUPS, 2])
        ps = [s.psum(f"ps{i}", [P, UC, W]) for i in range(NU)]
        consts_loaded = s.sem("consts_loaded")
        cleared = s.sem("cleared")
        bands_ready = s.sem("bands_ready")
        step = s.sem("step")
        x_loaded = [s.sem(f"x_loaded{i}") for i in range(NS)]
        y_stored = [s.sem(f"y_stored{i}") for i in range(NS)]
        normalised = s.sem("normalised")
        edges_loaded = [s.sem(f"edges_loaded{i}") for i in range(2)]
        padded_used = s.sem("padded_used")
        conv_done = s.sem("conv_done")
        cap_ready = s.sem("cap_ready")
        exp_ready = s.sem("exp_ready")
        chain = s.sem("chain")
        unit_free = s.sem("unit_free")
        y_ready = s.sem("y_ready")
        may_aggregate = s.sem("may_aggregate")
        aggregated = s.sem("aggregated")
        summed = s.sem("summed")
        may_copy = s.sem("may_copy")
        may_normalise = s.sem("may_normalise")
        CH = 4
        XL = 16 * 3
        block = s.block()

        def rows_of(dram, b, t):
            return dram[b, t * CT:(t + 1) * CT, :, :].rearrange("c (f h) w -> f h c w", f=2)

        def images(eng, image):
            if B > 1:
                with eng.Fori(0, B - 1) as b:
                    image(b, False)
            image(B - 1, True)

        @block.sync
        def _(sp):
            for dst, src in ((k_all[:, :], kernel_all), (place[:, :, :], consts["place"]),
                             (place_halo[:, :, :, :], consts["place_halo"]), (k_halo[:, :], kernel_halo)):
                sp.dma_start(dst, src).then_inc(consts_loaded, 16)

            def load(b, t, first=False):
                n = t % NS
                if not first:
                    sp.wait_ge(y_stored[n], b * (32 * NT // NS) + 32 * (t // NS))
                for half in range(2):
                    sp.dma_start(x_tile[n][:, half, :, :], rows_of(x, b, t)[half]).then_inc(x_loaded[n], 16)
                sp.dma_start(norm[n][:, :, :], stats_dram[b, t * CT:(t + 1) * CT, :].partition_broadcast(P)
                             ).then_inc(x_loaded[n], 16)

            AHEAD = NS - 1
            for t in range(AHEAD):
                load(0, t, True)

            def image(b, last):
                for t in range(NT):
                    sp.wait_ge(y_ready, b * NT + t + 1)
                    for half in range(2):
                        sp.dma_start(rows_of(y, b, t)[half], x_tile[t % NS][:, half, :, :]
                                     ).then_inc(y_stored[t % NS], 16)
                    nt = t + AHEAD
                    if nt < NT:
                        load(b, nt) if not (isinstance(b, int) and b == 0 and nt < NS) else load(b, nt, True)
                    elif not last:
                        load(b + 1, nt - NT)

            images(sp, image)
            for n in range(NS):
                sp.wait_ge(y_stored[n], 32 * (B * NT // NS))

        @block.gpsimd
        def _(pool):
            for i in range(2):
                nc.gpsimd.memset(padded[i][:, :, :, :], 0.0)
                nc.gpsimd.memset(edge[i][:, :, :], 0.0).then_inc(cleared, 1)
            pool.wait_ge(cleared, 2)
            with pool.Fori(0, B) as b:
                for t in range(NT):
                    i = t % 2
                    pool.wait_ge(normalised, b * NT + t + 1)
                    nc.gpsimd.sem_inc(may_copy, 1)
                    for kw in range(KS):
                        p0 = HALO[0] + KR * kw
                        pool.dma_start(edge[i][p0:p0 + KR, :, :], padded[i][0:KR, 1, :, kw:kw + W]
                                       ).then_inc(edges_loaded[i], 16)
                        p1 = HALO[1] + KR * kw
                        pool.dma_start(edge[i][p1:p1 + KR, :, :], padded[i][P - KR:P, 0, :, kw:kw + W]
                                       ).then_inc(edges_loaded[i], 16)

        @block.scalar
        def _(act):
            act.wait_ge(cleared, 2)

            def exps(n0, t, units):
                for u in units:
                    act.wait_ge(cap_ready, n0 * NU + t * NU + u + 1)
                    nc.scalar.activation(power[u % 2][:, :, :], capped[u % 2][:, :, :], ACT.Exp).then_inc(exp_ready, 1)

            def normalise(b, t):
                i, n = t % 2, t % NS
                act.wait_ge(x_loaded[n], b * (XL * NT // NS) + XL * (t // NS) + XL)
                act.wait_ge(padded_used, b * NT + t + 1)
                nc.scalar.sem_inc(may_normalise, 1)
                for j in range(CT // 2):
                    for half in range(2):
                        last = nc.scalar.activation(
                            padded[i][:, half, 2 * j:2 * j + 2, KR:KR + W], x_tile[n][:, half, 2 * j:2 * j + 2, :],
                            ACT.Identity, scale=norm[n][:, 2 * j, 0:1], bias=norm[n][:, 2 * j, 1:2])
                last.then_inc(normalised, 1)

            normalise(0, 0)

            def image(b, last):
                for t in range(NT):
                    exps(b * NT, t, (0,))
                    if t < NT - 1:
                        normalise(b, t + 1)
                    elif not last:
                        normalise(b + 1, 0)
                    exps(b * NT, t, (1, 2, 3))

            images(act, image)

        @block.tensor
        def _(pe):
            nc.tensor.sem_inc(padded_used, 2)
            pe.wait_ge(bands_ready, 1)
            with pe.Fori(0, B) as b:
                for t in range(NT):
                    i = t % 2
                    pe.wait_ge(normalised, b * NT + t + 1)
                    pe.wait_ge(edges_loaded[i], b * (16 * 2 * KS * NT // 2) + 16 * 2 * KS * (t // 2 + 1))
                    for u in range(NU):
                        part, half = divmod(u, 2)
                        pe.wait_ge(unit_free, b * (NT * NU) + t * NU + u + 1)
                        for j in range(UC // 2):
                            c0 = part * UC + 2 * j
                            for kw in range(KS):
                                nc.tensor.matmul(ps[u][:, 2 * j:2 * j + 2, :], band[:, kw, :],
                                                 padded[i][:, half, c0:c0 + 2, kw:kw + W],
                                                 start=(kw == 0), stop=False)
                            last = nc.tensor.matmul(ps[u][:, 2 * j:2 * j + 2, :], band_edge[:, half, :],
                                                    edge[i][:, c0:c0 + 2, :], start=False, stop=True)
                        last.then_inc(conv_done, 1)
                    pe.wait_ge(conv_done, b * (NT * NU) + (t + 1) * NU)
                    nc.tensor.sem_inc(padded_used, 1)

        @block.vector
        def _(dve):
            done = [0]

            def chained(instruction):
                done[0] += 1
                instruction.then_inc(step, 1)
                dve.wait_ge(step, done[0])

            dve.wait_ge(consts_loaded, 64)
            for a in range(KS):
                for kw in range(KS):
                    w = k_all[:, a * KS + kw:a * KS + kw + 1]
                    if a == 0:
                        last = nc.vector.tensor_scalar(band[:, kw, :], place[:, a, :], w, None, ALU.mult)
                    else:
                        last = nc.vector.scalar_tensor_tensor(band[:, kw, :], place[:, a, :], w, band[:, kw, :],
                                                              ALU.mult, ALU.add)
                for half in range(2):
                    w = k_halo[:, a:a + 1]
                    src = place_halo[:, half, a, :]
                    if a == 0:
                        last = nc.vector.tensor_scalar(band_edge[:, half, :], src, w, None, ALU.mult)
                    else:
                        last = nc.vector.scalar_tensor_tensor(band_edge[:, half, :], src, w, band_edge[:, half, :],
                                                              ALU.mult, ALU.add)
                if a < KS - 1:
                    chained(last)
            last.then_inc(bands_ready, 1)
            nc.vector.sem_inc(unit_free, NU)
            mo = moments[:, :, :].rearrange("p (b g) k -> p b g k", b=B)
            with dve.Fori(0, B) as b:
                for t in range(NT):
                    n = t % NS
                    for u in range(NU):
                        part, half = divmod(u, 2)
                        at = b * (NT * NU) + t * NU + u
                        c0 = part * UC
                        here = x_tile[n][:, half, c0:c0 + UC, :]
                        dve.wait_ge(conv_done, at + 1)
                        nc.vector.tensor_scalar(capped[u % 2][:, :, :], ps[u][:, :, :], 20.0, None, ALU.min
                                                ).then_inc(cap_ready, 1)
                        dve.wait_ge(exp_ready, at + 1)
                        e = power[u % 2][:, :, :]
                        nc.vector.scalar_tensor_tensor(numer[:, :, :], e, 2.0, e, ALU.add, ALU.mult).then_inc(chain, 1)
                        dve.wait_ge(chain, at * CH + 1)
                        nc.vector.tensor_scalar(denom[:, :, :], numer[:, :, :], 2.0, None, ALU.add).then_inc(chain, 1)
                        nc.vector.tensor_tensor(numer[:, :, :], ps[u][:, :, :], numer[:, :, :], ALU.mult
                                                ).then_inc(unit_free, 1)
                        dve.wait_ge(chain, at * CH + 2)
                        nc.vector.reciprocal(denom[:, :, :], denom[:, :, :]).then_inc(chain, 1)
                        dve.wait_ge(chain, at * CH + 3)
                        dve.wait_ge(unit_free, at + 1 + NU)
                        nc.vector.tensor_tensor(numer[:, :, :], numer[:, :, :], denom[:, :, :], ALU.mult
                                                ).then_inc(chain, 1)
                        dve.wait_ge(chain, at * CH + 4)
                        nc.vector.tensor_tensor(here, here, numer[:, :, :], ALU.add).then_inc(summed, 1)
                        dve.wait_ge(summed, at + 1)
                        for j in range(UC // 2):
                            last = nc.vector.bn_stats(stats[:, part * UC // 2 + j, half, :],
                                                      x_tile[n][:, half, c0 + 2 * j:c0 + 2 * j + 2, :])
                    last.then_inc(y_ready, 1)
                    dve.wait_ge(y_ready, b * NT + t + 1)
                    nc.vector.sem_inc(may_aggregate, 1)
                    for j in range(CT // 2):
                        last = nc.vector.bn_aggr(image_moments[:, t * CT // 2 + j, :], stats[:, j, :, :])
                last.then_inc(aggregated, 1)
                dve.wait_ge(aggregated, b + 1)
                nc.vector.tensor_copy(mo[:, b, :, :], image_moments[:, :, :])


def mish_constants():
    src, dst = np.arange(P)[:, None], np.arange(P)[None, :]
    place = np.stack([(src - dst + KR == a) for a in range(KS)], 1)
    halo = np.zeros((P, 2, KS, P))
    for kw in range(KS):
        for r in range(KR):
            for a in range(KS):
                halo[KR * kw + r, 0, a] = (P + r - np.arange(P) + KR == a)
                halo[32 + KR * kw + r, 1, a] = (r - np.arange(P) == a)
    return {n: np.ascontiguousarray(v, dtype=np.float32) for n, v in (("place", place), ("place_halo", halo))}


def mish_kernels(kernel):
    turned = kernel[::-1, ::-1]
    k_all = np.broadcast_to(turned.reshape(1, KS * KS), (P, KS * KS))
    k_halo = np.zeros((P, KS), kernel.dtype)
    for first in (0, 32):
        k_halo[first:first + KR * KS] = np.repeat(turned.T, KR, axis=0)
    return np.ascontiguousarray(k_all), k_halo


PATCH = 8
CIN = 384


def patch_filter_block(nc, x, y, consts, w_in, w_dw, filt, w_out, stats_dram, B):
    S = H // PATCH
    NB = 4
    LEAD = 3
    HW_ = W // 2
    NJ = HW_ // (2 * PATCH)
    BJ = NJ // 2
    CTS = CIN // P
    RU = 4
    TAPS = [(0, 0), (0, 2), (2, 0), (2, 2), (0, 1), (2, 1), (1, 0), (1, 2), (1, 1)]
    UNITS = [(0, 0), (0, 1), (0, 2), (1, 2), (1, 0), (1, 1)]
    NUN = len(UNITS)
    NPE = 3
    NCHAIN = len(TAPS) - NPE - 1
    with Stage(nc, "l3") as s:
        x_in = [s.sbuf(f"x_in{i}", [P, PATCH, HW_]) for i in range(2)]
        x_res = [s.sbuf(f"x_res{i}", [P, PATCH, HW_]) for i in range(2)]
        normed = s.sbuf("normed", [P, NJ, PATCH, 2 * PATCH])
        grid = [s.sbuf(f"grid{i}", [P, CTS, PATCH + 2, W + 2]) for i in range(NB)]
        turned = s.sbuf("turned", [P, BJ, P])
        spectrum = s.sbuf("spectrum", [P, BJ, P])
        wide = s.sbuf("wide", [P, 2, BJ, CIN])
        acc = [[s.sbuf(f"acc{r}{c}", [P, RU, W]) for c in range(CTS)] for r in range(2)]
        gated = [s.sbuf(f"gated{r}", [P, RU, W]) for r in range(2)]
        norm = s.sbuf("norm", [P, B, 2])
        zero = s.sbuf("zero", [P, 1, 1])
        ident = s.sbuf("ident", [P, P])
        to_freq = s.sbuf("to_freq", [P, P])
        to_pixel = s.sbuf("to_pixel", [P, P])
        gain = s.sbuf("gain", [P, CIN])
        w_in_s = s.sbuf("w_in", [P, 2, CIN])
        w_dw_s = s.sbuf("w_dw", [P, CTS, 9])
        diag = s.sbuf("diag", [P, CTS, NPE, P])
        w_out_s = s.sbuf("w_out", [P, 2, C])
        spread = x_in[0][0:40, 0, 0:P]
        filt_s = x_in[1][0:40, 0:3, :]
        ps_turn = s.psum("ps_turn", [P, BJ, P])
        ps_out = s.psum("ps_out", [P, RU, HW_])
        ps_wide = [s.psum(f"ps_wide{i}", [P, BANK]) for i in range(2)]
        ps_grid = [s.psum(f"ps_grid{i}", [P, BJ, PATCH, 2 * PATCH]) for i in range(2)]
        ps_taps = s.psum("ps_taps", [P, RU, W])
        consts_loaded = s.sem("consts_loaded")
        cleared = s.sem("cleared")
        gain_done = s.sem("gain_done")
        gain_ready = s.sem("gain_ready")
        in_loaded = [s.sem(f"in_loaded{i}") for i in range(2)]
        res_loaded = [s.sem(f"res_loaded{i}") for i in range(2)]
        y_stored = [s.sem(f"y_stored{i}") for i in range(2)]
        may_normalise = s.sem("may_normalise")
        normed_ready = s.sem("normed_ready")
        turned_done = s.sem("turned_done")
        turned_ready = s.sem("turned_ready")
        spectrum_done = s.sem("spectrum_done")
        spectrum_ready = s.sem("spectrum_ready")
        wide_done = s.sem("wide_done")
        wide_copied = s.sem("wide_copied")
        wide_ready = s.sem("wide_ready")
        grid_done = s.sem("grid_done")
        grid_ready = s.sem("grid_ready")
        halo_ready = s.sem("halo_ready")
        taps_done = s.sem("taps_done")
        taps_copied = s.sem("taps_copied")
        chain = s.sem("chain")
        unit_ready = s.sem("unit_ready")
        gelu_ready = s.sem("gelu_ready")
        gate_ready = s.sem("gate_ready")
        out_done = s.sem("out_done")
        y_ready = s.sem("y_ready")
        block = s.block()
        UNIT0 = NB * NUN
        NSMALL = 10
        GATES = 4

        def strips_of(dram, b, q):
            v = dram[b].rearrange("c (q r) (f w) -> q f c r w", r=PATCH, f=2)
            return v[q]

        def steps(eng, step):
            for q in range(LEAD):
                step(None, (0, q, q), (0, q - 1, q - 1) if q else None, None)

            def inner(b, q, i, first=False):
                step((b, q, i), (b, q + LEAD, (i + LEAD) % NB), (b, q + LEAD - 1, (i + LEAD - 1) % NB),
                     None if first else (b, q - 1, (i - 1) % NB))

            def image(b, first, last):
                if first:
                    for i in range(NB):
                        inner(b, i, i, i == 0)
                with eng.Fori(1 if first else 0, S // NB - 1) as j:
                    for i in range(NB):
                        inner(b, j * NB + i, i)
                for i in range(NB):
                    q = S - NB + i
                    ahead = []
                    for lead in (LEAD, LEAD - 1):
                        if q + lead < S:
                            ahead.append((b, q + lead, (i + lead) % NB))
                        else:
                            ahead.append(None if last else (b + 1, q + lead - S, (i + lead) % NB))
                    step((b, q, i), *ahead, (b, q - 1, (i - 1) % NB))
                if last:
                    step(None, None, None, (b, S - 1, NB - 1))

            image(0, True, B == 1)
            if B > 2:
                with eng.Fori(1, B - 1) as b:
                    image(b, False, False)
            if B > 1:
                image(B - 1, False, True)

        def edge(q, value):
            return isinstance(q, int) and q == value

        @block.sync
        def _(sp):
            small = [(spread, consts["spread"]), (filt_s.rearrange("p a b -> p (a b)"), filt),
                     (ident[:, :], consts["ident"]), (to_freq[:, :], consts["to_freq"]),
                     (to_pixel[:, :], consts["to_pixel"]), (w_dw_s[:, :, :], w_dw)]
            sp.wait_ge(cleared, 2)
            for half in range(2):
                hp = slice(half * C, (half + 1) * C)
                small += [(norm[hp, :, :], stats_dram.rearrange("b c k -> c b k")), (w_in_s[hp, half, :], w_in)]
            small += [(w_out_s[:, 0, :], w_out[0:P, :]), (w_out_s[C:P, 1, :], w_out[P:P + C, :])]
            for dst, src in small:
                sp.dma_start(dst, src).then_inc(consts_loaded, 16)
            assert len(small) == NSMALL + 2

            sp.wait_ge(gain_ready, 1)

            def load(tiles, i, b, q, done):
                for half in range(2):
                    sp.dma_start(tiles[i][half * C:(half + 1) * C, :, :], strips_of(x, b, q)[half]).then_inc(done[i], 16)

            def next_in(b, q, i):
                if not (isinstance(b, int) and isinstance(q, int) and b == 0 and q < 2):
                    sp.wait_ge(normed_ready, b * S + q - 1)
                load(x_in, i, b, q, in_loaded)

            def next_res(b, q, i):
                if not (isinstance(b, int) and isinstance(q, int) and b == 0 and q < 2):
                    sp.wait_ge(y_stored[i], b * (32 * S // 2) + q // 2 * 32)
                load(x_res, i, b, q, res_loaded)

            def store(b, q, i):
                sp.wait_ge(y_ready, b * (2 * S) + q * 2 + 3)
                for half in range(2):
                    sp.dma_start(strips_of(y, b, q)[half], x_res[i][half * C:(half + 1) * C, :, :]
                                 ).then_inc(y_stored[i], 16)

            next_in(0, 0, 0)
            next_in(0, 1, 1)
            next_res(0, 0, 0)
            next_res(0, 1, 1)
            for q in range(2, LEAD + 2):
                next_in(0, q, q % 2)

            def step(b, q, i, last):
                store(b, q, i % 2)
                for fetch, ahead in ((next_res, 2), (next_in, LEAD + 2)):
                    if not isinstance(q, int) or q + ahead < S:
                        fetch(b, q + ahead, (i + ahead) % 2)
                    elif not last:
                        fetch(b + 1, q + ahead - S, (i + ahead) % 2)

            def image(b, last):
                tail = 2 * NB
                with sp.Fori(0, (S - tail) // NB) as j:
                    for i in range(NB):
                        step(b, j * NB + i, i, last)
                for q in range(S - tail, S):
                    step(b, q, q % NB, last)

            if B > 1:
                with sp.Fori(0, B - 1) as b:
                    image(b, False)
            image(B - 1, True)
            for i in range(2):
                sp.wait_ge(y_stored[i], 32 * (B * S // 2))

        @block.gpsimd
        def _(pool):
            for r in range(2):
                nc.gpsimd.memset(gated[r][:, :, :], 0.0)
            for i in range(NB):
                nc.gpsimd.memset(grid[i][:, :, :, 0:1], 0.0)
                nc.gpsimd.memset(grid[i][:, :, :, W + 1:W + 2], 0.0)
            last = nc.gpsimd.memset(zero[:, :, :], 0.0)
            last.then_inc(cleared, 1)

        @block.scalar
        def _(act):
            nc.scalar.sem_inc(grid_ready, 2)
            nc.scalar.sem_inc(wide_copied, 2)
            nc.scalar.sem_inc(taps_copied, 1)
            act.wait_ge(consts_loaded, 16 * (NSMALL + 2))

            def step(conv, idft, late, prev):
                if idft:
                    b, q, i = idft
                    n = b * S + q

                def normalise():
                    act.wait_ge(in_loaded[i % 2], b * (32 * S // 2) + q // 2 * 32 + 32)
                    if not (isinstance(n, int) and n == 0):
                        act.wait_ge(turned_done, n * 2)
                    nc.scalar.sem_inc(may_normalise, 1)
                    nc.scalar.activation(normed[:, :, :, :].rearrange("p j r c -> p r j c"),
                                         x_in[i % 2][:, :, :].rearrange("p r (j c) -> p r j c", j=NJ),
                                         ACT.Identity, scale=norm[:, b, 0:1], bias=norm[:, b, 1:2]
                                         ).then_inc(normed_ready, 1)

                def turn_copy(k):
                    act.wait_ge(turned_done, n * 2 + k + 1)
                    nc.scalar.activation(turned[:, :, :], ps_turn[:, :, :], ACT.Copy).then_inc(turned_ready, 1)

                def spectrum_copy(k):
                    act.wait_ge(spectrum_done, n * 2 + k + 1)
                    nc.scalar.activation(spectrum[:, :, :], ps_turn[:, :, :], ACT.Copy).then_inc(spectrum_ready, 1)

                def wide_copies(k, half):
                    for j in range(BJ):
                        m = half * BJ + j
                        act.wait_ge(wide_done, n * (4 * BJ) + k * 2 * BJ + m + 1)
                        nc.scalar.activation(wide[:, half, j, :], ps_wide[m % 2][:, 0:CIN], ACT.Copy
                                             ).then_inc(wide_copied, 1)

                def taps_copy(u):
                    cb, cq, _ = conv
                    at = cb * S + cq
                    r, ct = UNITS[u]
                    if ct == 1:
                        act.wait_ge(out_done, at * 2 + r + 1)
                    else:
                        gates = {0: 1, 2: 2, 3: 3, 4: 4}[u]
                        act.wait_ge(gate_ready, at * GATES + gates)
                    act.wait_ge(taps_done, at * NUN + u + 1)
                    nc.scalar.activation(acc[r][ct][:, :, :], ps_taps[:, :, :], ACT.Copy).then_inc(taps_copied, 1)

                def grid_copies(strip, k, half):
                    b, q, i = strip
                    n = b * S + q
                    if k == 0 and half == 0:
                        act.wait_ge(unit_ready, n * NUN + NUN)
                    for ct in range(CTS):
                        g = half * CTS + ct
                        act.wait_ge(grid_done, n * (4 * CTS) + k * 2 * CTS + g + 1)
                        c0 = 1 + half * HW_ + k * BJ * 2 * PATCH
                        dst = grid[i][:, ct, 1:PATCH + 1, c0:c0 + BJ * 2 * PATCH]
                        nc.scalar.activation(dst.rearrange("p r (j c) -> p r j c", j=BJ),
                                             ps_grid[g % 2][:, :, :, :].rearrange("p j r c -> p r j c"),
                                             ACT.Copy).then_inc(grid_ready, 1)

                def halo_copies(strip):
                    b, q, i = strip
                    act.wait_ge(grid_ready, (b * S + q) * (4 * CTS) + 4 * CTS + 2)
                    before = (i - 1) % NB

                    def rows(g, r):
                        return grid[g][:, :, r, 1:W + 1]

                    none = zero[:, :, :].broadcast_to([P, CTS, W])
                    if edge(q, 0):
                        last = nc.scalar.activation(rows(i, 0), none, ACT.Copy)
                    else:
                        nc.scalar.activation(rows(i, 0), rows(before, PATCH), ACT.Copy)
                        last = nc.scalar.activation(rows(before, PATCH + 1), rows(i, 1), ACT.Copy)
                    if edge(q, S - 1):
                        last = nc.scalar.activation(rows(i, PATCH + 1), none, ACT.Copy)
                    last.then_inc(halo_ready, 1)

                def gelu(u):
                    cb, cq, _ = conv
                    r, ct = UNITS[u]
                    act.wait_ge(unit_ready, cb * (S * NUN) + cq * NUN + u + 1 + UNIT0)
                    if ct == 0:
                        nc.scalar.activation(acc[r][0][:, :, :], acc[r][0][:, :, :], ACT.Gelu).then_inc(gelu_ready, 1)
                    else:
                        nc.scalar.activation(gated[r][C:P, :, :], acc[r][2][0:C, :, :], ACT.Gelu
                                             ).then_inc(gelu_ready, 1)

                if idft:
                    normalise()
                if conv:
                    taps_copy(0)
                if late:
                    grid_copies(late, 1, 0)
                if idft:
                    turn_copy(0)
                if conv:
                    taps_copy(1)
                if late:
                    grid_copies(late, 1, 1)
                    halo_copies(late)
                if idft:
                    spectrum_copy(0)
                if conv:
                    gelu(0)
                    taps_copy(2)
                if idft:
                    wide_copies(0, 0)
                    turn_copy(1)
                if conv:
                    taps_copy(3)
                if idft:
                    wide_copies(0, 1)
                    spectrum_copy(1)
                    grid_copies(idft, 0, 0)
                if conv:
                    gelu(2)
                    taps_copy(4)
                if idft:
                    wide_copies(1, 0)
                    grid_copies(idft, 0, 1)
                if conv:
                    gelu(3)
                    taps_copy(5)
                if idft:
                    wide_copies(1, 1)
                if conv:
                    gelu(4)

            steps(act, step)

        @block.tensor
        def _(pe):
            pe.wait_ge(consts_loaded, 16 * (NSMALL + 2))
            nc.tensor.matmul(ps_wide[0][:, 0:CIN], spread, filt_s.rearrange("p a b -> p (a b)"), start=True, stop=True
                             ).then_inc(gain_done, 1)
            nc.tensor.sem_inc(out_done, 2)
            pe.wait_ge(gain_ready, 1)

            def step(conv, idft, late, prev):
                if idft:
                    b, q, i = idft
                    n = b * S + q
                if conv:
                    cb, cq, ci = conv
                    at = cb * S + cq

                def turn(k):
                    pe.wait_ge(normed_ready, n + 1)
                    pe.wait_ge(spectrum_ready, n * 2 + k)
                    for j in range(BJ):
                        last = nc.tensor.matmul(ps_turn[:, j, :],
                                                normed[:, k * BJ + j, :, :].rearrange("p r c -> p (r c)"),
                                                ident[:, :], start=True, stop=True, is_transpose=True)
                    last.then_inc(turned_done, 1)

                def transform(k):
                    pe.wait_ge(turned_ready, n * 2 + k + 1)
                    for j in range(BJ):
                        last = nc.tensor.matmul(ps_turn[:, j, :], turned[:, j, :], to_freq[:, :],
                                                start=True, stop=True)
                    last.then_inc(spectrum_done, 1)

                def project(k, half):
                    pe.wait_ge(spectrum_ready, n * 2 + k + 1)
                    for j in range(BJ):
                        m = half * BJ + j
                        pe.wait_ge(wide_copied, n * (4 * BJ) + k * 2 * BJ + m + 1)
                        nc.tensor.matmul(ps_wide[m % 2][:, 0:CIN], spectrum[:, j, :], w_in_s[:, half, :],
                                         start=True, stop=True).then_inc(wide_done, 1)

                def invert(strip, k, half):
                    n = strip[0] * S + strip[1]
                    pe.wait_ge(wide_ready, n * 4 + k * 2 + half + 1)
                    for ct in range(CTS):
                        g = half * CTS + ct
                        pe.wait_ge(grid_ready, n * (4 * CTS) + k * 2 * CTS + g + 1)
                        for j in range(BJ):
                            last = nc.tensor.matmul(ps_grid[g % 2][:, j, :, :], wide[:, half, j, ct * P:(ct + 1) * P],
                                                    to_pixel[:, :], start=True, stop=True)
                        last.then_inc(grid_done, 1)

                def taps(u):
                    r, ct = UNITS[u]
                    if u == 0:
                        pe.wait_ge(halo_ready, at + (1 if edge(cq, S - 1) else 2))
                    pe.wait_ge(taps_copied, at * NUN + u + 1)
                    for h in range(RU // 2):
                        for m, (kh, kw) in enumerate(TAPS[:NPE]):
                            r0 = r * RU + 2 * h + kh
                            last = nc.tensor.matmul(ps_taps[:, 2 * h:2 * h + 2, :], diag[:, ct, m, :],
                                                    grid[ci][:, ct, r0:r0 + 2, kw:kw + W],
                                                    start=(m == 0), stop=(m == NPE - 1))
                    last.then_inc(taps_done, 1)

                def output(strip, r):
                    at = strip[0] * S + strip[1]
                    pe.wait_ge(gate_ready, at * GATES + 2 * r + 2 + GATES)
                    pe.wait_ge(y_ready, at * 2 + r + 1)
                    for half in range(2):
                        cols = slice(half * HW_, (half + 1) * HW_)
                        dst = ps_out[half * C:(half + 1) * C, :, :]
                        nc.tensor.matmul(dst, w_out_s[:, 1, :], gated[r][:, :, cols], start=True, stop=False)
                        last = nc.tensor.matmul(dst, w_out_s[:, 0, :], acc[r][1][:, :, cols], start=False, stop=True)
                    last.then_inc(out_done, 1)

                if conv:
                    taps(0)
                if late:
                    invert(late, 1, 0)
                if idft:
                    turn(0)
                if conv:
                    taps(1)
                if prev:
                    output(prev, 1)
                if late:
                    invert(late, 1, 1)
                if idft:
                    transform(0)
                if conv:
                    taps(2)
                if idft:
                    project(0, 0)
                    turn(1)
                if conv:
                    taps(3)
                if idft:
                    project(0, 1)
                    transform(1)
                    invert(idft, 0, 0)
                if conv:
                    taps(4)
                if idft:
                    project(1, 0)
                    invert(idft, 0, 1)
                if conv:
                    taps(5)
                    output(conv, 0)
                if idft:
                    project(1, 1)

            steps(pe, step)

        @block.vector
        def _(dve):
            nc.vector.memset(w_in_s[:, :, :], 0.0)
            nc.vector.memset(w_out_s[:, :, :], 0.0).then_inc(cleared, 1)
            dve.wait_ge(consts_loaded, 16 * (NSMALL + 2))
            for ct in range(CTS):
                for m, (kh, kw) in enumerate(TAPS[:NPE]):
                    k = kh * 3 + kw
                    nc.vector.tensor_scalar(diag[:, ct, m, :], ident[:, :], w_dw_s[:, ct, k:k + 1], None, ALU.mult)
            dve.wait_ge(gain_done, 1)
            nc.vector.tensor_copy(gain[:, :], ps_wide[0][:, 0:CIN]).then_inc(gain_ready, 1)
            nc.vector.sem_inc(gate_ready, GATES)
            nc.vector.sem_inc(unit_ready, UNIT0)
            nc.vector.sem_inc(y_ready, 1)
            dve.wait_ge(gain_ready, 1)

            def step(conv, idft, late, prev):
                if idft:
                    b, q, i = idft
                    n = b * S + q
                if conv:
                    cb, cq, ci = conv
                    at = cb * S + cq

                def scale(k, half):
                    dve.wait_ge(wide_copied, n * (4 * BJ) + k * 2 * BJ + (half + 1) * BJ + 2)
                    nc.vector.tensor_tensor(wide[:, half, :, :], wide[:, half, :, :],
                                            gain[:, :].unsqueeze(1).broadcast_to([P, BJ, CIN]), ALU.mult).then_inc(wide_ready, 1)

                def unit(u, extras=()):
                    r, ct = UNITS[u]
                    extras = list(extras)
                    for t, (kh, kw) in enumerate(TAPS[NPE:]):
                        src = grid[ci][:, ct, r * RU + kh:r * RU + kh + RU, kw:kw + W]
                        w = w_dw_s[:, ct, kh * 3 + kw:kh * 3 + kw + 1]
                        if t == 0:
                            dve.wait_ge(taps_copied, at * NUN + u + 2)
                        nc.vector.scalar_tensor_tensor(acc[r][ct][:, :, :], src, w, acc[r][ct][:, :, :],
                                                       ALU.mult, ALU.add
                                                       ).then_inc(chain if t < NCHAIN else unit_ready, 1)
                        if t >= 1 and extras:
                            extras.pop(0)()
                        if t < NCHAIN:
                            dve.wait_ge(chain, (at * NUN + u) * NCHAIN + t + 1)
                    for extra in extras:
                        extra()

                def gate(k, u_b):
                    r, ct = UNITS[u_b]
                    dve.wait_ge(unit_ready, at * NUN + u_b + 1 + UNIT0)
                    dve.wait_ge(gelu_ready, at * GATES + k + 1)
                    if ct == 1:
                        a, dst = acc[r][0][:, :, :], acc[r][1][:, :, :]
                        last = nc.vector.tensor_tensor(dst, dst, a, ALU.mult)
                    else:
                        a, dst = acc[r][2][C:P, :, :], gated[r][C:P, :, :]
                        last = nc.vector.tensor_tensor(dst, dst, a, ALU.mult)
                    last.then_inc(gate_ready, 1)

                def add_x(strip, r):
                    b, q, i = strip
                    if r == 0:
                        dve.wait_ge(res_loaded[i % 2], b * (32 * S // 2) + q // 2 * 32 + 32)
                    dve.wait_ge(out_done, (b * S + q) * 2 + r + 1 + 2)
                    here = x_res[i % 2][:, r * RU:(r + 1) * RU, :]
                    nc.vector.tensor_tensor(here, ps_out[:, :, :], here, ALU.add).then_inc(y_ready, 1)

                def scaled(k, half):
                    return [lambda: scale(k, half)] if idft else []

                last_rows = [lambda: add_x(prev, 1)] if prev else []
                if not conv:
                    for extra in last_rows + [e for k in range(2) for h in range(2) for e in scaled(k, h)]:
                        extra()
                    return
                wait_a_tap = [lambda: None]
                unit(0)
                unit(1, last_rows)
                gate(0, 1)
                unit(2, scaled(0, 0))
                unit(3, scaled(0, 1))
                gate(1, 2)
                unit(4, scaled(1, 0))
                gate(2, 3)
                unit(5, wait_a_tap * 3 + [lambda: add_x(conv, 0)] + scaled(1, 1))
                gate(3, 5)

            steps(dve, step)


def patch_constants():
    n = PATCH
    r, c = np.meshgrid(np.arange(n), np.arange(n), indexing="ij")
    basis, spread = [], []
    for kx, ky in [(kx, ky) for ky in range(n // 2 + 1) for kx in range(n)]:
        own = ky in (0, n // 2)
        mirror = (-kx) % n
        if own and mirror < kx:
            continue
        ang = 2 * np.pi * (kx * r + ky * c) / n
        gain = np.zeros((n, n // 2 + 1))
        gain[kx, ky] += 0.5 if own else 1.0
        gain[mirror, ky] += 0.5 if own else 0.0
        for f in [np.cos(ang)] + ([] if own and mirror == kx else [np.sin(ang)]):
            basis.append((f / np.linalg.norm(f)).ravel())
            spread.append(gain.ravel())
    basis = np.array(basis)
    assert basis.shape == (n * n, n * n) and np.allclose(basis @ basis.T, np.eye(n * n))
    to_freq = np.zeros((n, 2, n, 2, n * n))
    for patch in range(2):
        to_freq[:, patch, :, patch, :] = basis.T.reshape(n, n, n * n)
    to_freq = to_freq.reshape(P, P)
    out = {"ident": np.eye(P), "to_freq": to_freq, "to_pixel": to_freq.T,
           "spread": np.tile(np.array(spread).T, (1, 2))}
    return {k: np.ascontiguousarray(v, dtype=np.float32) for k, v in out.items()}


def channel_order():
    h = CIN // 2
    return np.r_[0:P, h:h + P, P:h, h + P:CIN]


def projection_layouts(w_in, w_dw, filt, w_out):
    order = channel_order()
    w_in = np.ascontiguousarray(w_in[order].T)
    w_dw = np.ascontiguousarray(w_dw.reshape(CIN, 9)[order].reshape(CIN // P, P, 9).transpose(1, 0, 2))
    filt = np.ascontiguousarray(filt.reshape(CIN, 40)[order].T)
    return w_in, w_dw, filt, np.ascontiguousarray(w_out.T)


def build(nc, B, x, w_real, w_imag, dil_taps, dil_bias, kernel_all, kernel_halo, w_in, w_dw, filt, w_out, consts, y):
    def scratch(name, shape):
        return nc.dram_tensor(name, shape, FP32, kind="Internal").ap()

    shape = [B, C, H, W]
    x1, x2, x3 = (scratch(f"x{i}", shape) for i in (1, 2, 3))
    stats = [scratch(f"norm{i}", [B, C, 2]) for i in range(4)]
    modes_mixed = scratch("modes_mixed", [2 * B, MODES * MODES, C])
    with Stage(nc, "layer0a") as s:
        moments = s.sbuf("moments", [P, B * GROUPS, 2])
        modes_in = s.sbuf("modes_in", [P, MODES, MODES, 2 * B])
        spectral_forward(nc, x, consts, moments, modes_in, B)
        finish_statistics(nc, "norm0", moments, B * GROUPS, consts["average_all"], row_layout_stores(stats[0], B))
        spectral_mix(nc, w_real, w_imag, stats[0], modes_in, modes_mixed, B)
    with Stage(nc, "layer0b") as s:
        moments = s.sbuf("moments", [P, B * GROUPS, 2])
        spectral_inverse(nc, x, x1, consts, modes_mixed, moments, B)
        finish_statistics(nc, "norm1", moments, B * GROUPS, consts["average_all"], row_layout_stores(stats[1], B))
    with Stage(nc, "layer1") as s:
        moments = s.sbuf("moments", [P, B * 4, 2])
        dilated_conv(nc, x1, x2, dil_taps, dil_bias, stats[1], consts["slab_masks"], moments, B)
        finish_statistics(nc, "norm2", moments, B * 4, consts["average_pairs"], channel_layout_stores(stats[2], B))
    with Stage(nc, "layer2") as s:
        moments = s.sbuf("moments", [P, B * GROUPS, 2])
        depthwise_mish(nc, x2, x3, consts, kernel_all, kernel_halo, stats[2], moments, B)
        finish_statistics(nc, "norm3", moments, B * GROUPS, consts["average_all"], row_layout_stores(stats[3], B))
    patch_filter_block(nc, x3, y, consts, w_in, w_dw, filt, w_out, stats[3], B)


def kernel(x, L0_conv_weight_real, L0_conv_weight_imag, L1_conv_weight, L1_conv_bias, L2_conv_kernel,
           L3_conv_w_in, L3_conv_w_dw, L3_conv_fft_filter, L3_conv_w_out):
    import concourse.bacc as bacc
    from concourse.bass_utils import run_bass_kernel_spmd

    B = x.shape[0]
    consts = {**constants(), **pair_constants(), **mish_constants(), **patch_constants()}
    kernel_all, kernel_halo = mish_kernels(np.asarray(L2_conv_kernel))
    w_in, w_dw, filt, w_out = projection_layouts(*map(np.asarray, (L3_conv_w_in, L3_conv_w_dw, L3_conv_fft_filter,
                                                                  L3_conv_w_out)))
    arrays = {
        "x": np.asarray(x), "w_real": np.asarray(L0_conv_weight_real), "w_imag": np.asarray(L0_conv_weight_imag),
        "dil_taps": np.asarray(L1_conv_weight).reshape(4, 16, 16, 9).transpose(2, 0, 3, 1),
        "dil_bias": np.asarray(L1_conv_bias).reshape(4, 16).T,
        "kernel_all": kernel_all, "kernel_halo": kernel_halo,
        "w_in": w_in, "w_dw": w_dw, "filt": filt, "w_out": w_out,
    }
    arrays = {f"in_{k}": np.ascontiguousarray(v) for k, v in arrays.items()}
    tables = {f"const_{k}": v for k, v in consts.items()}
    nc = bacc.Bacc("TRN2", target_bir_lowering=False, num_devices=1)

    def declare(name, a):
        return nc.dram_tensor(name, a.shape, mybir.dt.from_np(a.dtype), kind="ExternalInput").ap()

    ins = {k[3:]: declare(k, v) for k, v in arrays.items()}
    const_aps = {k[6:]: declare(k, v) for k, v in tables.items()}
    y = nc.dram_tensor("out_y", [B, C, H, W], FP32, kind="ExternalOutput").ap()
    build(nc, B, consts=const_aps, y=y, **ins)
    r = run_bass_kernel_spmd(nc, [{**arrays, **tables}], core_ids=[0])
    return r.results[0]["out_y"]
```

```python
import numpy as np
import concourse.bass as bass
from concourse import mybir
from contextlib import ExitStack

FP32 = mybir.dt.float32
ALU = mybir.AluOpType
ACT = mybir.ActivationFunctionType

C, H, W = 64, 256, 256
P = 128
GROUPS = 32
MODES = 32
EPS = 1e-5
BANK = 512
CT = 8
NT = C // CT


class Stage:

    def __init__(self, nc, name):
        self.nc, self.name, self.stack = nc, name, ExitStack()

    def __enter__(self):
        self.stack.__enter__()
        return self

    def __exit__(self, *exc):
        return self.stack.__exit__(*exc)

    def sbuf(self, name, shape):
        return self.stack.enter_context(self.nc.sbuf_tensor(f"{self.name}_{name}", shape, FP32))

    def psum(self, name, shape):
        return self.stack.enter_context(self.nc.psum_tensor(f"{self.name}_{name}", shape, FP32))

    def sem(self, name):
        return self.stack.enter_context(self.nc.semaphore(f"{self.name}_{name}"))

    def block(self):
        return self.stack.enter_context(self.nc.Block())


def finish_statistics(nc, name, moments, n, averager, stores, weights_dram=None):
    weighted = weights_dram is not None
    parts = weights_dram.shape[1] if weighted else 1
    parted = moments[:, :, :, :] if weighted else moments[:, :, :].unsqueeze(1)
    with Stage(nc, name) as s:
        avg = s.sbuf("avg", [P, P])
        mean = s.sbuf("mean", [P, n])
        share = s.sbuf("share", [P, parts, n])
        spread = s.sbuf("spread", [P, parts, n])
        var = s.sbuf("var", [P, n])
        root = s.sbuf("root", [P, n])
        rstd = s.sbuf("rstd", [P, n])
        result = s.sbuf("result", [P, n, 2])
        if weighted:
            q = weights_dram.shape[2]
            weights = s.sbuf("weights", [P, parts, q])
            weight = weights[:, :, :].unsqueeze(2).broadcast_to([P, parts, n // q, q])

            def by_image(tile):
                return tile[:, :, :].rearrange("p m (b q) -> p m b q", q=q)
        mean_ps = s.psum("mean_ps", [P, BANK])
        var_ps = s.psum("var_ps", [P, BANK])
        avg_loaded = s.sem("avg_loaded")
        averaged = s.sem("averaged")
        step = s.sem("step")
        sums_ready = s.sem("sums_ready")
        var_ready = s.sem("var_ready")
        root_ready = s.sem("root_ready")
        result_ready = s.sem("result_ready")
        stored = s.sem("stored")
        pairs = stores(result)
        block = s.block()

        @block.sync
        def _(sp):
            sp.dma_start(avg[:, :], averager).then_inc(avg_loaded, 16)
            if weighted:
                sp.dma_start(weights[:, :, :], weights_dram).then_inc(avg_loaded, 16)
            sp.wait_ge(result_ready, 1)
            for dst, src in pairs:
                sp.dma_start(dst, src).then_inc(stored, 16)
            sp.wait_ge(stored, 16 * len(pairs))

        @block.tensor
        def _(pe):
            pe.wait_ge(avg_loaded, 32 if weighted else 16)
            pe.wait_ge(sums_ready, 1)
            for m in range(parts):
                last = nc.tensor.matmul(mean_ps[:, 0:n], avg[:, :], share[:, m, :], start=(m == 0),
                                        stop=(m == parts - 1))
            last.then_inc(averaged, 1)
            pe.wait_ge(sums_ready, 2)
            for m in range(parts):
                last = nc.tensor.matmul(var_ps[:, 0:n], avg[:, :], spread[:, m, :], start=(m == 0),
                                        stop=(m == parts - 1))
            last.then_inc(averaged, 1)

        @block.scalar
        def _(act):
            act.wait_ge(var_ready, 1)
            nc.scalar.activation(root[:, :], var[:, :], ACT.Sqrt).then_inc(root_ready, 1)

        @block.vector
        def _(dve):
            done = [0]

            def chained(instruction):
                done[0] += 1
                instruction.then_inc(step, 1)
                dve.wait_ge(step, done[0])

            if weighted:
                dve.wait_ge(avg_loaded, 32)
                nc.vector.tensor_tensor(by_image(share), by_image(parted[:, :, :, 0]), weight, ALU.mult
                                        ).then_inc(sums_ready, 1)
            else:
                nc.vector.tensor_copy(share[:, :, :], parted[:, :, :, 0]).then_inc(sums_ready, 1)
            dve.wait_ge(averaged, 1)
            chained(nc.vector.tensor_copy(mean[:, :], mean_ps[:, 0:n]))
            for m in range(parts):
                last = nc.vector.tensor_tensor(spread[:, m, :], parted[:, m, :, 0], mean[:, :], ALU.subtract)
            chained(last)
            chained(nc.vector.tensor_tensor(spread[:, :, :], spread[:, :, :], spread[:, :, :], ALU.mult))
            last = nc.vector.tensor_tensor(spread[:, :, :], spread[:, :, :], parted[:, :, :, 1], ALU.add)
            if weighted:
                chained(last)
                last = nc.vector.tensor_tensor(by_image(spread), by_image(spread), weight, ALU.mult)
            last.then_inc(sums_ready, 1)
            dve.wait_ge(averaged, 2)
            nc.vector.tensor_scalar(var[:, :], var_ps[:, 0:n], EPS, None, ALU.add).then_inc(var_ready, 1)
            dve.wait_ge(root_ready, 1)
            chained(nc.vector.reciprocal(rstd[:, :], root[:, :]))
            chained(nc.vector.tensor_tensor(root[:, :], rstd[:, :], rstd[:, :], ALU.mult))
            chained(nc.vector.tensor_tensor(root[:, :], root[:, :], var[:, :], ALU.mult))
            chained(nc.vector.tensor_scalar(root[:, :], root[:, :], -0.5, 1.5, ALU.mult, ALU.add))
            chained(nc.vector.tensor_tensor(result[:, :, 0], rstd[:, :], root[:, :], ALU.mult))
            nc.vector.scalar_tensor_tensor(result[:, :, 1], mean[:, :], -1.0, result[:, :, 0],
                                           ALU.mult, ALU.mult).then_inc(result_ready, 1)


def row_layout_stores(stats_dram, B):
    def stores(result):
        src = result[0:1, :, :].rearrange("p (b g) k -> p b g k", b=B)
        dst = stats_dram.rearrange("b (g t) k -> t b g k", t=2)
        return [(dst[t:t + 1, b, :, :], src[:, b, :, :]) for t in range(2) for b in range(B)]
    return stores


def spectral_forward(nc, x, consts, moments, modes_in, B):
    K2 = 2 * MODES
    NX = 4
    with Stage(nc, "fwd") as s:
        x_tile = [s.sbuf(f"x{i}", [P, 2, CT, W]) for i in range(NX)]
        f_rows = s.sbuf("f_rows", [P, 2, K2])
        f_cols = s.sbuf("f_cols", [P, 2, 2, K2])
        col_modes = s.sbuf("col_modes", [P, 2, K2, C])
        stats = [s.sbuf(f"stats{i}", [P, CT // 2, 2, 6]) for i in range(2)]
        image_moments = s.sbuf("image_moments", [P, GROUPS, 2])
        rows_ps = [s.psum(f"rows_ps{i}", [P, 2, CT, K2]) for i in range(2)]
        QN = 4
        KQ = MODES // QN
        modes_ps = [s.psum(f"modes_ps{i}", [C, KQ, K2]) for i in range(QN)]
        consts_loaded = s.sem("consts_loaded")
        x_loaded = [s.sem(f"x_loaded{i}") for i in range(NX)]
        x_transformed = s.sem("x_transformed")
        x_measured = s.sem("x_measured")
        cols_ready = s.sem("cols_ready")
        modes_done = s.sem("modes_done")
        modes_free = s.sem("modes_free")
        may_aggregate = s.sem("may_aggregate")
        aggregated = s.sem("aggregated")
        block = s.block()

        @block.sync
        def _(sp):
            sp.dma_start(f_rows[:, :, :], consts["f_rows"]).then_inc(consts_loaded, 16)
            sp.dma_start(f_cols[:, :, :, :], consts["f_cols"]).then_inc(consts_loaded, 16)

            def load(b, t):
                for half in range(2):
                    src = x[b, t * CT:(t + 1) * CT, half * P:(half + 1) * P, :].rearrange("c h w -> h c w")
                    sp.dma_start(x_tile[t % NX][:, half, :, :], src).then_inc(x_loaded[t % NX], 16)

            with sp.Fori(0, B) as b:
                for t in range(NT):
                    sp.wait_ge(x_transformed, b * NT + t + 1)
                    sp.wait_ge(x_measured, b * NT + t + 1)
                    load(b, t)

        @block.tensor
        def _(pe):
            nc.tensor.sem_inc(x_transformed, NX)
            pe.wait_ge(consts_loaded, 32)
            with pe.Fori(0, B) as b:
                for t in range(NT):
                    pe.wait_ge(x_loaded[t % NX], b * (32 * NT // NX) + 32 * (t // NX + 1))
                    pe.wait_ge(cols_ready, b * NT + t + 1)
                    for half_w in range(2):
                        for c in range(CT):
                            for half in range(2):
                                last = nc.tensor.matmul(
                                    rows_ps[t % 2][:, half_w, c, :],
                                    x_tile[t % NX][:, half, c, half_w * P:(half_w + 1) * P],
                                    f_rows[:, half, :], start=(half == 0), stop=(half == 1))
                    last.then_inc(x_transformed, 1)
                pe.wait_ge(cols_ready, b * NT + NT + 2)
                for q in range(QN):
                    pe.wait_ge(modes_free, b * QN + q + 1)
                    for k in range(KQ):
                        kx = q * KQ + k
                        n = 0
                        for half_w in range(2):
                            for part in range(2):
                                last = nc.tensor.matmul(
                                    modes_ps[q][:, k, :], col_modes[:, half_w, part * MODES + kx, :],
                                    f_cols[:, half_w, part, :], start=(n == 0), stop=(n == 3))
                                n += 1
                    last.then_inc(modes_done, 1)

        @block.scalar
        def _(act):
            nc.scalar.sem_inc(cols_ready, 2)
            with act.Fori(0, B) as b:
                act.wait_ge(modes_free, b * QN + QN)
                for t in range(NT):
                    act.wait_ge(x_transformed, b * NT + t + 1 + NX)
                    for half_w in range(2):
                        last = nc.scalar.activation(
                            col_modes[:, half_w, :, t * CT:(t + 1) * CT].rearrange("p k c -> p c k"),
                            rows_ps[t % 2][:, half_w, :, :], ACT.Copy)
                    last.then_inc(cols_ready, 1)

        @block.vector
        def _(dve):
            nc.vector.sem_inc(x_measured, NX)
            nc.vector.sem_inc(modes_free, QN)
            mo = moments[:, :, :].rearrange("p (b g) k -> p b g k", b=B)
            with dve.Fori(0, B) as b:
                for t in range(NT):
                    dve.wait_ge(x_loaded[t % NX], b * (32 * NT // NX) + 32 * (t // NX + 1))
                    for j in range(CT // 2):
                        for half in range(2):
                            last = nc.vector.bn_stats(stats[t % 2][:, j, half, :],
                                                      x_tile[t % NX][:, half, 2 * j:2 * j + 2, :])
                    last.then_inc(x_measured, 1)
                    dve.wait_ge(x_measured, b * NT + t + 1 + NX)
                    nc.vector.sem_inc(may_aggregate, 1)
                    for j in range(CT // 2):
                        last = nc.vector.bn_aggr(image_moments[:, t * CT // 2 + j, :], stats[t % 2][:, j, :, :])
                last.then_inc(aggregated, 1)
                dve.wait_ge(aggregated, b + 1)
                nc.vector.tensor_copy(mo[:, b, :, :], image_moments[:, :, :])
                for q in range(QN):
                    dve.wait_ge(modes_done, b * QN + q + 1)
                    re = modes_ps[q][:, :, 0:MODES]
                    im = modes_ps[q][:, :, MODES:K2]
                    dst = modes_in[:, q * KQ:(q + 1) * KQ, :, :]
                    nc.vector.tensor_copy(dst[0:C, :, :, b], re)
                    nc.vector.tensor_scalar(dst[C:P, :, :, b], im, -1.0, None, ALU.mult)
                    nc.vector.tensor_copy(dst[0:C, :, :, B + b], im)
                    nc.vector.tensor_copy(dst[C:P, :, :, B + b], re).then_inc(modes_free, 1)


def spectral_mix(nc, w_real, w_imag, stats_dram, modes_in, modes_out, B):
    MC = 4 * MODES
    NCH = MODES * MODES // MC
    MB = BANK // C
    NB = MC // MB
    with Stage(nc, "mix") as s:
        norm = s.sbuf("norm", [P, B, 2])
        scale = s.sbuf("scale", [P, 2, B])
        shift = s.sbuf("shift", [P, B])
        w = [s.sbuf(f"w{i}", [P, C, MC]) for i in range(2)]
        chunk = [s.sbuf(f"chunk{i}", [P, MC, 2 * B]) for i in range(2)]
        mixed = s.sbuf("mixed", [2 * B, MC, C])
        mixed_ps = [s.psum(f"mixed_ps{i}", [2 * B, MB, C]) for i in range(8)]
        norm_loaded = s.sem("norm_loaded")
        w_loaded = [s.sem(f"w_loaded{i}") for i in range(2)]
        step = s.sem("step")
        normalised = s.sem("normalised")
        chunk_ready = s.sem("chunk_ready")
        chunk_mixed = s.sem("chunk_mixed")
        bank_mixed = s.sem("bank_mixed")
        bank_free = s.sem("bank_free")
        may_store = s.sem("may_store")
        out_stored = s.sem("out_stored")
        block = s.block()
        flat_in = modes_in[:, :, :, :].rearrange("p x y n -> p (x y) n")

        @block.sync
        def _(sp):
            for half in range(2):
                sp.dma_start(norm[half * C:(half + 1) * C, :, :],
                             stats_dram.rearrange("b c k -> c b k")).then_inc(norm_loaded, 16)
            with sp.Fori(0, NCH // 2) as pair:
                for i in range(2):
                    sp.wait_ge(chunk_mixed, pair * 2 + i + 1)
                    for half, src in enumerate((w_real, w_imag)):
                        sp.dma_start(w[i][half * C:(half + 1) * C, :, :],
                                     src.rearrange("c o x y -> c o (x y)")[:, :, bass.ds((pair * 2 + i) * MC, MC)]
                                     ).then_inc(w_loaded[i], 16)

        @block.gpsimd
        def _(pool):
            with pool.Fori(0, NCH) as ch:
                pool.wait_ge(bank_free, ch * NB + NB + 8)
                nc.gpsimd.sem_inc(may_store, 1)
                pool.dma_start(modes_out[:, bass.ds(ch * MC, MC), :], mixed[:, :, :]).then_inc(out_stored, 16)
            pool.wait_ge(out_stored, 16 * NCH)

        @block.scalar
        def _(act):
            act.wait_ge(normalised, 1)
            with act.Fori(0, NCH // 2) as pair:
                for i in range(2):
                    act.wait_ge(chunk_mixed, pair * 2 + i + 1)
                    nc.scalar.activation(chunk[i][:, :, :], flat_in[:, bass.ds((pair * 2 + i) * MC, MC), :],
                                         ACT.Copy).then_inc(chunk_ready, 1)

        @block.tensor
        def _(pe):
            nc.tensor.sem_inc(chunk_mixed, 2)
            with pe.Fori(0, NCH // 2) as pair:
                for i in range(2):
                    pe.wait_ge(chunk_ready, pair * 2 + i + 1)
                    pe.wait_ge(w_loaded[i], pair * 32 + 32)
                    for k in range(NB):
                        pe.wait_ge(bank_free, pair * (2 * NB) + i * NB + k + 1)
                        for j in range(MB):
                            m = k * MB + j
                            last = nc.tensor.matmul(mixed_ps[k % 8][:, j, :], chunk[i][:, m, :], w[i][:, :, m],
                                                    start=True, stop=True)
                        if k < NB - 1:
                            last.then_inc(bank_mixed, 1)
                    last.then_inc(bank_mixed, 1)
                    pe.wait_ge(bank_mixed, pair * (2 * NB) + (i + 1) * NB)
                    nc.tensor.sem_inc(chunk_mixed, 1)

        @block.vector
        def _(dve):
            done = [0]

            def chained(instruction):
                done[0] += 1
                instruction.then_inc(step, 1)
                dve.wait_ge(step, done[0])

            nc.vector.sem_inc(bank_free, 8)
            dve.wait_ge(norm_loaded, 32)
            nc.vector.tensor_copy(scale[:, 0, :], norm[:, :, 0])
            chained(nc.vector.tensor_copy(scale[:, 1, :], norm[:, :, 0]))
            chained(nc.vector.tensor_scalar(shift[:, :], norm[:, :, 1], float(H * W) ** 0.5, None, ALU.mult))
            flat_scale = scale[:, :, :].rearrange("p k b -> p (k b)")
            chained(nc.vector.tensor_tensor(
                flat_in, flat_in, flat_scale.unsqueeze(1).to_broadcast([P, MODES * MODES, 2 * B]), ALU.mult))
            nc.vector.tensor_tensor(flat_in[0:C, 0, 0:B], flat_in[0:C, 0, 0:B], shift[0:C, :], ALU.add)
            nc.vector.tensor_tensor(flat_in[C:P, 0, B:2 * B], flat_in[C:P, 0, B:2 * B], shift[C:P, :],
                                    ALU.add).then_inc(normalised, 1)

            def copy_out(ch, first=False):
                if not first:
                    dve.wait_ge(out_stored, ch * 16)
                for k in range(NB):
                    dve.wait_ge(bank_mixed, ch * NB + k + 1)
                    nc.vector.tensor_copy(mixed[:, k * MB:(k + 1) * MB, :], mixed_ps[k % 8][:, :, :]
                                          ).then_inc(bank_free, 1)

            copy_out(0, True)
            with dve.Fori(1, NCH) as ch:
                copy_out(ch)


def spectral_inverse(nc, x, y, consts, modes_out, moments, B):
    K2 = 2 * MODES
    with Stage(nc, "inv") as s:
        x_tile = [s.sbuf(f"x{i}", [P, 2, CT, W]) for i in range(4)]
        g_cols = s.sbuf("g_cols", [P, W])
        g_rows = s.sbuf("g_rows", [P, 2, P])
        modes = [s.sbuf(f"modes{i}", [P, 2, MODES, C]) for i in range(2)]
        rows = [s.sbuf(f"rows{i}", [P, CT, W]) for i in range(2)]
        stats = [s.sbuf(f"stats{i}", [P, CT // 2, 2, 6]) for i in range(2)]
        image_moments = s.sbuf("image_moments", [P, GROUPS, 2])
        HT = CT // 2
        rows_ps = [s.psum(f"rows_ps{i}", [K2, HT, W]) for i in range(2)]
        y_ps = [s.psum(f"y_ps{i}", [P, 2, W]) for i in range(4)]
        consts_loaded = s.sem("consts_loaded")
        x_loaded = [s.sem(f"x_loaded{i}") for i in range(4)]
        y_stored = [s.sem(f"y_stored{i}") for i in range(4)]
        modes_loaded = [s.sem(f"modes_loaded{i}") for i in range(2)]
        modes_ready = s.sem("modes_ready")
        modes_used = s.sem("modes_used")
        rows_done = s.sem("rows_done")
        rows_ready = s.sem("rows_ready")
        y_done = s.sem("y_done")
        y_added = s.sem("y_added")
        measured = s.sem("measured")
        may_aggregate = s.sem("may_aggregate")
        aggregated = s.sem("aggregated")
        cleared = s.sem("cleared")
        may_store = s.sem("may_store")
        block = s.block()

        def rows_of(t, b, i, dram):
            return dram[b * 2 + i, t * CT:(t + 1) * CT, :, :].rearrange("c (f h) w -> f h c w", f=2)

        @block.sync
        def _(sp):
            sp.dma_start(g_cols[:, :], consts["g_cols"]).then_inc(consts_loaded, 16)
            sp.dma_start(g_rows[:, :, :], consts["g_rows"]).then_inc(consts_loaded, 16)

            def two_images(pair, first=False):
                for i in range(2):
                    sp.wait_ge(modes_used, pair * 2 + i + 1)
                    for top in range(2):
                        for part in range(2):
                            src = modes_out.rearrange("(r b) (x y) o -> r b y x o", r=2, y=MODES)
                            sp.dma_start(modes[i][top * MODES:(top + 1) * MODES, part, :, :],
                                         src[part ^ top, pair * 2 + i]).then_inc(modes_loaded[i], 16)
                    for t in range(NT):
                        n = (i * NT + t) % 4
                        if not first or i * NT + t >= 4:
                            sp.wait_ge(y_stored[n], pair * (32 * NT // 2) + 32 * ((i * NT + t) // 4))
                        for half in range(2):
                            sp.dma_start(x_tile[n][:, half, :, :], rows_of(t, pair, i, x)[half]
                                         ).then_inc(x_loaded[n], 16)

            two_images(0, True)
            if B > 2:
                with sp.Fori(1, B // 2) as pair:
                    two_images(pair)

        @block.gpsimd
        def _(pool):
            with pool.Fori(0, B // 2) as pair:
                for m in range(2 * NT):
                    i, t = divmod(m, NT)
                    pool.wait_ge(measured, pair * (2 * NT) + m + 1)
                    nc.gpsimd.sem_inc(may_store, 1)
                    for half in range(2):
                        pool.dma_start(rows_of(t, pair, i, y)[half], x_tile[m % 4][:, half, :, :]
                                       ).then_inc(y_stored[m % 4], 16)
            for n in range(4):
                pool.wait_ge(y_stored[n], 32 * (B * NT // 4))

        @block.tensor
        def _(pe):
            nc.tensor.sem_inc(modes_used, 2)
            pe.wait_ge(consts_loaded, 32)
            pe.wait_ge(cleared, 1)
            with pe.Fori(0, B // 2) as pair:
                for m in range(2 * NT):
                    i, t = divmod(m, NT)
                    if t == 0:
                        pe.wait_ge(modes_ready, pair * 2 + i + 1)
                    for part in range(2):
                        pe.wait_ge(rows_ready, pair * (4 * NT) + 2 * m + part + 1)
                        for c in range(HT):
                            last = nc.tensor.matmul(
                                rows_ps[part][:, c, :],
                                modes[i][:, :, :, t * CT + part * HT + c].rearrange("p r k -> p (r k)"),
                                g_cols[:, :], start=True, stop=True)
                        last.then_inc(rows_done, 1)
                    if t == NT - 1:
                        pe.wait_ge(rows_done, pair * (4 * NT) + 2 * m + 2)
                        nc.tensor.sem_inc(modes_used, 1)
                    for part in range(2):
                        pe.wait_ge(rows_ready, pair * (4 * NT) + 2 * m + part + 3)
                        for j in range(HT // 2):
                            for half in range(2):
                                u = part * HT + j * 2 + half
                                pe.wait_ge(y_added, pair * (16 * NT) + 8 * m + u + 1)
                                c0 = part * HT + 2 * j
                                nc.tensor.matmul(y_ps[u % 4][:, :, :], g_rows[:, half, :],
                                                 rows[m % 2][:, c0:c0 + 2, :],
                                                 start=True, stop=True).then_inc(y_done, 1)

        @block.scalar
        def _(act):
            nc.scalar.sem_inc(rows_ready, 2)
            with act.Fori(0, B // 2) as pair:
                for m in range(2 * NT):
                    i, t = divmod(m, NT)
                    if t == 0:
                        act.wait_ge(modes_loaded[i], pair * 64 + 64)
                        nc.scalar.activation(modes[i][MODES:K2, 1, :, :], modes[i][MODES:K2, 1, :, :],
                                             ACT.Copy, scale=-1.0).then_inc(modes_ready, 1)
                    for part in range(2):
                        act.wait_ge(rows_done, pair * (4 * NT) + 2 * m + part + 1)
                        nc.scalar.activation(rows[m % 2][0:K2, part * HT:(part + 1) * HT, :], rows_ps[part][:, :, :],
                                             ACT.Copy).then_inc(rows_ready, 1)

        @block.vector
        def _(dve):
            for i in range(2):
                nc.vector.memset(modes[i][K2:P, :, :, :], 0.0)
                last = nc.vector.memset(rows[i][K2:P, :, :], 0.0)
            last.then_inc(cleared, 1)
            nc.vector.sem_inc(y_added, 4)
            mo = moments[:, :, :].rearrange("p (b i g) k -> p b i g k", b=B // 2, i=2)
            with dve.Fori(0, B // 2) as pair:
                for m in range(2 * NT):
                    i, t = divmod(m, NT)
                    n = m % 4
                    dve.wait_ge(x_loaded[n], pair * (32 * NT // 2) + 32 * (m // 4) + 32)
                    for j in range(CT // 2):
                        for half in range(2):
                            u = 2 * j + half
                            here = x_tile[n][:, half, 2 * j:2 * j + 2, :]
                            dve.wait_ge(y_done, pair * (16 * NT) + 8 * m + u + 1)
                            nc.vector.tensor_tensor(here, y_ps[u % 4][:, :, :], here, ALU.add).then_inc(y_added, 1)
                            if u >= 1:
                                pj, ph = divmod(u - 1, 2)
                                dve.wait_ge(y_added, pair * (16 * NT) + 8 * m + u + 4)
                                nc.vector.bn_stats(stats[m % 2][:, pj, ph, :],
                                                   x_tile[n][:, ph, 2 * pj:2 * pj + 2, :])
                    dve.wait_ge(y_added, pair * (16 * NT) + 8 * m + 8 + 4)
                    nc.vector.bn_stats(stats[m % 2][:, CT // 2 - 1, 1, :],
                                       x_tile[n][:, 1, CT - 2:CT, :]).then_inc(measured, 1)
                    dve.wait_ge(measured, pair * (2 * NT) + m + 1)
                    nc.vector.sem_inc(may_aggregate, 1)
                    for j in range(CT // 2):
                        last = nc.vector.bn_aggr(image_moments[:, t * CT // 2 + j, :], stats[m % 2][:, j, :, :])
                    if t == NT - 1:
                        last.then_inc(aggregated, 1)
                        dve.wait_ge(aggregated, pair * 2 + i + 1)
                        nc.vector.tensor_copy(mo[:, pair, i, :, :], image_moments[:, :, :])


def constants():
    k = np.arange(MODES)
    h = np.arange(H)
    ang = 2 * np.pi * np.outer(h, k) / H
    root = np.sqrt(float(H))
    cos, sin = np.cos(ang) / root, np.sin(ang) / root
    double = np.where(k == 0, 1.0, 2.0)
    f_rows = np.concatenate([cos, -sin], 1).reshape(2, P, 2 * MODES).transpose(1, 0, 2)
    f_cols = np.stack([np.concatenate([cos, -sin], 1), np.concatenate([sin, cos], 1)], 1)
    f_cols = f_cols.reshape(2, P, 2, 2 * MODES).transpose(1, 0, 2, 3)
    g_cols = np.concatenate([(cos * double).T, -(sin * double).T], 0)
    g_rows = np.concatenate([cos.T, -sin.T], 0).reshape(2 * MODES, 2, P)
    zeros = P - 2 * MODES
    g_cols = np.pad(g_cols, ((0, zeros), (0, 0)))
    g_rows = np.pad(g_rows, ((0, zeros), (0, 0), (0, 0)))
    out = {"f_rows": f_rows, "f_cols": f_cols, "g_cols": g_cols, "g_rows": g_rows,
           "average_all": np.full((P, P), 1.0 / P)}
    return {n: np.ascontiguousarray(v, dtype=np.float32) for n, v in out.items()}


DILATIONS = (1, 6, 12, 18)
GROUP = C // len(DILATIONS)
SLOTS = P // GROUP
RUN = SLOTS - 2
MARGIN = max(DILATIONS)


def dilated_rows(d):
    columns = []
    for k in range(-(-H // (RUN * d))):
        for f in range(d):
            row = k * RUN * d + f - d
            inside = [s for s in range(SLOTS) if 0 <= row + s * d < H]
            if inside[-1] > 0:
                columns.append((inside[0], inside[-1]))
    return columns


def dilated_parts(d):
    parts = []
    for i, (_, last) in enumerate(dilated_rows(d)):
        last = min(last, RUN)
        if parts and parts[-1][2] == last:
            parts[-1][1] = i + 1
        else:
            parts.append([i, i + 1, last])
    return parts


NPARTS = 3


def channel_layout_stores(stats_dram, B):
    def stores(result):
        src = result[0:GROUP, :, :].rearrange("c (b q) k -> c b q k", b=B)
        dst = stats_dram.rearrange("b (q c) k -> c b q k", c=GROUP)
        return [(dst[:, b, :, :], src[:, b, :, :]) for b in range(B)]
    return stores


def dilated_conv(nc, x, y, taps_dram, bias_dram, stats_dram, slot_masks, moments, B):
    NG = len(DILATIONS)
    NX = 3
    PAIR = BANK // W
    LARGEST = 24
    rows = [dilated_rows(d) for d in DILATIONS]
    chunks = []
    for g, d in enumerate(DILATIONS):
        n = len(rows[g])
        size = LARGEST // d * d if d > 1 else PAIR * (-(-n // (2 * PAIR)))
        chunks += [(g, c, min(c + size, n)) for c in range(0, n, size)]
    NC = len(chunks)
    assert NC % NX == 0
    items = [[(g, c, min(c + PAIR, c1)) for c in range(c0, c1, PAIR)] for g, c0, c1 in chunks]
    ends = [sum(len(i) for i in items[:n + 1]) for n in range(NC)]
    NI = ends[-1]

    def pieces(c, output):
        g, c0, c1 = chunks[c]
        d = DILATIONS[g]
        found = []
        for s in (range(1, RUN + 1) if output else range(SLOTS)):
            for k in range(c0 // d, -(-c1 // d)):
                n = sum(a <= s <= z for a, z in rows[g][k * d:(k + 1) * d])
                if n:
                    first = k * RUN * d + (s - 1) * d
                    before = found[-1] if found else None
                    if (before and before[0] == s and before[3] == n == d
                            and (d == 1 or before[4] + (before[2] + 1) * RUN * d <= H)):
                        before[2] += 1
                    else:
                        found.append([s, k * d - c0, 1, n, first])
        return found

    loads = [pieces(c, False) for c in range(NC)]
    stores = [pieces(c, True) for c in range(NC)]

    def finished(dmas, b, c):
        own = [16 * len(dmas[m]) for m in range(c % NX, NC, NX)]
        return b * sum(own) + sum(own[:c // NX + 1])

    kinds = [sorted(set(rows[g])) for g in range(NG)]
    assert all((0, SLOTS - 1) in kinds[g] for g in range(NG))
    NK = max(len(k) for k in kinds)

    with Stage(nc, "dil") as s:
        raw = [s.sbuf(f"raw{i}", [P, LARGEST, W]) for i in range(NX)]
        normed = [s.sbuf(f"normed{i}", [P, LARGEST, W + 2 * MARGIN]) for i in range(NX)]
        taps = s.sbuf("taps", [P, NG, 3, P])
        bias = s.sbuf("bias", [P, NG])
        masks = s.sbuf("masks", [P, SLOTS, SLOTS])
        norm = s.sbuf("norm", [P, B, NG, 2])
        norm_of = s.sbuf("norm_of", [P, NG, NK, B, 2])
        stats = s.sbuf("stats", [P, max(ends), 6])
        image_moments = s.sbuf("image_moments", [P, NPARTS, NG, 2])
        ps = [s.psum(f"ps{i}", [P, PAIR, W]) for i in range(8)]
        cleared = s.sem("cleared")
        consts_loaded = s.sem("consts_loaded")
        kinds_ready = s.sem("kinds_ready")
        loaded = [s.sem(f"loaded{i}") for i in range(NX)]
        stored = [s.sem(f"stored{i}") for i in range(NX)]
        may_normalise = s.sem("may_normalise")
        normed_ready = s.sem("normed_ready")
        item_done = s.sem("item_done")
        item_added = s.sem("item_added")
        out_ready = s.sem("out_ready")
        may_aggregate = s.sem("may_aggregate")
        aggregated = s.sem("aggregated")
        block = s.block()

        def transfers(dram, b, c, dmas):
            g = chunks[c][0]
            step = RUN * DILATIONS[g]
            for slot, at, blocks, n, first in dmas[c]:
                v = dram[b, g * GROUP:(g + 1) * GROUP, :, :]
                tile = raw[c % NX][slot * GROUP:(slot + 1) * GROUP, at:at + blocks * n, :]
                if n == 1:
                    yield v[:, first:first + (blocks - 1) * step + 1:step, :], tile
                elif blocks == 1:
                    yield v[:, first:first + n, :], tile
                else:
                    v = v[:, first:first + blocks * step, :].rearrange("c (k r) w -> c k r w", r=step)
                    yield v[:, :, 0:n, :], tile.rearrange("c (k r) w -> c k r w", r=n)

        @block.sync
        def _(sp):
            sp.wait_ge(cleared, 2 * NX + 1)
            for s_out in range(1, RUN + 1):
                for kh in range(3):
                    s_in = s_out + kh - 1
                    sp.dma_start(taps[s_in * GROUP:(s_in + 1) * GROUP, :, :, s_out * GROUP:(s_out + 1) * GROUP],
                                 taps_dram[:, :, 3 * kh:3 * kh + 3, :]).then_inc(consts_loaded, 16)
            for slot in range(SLOTS):
                mine = slice(slot * GROUP, (slot + 1) * GROUP)
                sp.dma_start(bias[mine, :], bias_dram).then_inc(consts_loaded, 16)
                sp.dma_start(norm[mine, :, :, :], stats_dram.rearrange("b (g c) k -> c b g k", c=GROUP)
                             ).then_inc(consts_loaded, 16)
            sp.dma_start(masks[:, :, :], slot_masks).then_inc(consts_loaded, 16)

            def load(b, c):
                for src, dst in transfers(x, b, c, loads):
                    sp.dma_start(dst, src).then_inc(loaded[c % NX], 16)

            def store(b, c):
                for dst, src in transfers(y, b, c, stores):
                    sp.dma_start(dst, src).then_inc(stored[c % NX], 16)

            AHEAD = NX - 1
            for c in range(AHEAD):
                load(0, c)

            def image(b, first, last):
                for c in range(NC):
                    sp.wait_ge(out_ready, b * NC + c + 1)
                    store(b, c)
                    if c + AHEAD < NC or not last:
                        if c > 0:
                            sp.wait_ge(stored[(c - 1) % NX], finished(stores, b, c - 1))
                        elif not first:
                            sp.wait_ge(stored[NX - 1], finished(stores, b - 1, NC - 1))
                        if c + AHEAD < NC:
                            load(b, c + AHEAD)
                        else:
                            load(b + 1, c + AHEAD - NC)

            image(0, True, B == 1)
            if B > 2:
                with sp.Fori(1, B - 1) as b:
                    image(b, False, False)
            if B > 1:
                image(B - 1, False, True)
            for n in range(NX):
                sp.wait_ge(stored[n], finished(stores, B - 1, NC - NX + n))

        @block.gpsimd
        def _(pool):
            for i in range(NX):
                nc.gpsimd.memset(normed[i][:, :, :], 0.0).then_inc(cleared, 1)

        @block.scalar
        def _(act):
            act.wait_ge(kinds_ready, 1)
            with act.Fori(0, B) as b:
                for c, (g, c0, c1) in enumerate(chunks):
                    i = c % NX
                    act.wait_ge(loaded[i], finished(loads, b, c))
                    act.wait_ge(item_done, b * NI + (ends[c - NX] + NI if c >= NX else ends[c - NX]))
                    nc.scalar.sem_inc(may_normalise, 1)
                    j = c0
                    while j < c1:
                        end = j
                        while end < c1 and rows[g][end] == rows[g][j]:
                            end += 1
                        scale = norm_of[:, g, kinds[g].index(rows[g][j]), b, :]
                        last = nc.scalar.activation(normed[i][:, j - c0:end - c0, MARGIN:MARGIN + W],
                                                    raw[i][:, j - c0:end - c0, :], ACT.Identity,
                                                    scale=scale[:, 0:1], bias=scale[:, 1:2])
                        j = end
                    last.then_inc(normed_ready, 1)

        @block.tensor
        def _(pe):
            nc.tensor.sem_inc(item_done, NI)
            pe.wait_ge(consts_loaded, 16 * (RUN * 3 + SLOTS * 2 + 1))
            with pe.Fori(0, B) as b:
                m = 0
                for c, (g, c0, _) in enumerate(chunks):
                    d = DILATIONS[g]
                    pe.wait_ge(normed_ready, b * NC + c + 1)
                    for _, j0, j1 in items[c]:
                        if m == 0:
                            pe.wait_ge(item_added, b * NI + 1)
                        elif m >= 8:
                            pe.wait_ge(item_added, b * NI + (m - 8 + 1) + 1)
                        for kw in range(3):
                            col = MARGIN + (kw - 1) * d
                            last = nc.tensor.matmul(ps[m % 8][:, 0:j1 - j0, :], taps[:, g, kw, :],
                                                    normed[c % NX][:, j0 - c0:j1 - c0, col:col + W],
                                                    start=(kw == 0), stop=(kw == 2))
                        last.then_inc(item_done, 1)
                        m += 1

        @block.vector
        def _(dve):
            for i in range(NX):
                nc.vector.memset(raw[i][:, :, :], 0.0).then_inc(cleared, 1)
            nc.vector.memset(image_moments[:, :, :, :], 0.0)
            nc.vector.memset(taps[:, :, :, :], 0.0).then_inc(cleared, 1)
            nc.vector.sem_inc(item_added, 1)
            dve.wait_ge(consts_loaded, 16 * (RUN * 3 + SLOTS * 2 + 1))
            for g in range(NG):
                for k, (lo, hi) in enumerate(kinds[g]):
                    last = nc.vector.tensor_scalar(norm_of[:, g, k, :, :], norm[:, :, g, :],
                                                   masks[:, lo, hi:hi + 1], None, ALU.mult)
            last.then_inc(kinds_ready, 1)
            mo = moments[:, :, :, :].rearrange("p m (b q) k -> p m b q k", b=B)
            with dve.Fori(0, B) as b:
                m = 0
                for c, (g, c0, c1) in enumerate(chunks):
                    for _, j0, j1 in items[c]:
                        dve.wait_ge(item_done, b * NI + m + 1 + NI)
                        here = raw[c % NX][:, j0 - c0:j1 - c0, :]
                        nc.vector.scalar_tensor_tensor(here, ps[m % 8][:, 0:j1 - j0, :], bias[:, g:g + 1], here,
                                                       ALU.add, ALU.add).then_inc(item_added, 1)
                        dve.wait_ge(item_added, b * NI + m + 1 + 1)
                        last = nc.vector.bn_stats(stats[:, m, :], here)
                        m += 1
                    last.then_inc(out_ready, 1)
                    if c1 == len(rows[g]):
                        dve.wait_ge(out_ready, b * NC + c + 1)
                        nc.vector.sem_inc(may_aggregate, 1)
                        m0 = m - -(-c1 // PAIR)
                        for part, (j0, j1, _) in enumerate(dilated_parts(DILATIONS[g])):
                            last = nc.vector.bn_aggr(image_moments[:, part, g, :],
                                                     stats[:, m0 + j0 // PAIR:m0 + -(-j1 // PAIR), :])
                        if g == NG - 1:
                            last.then_inc(aggregated, 1)
                dve.wait_ge(aggregated, b + 1)
                for part in range(NPARTS):
                    nc.vector.tensor_copy(mo[:, part, b, :, :], image_moments[:, part, :, :])


def dilated_constants():
    slot = np.arange(P) // GROUP
    pair = np.arange(P) % GROUP // 2
    first, last = np.meshgrid(np.arange(SLOTS), np.arange(SLOTS), indexing="ij")
    masks = (slot[:, None, None] >= first) & (slot[:, None, None] <= last)
    weights = np.zeros((P, NPARTS, len(DILATIONS)))
    for g, d in enumerate(DILATIONS):
        for part, (j0, j1, last) in enumerate(dilated_parts(d)):
            weights[:, part, g] = ((slot >= 1) & (slot <= last)) * (j1 - j0) / (2.0 * H)
    assert np.allclose(weights.sum((0, 1)), C // len(DILATIONS) // 2)
    out = {"sum_pairs": pair[:, None] == pair[None, :], "slot_masks": masks, "part_weights": weights}
    return {n: np.ascontiguousarray(v, dtype=np.float32) for n, v in out.items()}


KS = 7
KR = KS // 2


def depthwise_mish(nc, x, y, consts, kernel_all, kernel_halo, stats_dram, moments, B):
    NS, NU = 4, 4
    UC = CT // 2
    HALO = (0, 32)
    with Stage(nc, "dw") as s:
        x_tile = [s.sbuf(f"x{i}", [P, 2, CT, W]) for i in range(NS)]
        norm = [s.sbuf(f"norm{i}", [P, CT, 2]) for i in range(NS)]
        padded = [s.sbuf(f"padded{i}", [P, 2, CT, W + 2 * KR]) for i in range(2)]
        edge = [s.sbuf(f"edge{i}", [P, CT, W]) for i in range(2)]
        band = s.sbuf("band", [P, KS, P])
        band_edge = s.sbuf("band_edge", [P, 2, P])
        k_all = s.sbuf("k_all", [P, KS * KS])
        k_halo = s.sbuf("k_halo", [P, KS])
        place = s.sbuf("place", [P, KS, P])
        place_halo = s.sbuf("place_halo", [P, 2, KS, P])
        capped = [s.sbuf(f"capped{i}", [P, UC, W]) for i in range(2)]
        power = [s.sbuf(f"power{i}", [P, UC, W]) for i in range(2)]
        denom = [s.sbuf(f"denom{i}", [P, UC, W]) for i in range(2)]
        numer = [s.sbuf(f"numer{i}", [P, UC, W]) for i in range(2)]
        recip = [s.sbuf(f"recip{i}", [P, UC, W]) for i in range(2)]
        stats = s.sbuf("stats", [P, CT // 2, 2, 6])
        image_moments = s.sbuf("image_moments", [P, GROUPS, 2])
        ps = [s.psum(f"ps{i}", [P, UC, W]) for i in range(NU)]
        consts_loaded = s.sem("consts_loaded")
        cleared = s.sem("cleared")
        bands_ready = s.sem("bands_ready")
        step = s.sem("step")
        x_loaded = [s.sem(f"x_loaded{i}") for i in range(NS)]
        y_stored = [s.sem(f"y_stored{i}") for i in range(NS)]
        normalised = s.sem("normalised")
        edges_loaded = [s.sem(f"edges_loaded{i}") for i in range(2)]
        padded_used = s.sem("padded_used")
        conv_done = s.sem("conv_done")
        cap_ready = s.sem("cap_ready")
        exp_ready = s.sem("exp_ready")
        numer_ready = s.sem("numer_ready")
        denom_ready = s.sem("denom_ready")
        log_ready = s.sem("log_ready")
        recip_ready = s.sem("recip_ready")
        chain = s.sem("chain")
        unit_free = s.sem("unit_free")
        y_ready = s.sem("y_ready")
        may_aggregate = s.sem("may_aggregate")
        aggregated = s.sem("aggregated")
        summed = s.sem("summed")
        may_copy = s.sem("may_copy")
        may_normalise = s.sem("may_normalise")
        CH = 3
        XL = 16 * 3
        block = s.block()

        def rows_of(dram, b, t):
            return dram[b, t * CT:(t + 1) * CT, :, :].rearrange("c (f h) w -> f h c w", f=2)

        def images(eng, image):
            image(0, True, B == 1)
            if B > 2:
                with eng.Fori(1, B - 1) as b:
                    image(b, False, False)
            if B > 1:
                image(B - 1, False, True)

        @block.sync
        def _(sp):
            for dst, src in ((k_all[:, :], kernel_all), (place[:, :, :], consts["place"]),
                             (place_halo[:, :, :, :], consts["place_halo"]), (k_halo[:, :], kernel_halo)):
                sp.dma_start(dst, src).then_inc(consts_loaded, 16)

            def load(b, t, first=False):
                n = t % NS
                if not first:
                    sp.wait_ge(y_stored[n], b * (32 * NT // NS) + 32 * (t // NS))
                for half in range(2):
                    sp.dma_start(x_tile[n][:, half, :, :], rows_of(x, b, t)[half]).then_inc(x_loaded[n], 16)
                sp.dma_start(norm[n][:, :, :], stats_dram[b, t * CT:(t + 1) * CT, :].partition_broadcast(P)
                             ).then_inc(x_loaded[n], 16)

            AHEAD = NS - 1
            for t in range(AHEAD):
                load(0, t, True)

            def image(b, first, last):
                for t in range(NT):
                    sp.wait_ge(y_ready, b * NT + t + 1)
                    for half in range(2):
                        sp.dma_start(rows_of(y, b, t)[half], x_tile[t % NS][:, half, :, :]
                                     ).then_inc(y_stored[t % NS], 16)
                    nt = t + AHEAD
                    if nt < NT:
                        load(b, nt, first and nt < NS)
                    elif not last:
                        load(b + 1, nt - NT)

            images(sp, image)
            for n in range(NS):
                sp.wait_ge(y_stored[n], 32 * (B * NT // NS))

        @block.gpsimd
        def _(pool):
            for i in range(2):
                nc.gpsimd.memset(padded[i][:, :, :, :], 0.0)
                nc.gpsimd.memset(edge[i][:, :, :], 0.0).then_inc(cleared, 1)
            pool.wait_ge(cleared, 2)
            with pool.Fori(0, B) as b:
                for t in range(NT):
                    i = t % 2
                    pool.wait_ge(normalised, b * NT + t + 1)
                    nc.gpsimd.sem_inc(may_copy, 1)
                    for kw in range(KS):
                        p0 = HALO[0] + KR * kw
                        pool.dma_start(edge[i][p0:p0 + KR, :, :], padded[i][0:KR, 1, :, kw:kw + W]
                                       ).then_inc(edges_loaded[i], 16)
                        p1 = HALO[1] + KR * kw
                        pool.dma_start(edge[i][p1:p1 + KR, :, :], padded[i][P - KR:P, 0, :, kw:kw + W]
                                       ).then_inc(edges_loaded[i], 16)

        @block.scalar
        def _(act):
            act.wait_ge(cleared, 2)

            def normalise(b, t):
                i, n = t % 2, t % NS
                act.wait_ge(x_loaded[n], b * (XL * NT // NS) + XL * (t // NS) + XL)
                act.wait_ge(padded_used, b * NT + t + 1)
                nc.scalar.sem_inc(may_normalise, 1)
                for j in range(CT // 2):
                    for half in range(2):
                        last = nc.scalar.activation(
                            padded[i][:, half, 2 * j:2 * j + 2, KR:KR + W], x_tile[n][:, half, 2 * j:2 * j + 2, :],
                            ACT.Identity, scale=norm[n][:, 2 * j, 0:1], bias=norm[n][:, 2 * j, 1:2])
                last.then_inc(normalised, 1)

            normalise(0, 0)

            def image(b, first, last):
                for t in range(NT):
                    for u in range(NU):
                        at = b * (NT * NU) + t * NU + u
                        i = u % 2
                        act.wait_ge(cap_ready, at + 1)
                        nc.scalar.activation(power[i][:, :, :], capped[i][:, :, :], ACT.Exp).then_inc(exp_ready, 1)
                        act.wait_ge(denom_ready, at + 1)
                        nc.scalar.activation(recip[i][:, :, :], denom[i][:, :, :], ACT.Ln).then_inc(log_ready, 1)
                        act.wait_ge(log_ready, at + 1)
                        nc.scalar.activation(recip[i][:, :, :], recip[i][:, :, :], ACT.Exp, scale=-1.0
                                             ).then_inc(recip_ready, 1)
                        if u == 0 and t < NT - 1:
                            normalise(b, t + 1)
                        elif u == 0 and not last:
                            normalise(b + 1, 0)

            images(act, image)

        @block.tensor
        def _(pe):
            nc.tensor.sem_inc(padded_used, 2)
            pe.wait_ge(bands_ready, 1)
            with pe.Fori(0, B) as b:
                for t in range(NT):
                    i = t % 2
                    pe.wait_ge(normalised, b * NT + t + 1)
                    pe.wait_ge(edges_loaded[i], b * (16 * 2 * KS * NT // 2) + 16 * 2 * KS * (t // 2 + 1))
                    for u in range(NU):
                        part, half = divmod(u, 2)
                        pe.wait_ge(unit_free, b * (NT * NU) + t * NU + u + 1)
                        for j in range(UC // 2):
                            c0 = part * UC + 2 * j
                            for kw in range(KS):
                                nc.tensor.matmul(ps[u][:, 2 * j:2 * j + 2, :], band[:, kw, :],
                                                 padded[i][:, half, c0:c0 + 2, kw:kw + W],
                                                 start=(kw == 0), stop=False)
                            last = nc.tensor.matmul(ps[u][:, 2 * j:2 * j + 2, :], band_edge[:, half, :],
                                                    edge[i][:, c0:c0 + 2, :], start=False, stop=True)
                        last.then_inc(conv_done, 1)
                    pe.wait_ge(conv_done, b * (NT * NU) + (t + 1) * NU)
                    nc.tensor.sem_inc(padded_used, 1)

        @block.vector
        def _(dve):
            done = [0]

            def chained(instruction):
                done[0] += 1
                instruction.then_inc(step, 1)
                dve.wait_ge(step, done[0])

            dve.wait_ge(consts_loaded, 64)
            for a in range(KS):
                for kw in range(KS):
                    w = k_all[:, a * KS + kw:a * KS + kw + 1]
                    if a == 0:
                        last = nc.vector.tensor_scalar(band[:, kw, :], place[:, a, :], w, None, ALU.mult)
                    else:
                        last = nc.vector.scalar_tensor_tensor(band[:, kw, :], place[:, a, :], w, band[:, kw, :],
                                                              ALU.mult, ALU.add)
                for half in range(2):
                    w = k_halo[:, a:a + 1]
                    src = place_halo[:, half, a, :]
                    if a == 0:
                        last = nc.vector.tensor_scalar(band_edge[:, half, :], src, w, None, ALU.mult)
                    else:
                        last = nc.vector.scalar_tensor_tensor(band_edge[:, half, :], src, w, band_edge[:, half, :],
                                                              ALU.mult, ALU.add)
                if a < KS - 1:
                    chained(last)
            last.then_inc(bands_ready, 1)
            nc.vector.sem_inc(unit_free, NU)
            mo = moments[:, :, :].rearrange("p (b g) k -> p b g k", b=B)
            with dve.Fori(0, B) as b:
                for t in range(NT):
                    n = t % NS

                    def place_of(u):
                        part, half = divmod(u, 2)
                        return b * (NT * NU) + t * NU + u, part, half, u % 2

                    def cap(u):
                        at, _, _, i = place_of(u)
                        dve.wait_ge(conv_done, at + 1)
                        nc.vector.tensor_scalar(capped[i][:, :, :], ps[u][:, :, :], 20.0, None, ALU.min
                                                ).then_inc(cap_ready, 1)

                    def fraction(u):
                        at, _, _, i = place_of(u)
                        e, top = power[i][:, :, :], numer[i][:, :, :]
                        dve.wait_ge(exp_ready, at + 1)
                        nc.vector.scalar_tensor_tensor(top, e, 2.0, e, ALU.add, ALU.mult).then_inc(numer_ready, 1)
                        dve.wait_ge(numer_ready, at + 1)
                        nc.vector.tensor_scalar(denom[i][:, :, :], top, 2.0, None, ALU.add).then_inc(denom_ready, 1)
                        nc.vector.tensor_tensor(top, ps[u][:, :, :], top, ALU.mult).then_inc(unit_free, 1)

                    def finish(u):
                        at, part, half, i = place_of(u)
                        c0 = part * UC
                        here = x_tile[n][:, half, c0:c0 + UC, :]
                        down, top, r = denom[i][:, :, :], numer[i][:, :, :], recip[i][:, :, :]
                        dve.wait_ge(recip_ready, at + 1)
                        nc.vector.tensor_tensor(down, down, r, ALU.mult).then_inc(chain, 1)
                        dve.wait_ge(chain, at * CH + 1)
                        nc.vector.scalar_tensor_tensor(down, down, 2.0, r, ALU.subtract, ALU.mult).then_inc(chain, 1)
                        dve.wait_ge(chain, at * CH + 2)
                        dve.wait_ge(unit_free, at + 1 + NU)
                        nc.vector.tensor_tensor(top, top, down, ALU.mult).then_inc(chain, 1)
                        dve.wait_ge(chain, at * CH + 3)
                        nc.vector.tensor_tensor(here, here, top, ALU.subtract).then_inc(summed, 1)
                        dve.wait_ge(summed, at + 1)
                        for j in range(UC // 2):
                            last = nc.vector.bn_stats(stats[:, part * UC // 2 + j, half, :],
                                                      x_tile[n][:, half, c0 + 2 * j:c0 + 2 * j + 2, :])
                        return last

                    for u in range(NU):
                        cap(u)
                        if u > 0:
                            finish(u - 1)
                        fraction(u)
                    last = finish(NU - 1)
                    last.then_inc(y_ready, 1)
                    dve.wait_ge(y_ready, b * NT + t + 1)
                    nc.vector.sem_inc(may_aggregate, 1)
                    for j in range(CT // 2):
                        last = nc.vector.bn_aggr(image_moments[:, t * CT // 2 + j, :], stats[:, j, :, :])
                last.then_inc(aggregated, 1)
                dve.wait_ge(aggregated, b + 1)
                nc.vector.tensor_copy(mo[:, b, :, :], image_moments[:, :, :])


def mish_constants():
    src, dst = np.arange(P)[:, None], np.arange(P)[None, :]
    place = np.stack([(src - dst + KR == a) for a in range(KS)], 1)
    halo = np.zeros((P, 2, KS, P))
    for kw in range(KS):
        for r in range(KR):
            for a in range(KS):
                halo[KR * kw + r, 0, a] = (P + r - np.arange(P) + KR == a)
                halo[32 + KR * kw + r, 1, a] = (r - np.arange(P) == a)
    return {n: np.ascontiguousarray(v, dtype=np.float32) for n, v in (("place", place), ("place_halo", halo))}


def mish_kernels(kernel):
    turned = kernel[::-1, ::-1]
    k_all = np.broadcast_to(turned.reshape(1, KS * KS), (P, KS * KS))
    k_halo = np.zeros((P, KS), kernel.dtype)
    for first in (0, 32):
        k_halo[first:first + KR * KS] = np.repeat(turned.T, KR, axis=0)
    return np.ascontiguousarray(k_all), k_halo


PATCH = 8
CIN = 384


def patch_filter_block(nc, x, y, consts, w_in, w_dw, filt, w_out, stats_dram, B):
    S = H // PATCH
    NB = 4
    LEAD = 3
    HW_ = W // 2
    NJ = HW_ // (2 * PATCH)
    BJ = NJ // 2
    CTS = CIN // P
    RU = 4
    TAPS = [(0, 0), (0, 2), (2, 0), (2, 2), (0, 1), (2, 1), (1, 0), (1, 2), (1, 1)]
    UNITS = [(0, 0), (0, 1), (0, 2), (1, 2), (1, 0), (1, 1)]
    NUN = len(UNITS)
    NPE = 3
    NCHAIN = len(TAPS) - NPE - 1
    with Stage(nc, "l3") as s:
        x_in = [s.sbuf(f"x_in{i}", [P, PATCH, HW_]) for i in range(2)]
        x_res = [s.sbuf(f"x_res{i}", [P, PATCH, HW_]) for i in range(2)]
        normed = s.sbuf("normed", [P, NJ, PATCH, 2 * PATCH])
        grid = [s.sbuf(f"grid{i}", [P, CTS, PATCH + 2, W + 2]) for i in range(NB)]
        turned = s.sbuf("turned", [P, BJ, P])
        spectrum = s.sbuf("spectrum", [P, BJ, P])
        wide = s.sbuf("wide", [P, 2, BJ, CIN])
        acc = [[s.sbuf(f"acc{r}{c}", [P, RU, W]) for c in range(CTS)] for r in range(2)]
        gated = [s.sbuf(f"gated{r}", [P, RU, W]) for r in range(2)]
        norm = s.sbuf("norm", [P, B, 2])
        zero = s.sbuf("zero", [P, 1, 1])
        ident = s.sbuf("ident", [P, P])
        to_freq = s.sbuf("to_freq", [P, P])
        to_pixel = s.sbuf("to_pixel", [P, P])
        gain = s.sbuf("gain", [P, CIN])
        w_in_s = s.sbuf("w_in", [P, 2, CIN])
        w_dw_s = s.sbuf("w_dw", [P, CTS, 9])
        diag = s.sbuf("diag", [P, CTS, NPE, P])
        w_out_s = s.sbuf("w_out", [P, 2, C])
        spread = x_in[0][0:40, 0, 0:P]
        filt_s = x_in[1][0:40, 0:3, :]
        ps_turn = s.psum("ps_turn", [P, BJ, P])
        ps_out = s.psum("ps_out", [P, RU, HW_])
        ps_wide = [s.psum(f"ps_wide{i}", [P, BANK]) for i in range(2)]
        ps_grid = [s.psum(f"ps_grid{i}", [P, BJ, PATCH, 2 * PATCH]) for i in range(2)]
        ps_taps = s.psum("ps_taps", [P, RU, W])
        consts_loaded = s.sem("consts_loaded")
        cleared = s.sem("cleared")
        gain_done = s.sem("gain_done")
        gain_ready = s.sem("gain_ready")
        in_loaded = [s.sem(f"in_loaded{i}") for i in range(2)]
        res_loaded = [s.sem(f"res_loaded{i}") for i in range(2)]
        y_stored = [s.sem(f"y_stored{i}") for i in range(2)]
        may_normalise = s.sem("may_normalise")
        normed_ready = s.sem("normed_ready")
        turned_done = s.sem("turned_done")
        turned_ready = s.sem("turned_ready")
        spectrum_done = s.sem("spectrum_done")
        spectrum_ready = s.sem("spectrum_ready")
        wide_done = s.sem("wide_done")
        wide_copied = s.sem("wide_copied")
        wide_ready = s.sem("wide_ready")
        grid_done = s.sem("grid_done")
        grid_ready = s.sem("grid_ready")
        halo_ready = s.sem("halo_ready")
        taps_done = s.sem("taps_done")
        taps_copied = s.sem("taps_copied")
        chain = s.sem("chain")
        unit_ready = s.sem("unit_ready")
        gelu_ready = s.sem("gelu_ready")
        gate_ready = s.sem("gate_ready")
        out_done = s.sem("out_done")
        y_ready = s.sem("y_ready")
        block = s.block()
        UNIT0 = NB * NUN
        NSMALL = 10
        GATES = 4

        def strips_of(dram, b, q):
            v = dram[b].rearrange("c (q r) (f w) -> q f c r w", r=PATCH, f=2)
            return v[q]

        def steps(eng, step):
            for q in range(LEAD):
                step(None, (0, q, q), (0, q - 1, q - 1) if q else None, None)

            def inner(b, q, i, first=False):
                step((b, q, i), (b, q + LEAD, (i + LEAD) % NB), (b, q + LEAD - 1, (i + LEAD - 1) % NB),
                     None if first else (b, q - 1, (i - 1) % NB))

            def image(b, first, last):
                if first:
                    for i in range(NB):
                        inner(b, i, i, i == 0)
                with eng.Fori(1 if first else 0, S // NB - 1) as j:
                    for i in range(NB):
                        inner(b, j * NB + i, i)
                for i in range(NB):
                    q = S - NB + i
                    ahead = []
                    for lead in (LEAD, LEAD - 1):
                        if q + lead < S:
                            ahead.append((b, q + lead, (i + lead) % NB))
                        else:
                            ahead.append(None if last else (b + 1, q + lead - S, (i + lead) % NB))
                    step((b, q, i), *ahead, (b, q - 1, (i - 1) % NB))
                if last:
                    step(None, None, None, (b, S - 1, NB - 1))

            image(0, True, B == 1)
            if B > 2:
                with eng.Fori(1, B - 1) as b:
                    image(b, False, False)
            if B > 1:
                image(B - 1, False, True)

        def edge(q, value):
            return isinstance(q, int) and q == value

        @block.sync
        def _(sp):
            small = [(spread, consts["spread"]), (filt_s.rearrange("p a b -> p (a b)"), filt),
                     (ident[:, :], consts["ident"]), (to_freq[:, :], consts["to_freq"]),
                     (to_pixel[:, :], consts["to_pixel"]), (w_dw_s[:, :, :], w_dw)]
            sp.wait_ge(cleared, 2)
            for half in range(2):
                hp = slice(half * C, (half + 1) * C)
                small += [(norm[hp, :, :], stats_dram.rearrange("b c k -> c b k")), (w_in_s[hp, half, :], w_in)]
            small += [(w_out_s[:, 0, :], w_out[0:P, :]), (w_out_s[C:P, 1, :], w_out[P:P + C, :])]
            for dst, src in small:
                sp.dma_start(dst, src).then_inc(consts_loaded, 16)
            assert len(small) == NSMALL + 2

            sp.wait_ge(gain_ready, 1)

            def load(tiles, i, b, q, done):
                for half in range(2):
                    sp.dma_start(tiles[i][half * C:(half + 1) * C, :, :], strips_of(x, b, q)[half]
                                 ).then_inc(done[i], 16)

            def next_in(b, q, i):
                if not (isinstance(b, int) and isinstance(q, int) and b == 0 and q < 2):
                    sp.wait_ge(normed_ready, b * S + q - 1)
                load(x_in, i, b, q, in_loaded)

            def next_res(b, q, i):
                if not (isinstance(b, int) and isinstance(q, int) and b == 0 and q < 2):
                    sp.wait_ge(y_stored[i], b * (32 * S // 2) + q // 2 * 32)
                load(x_res, i, b, q, res_loaded)

            def store(b, q, i):
                sp.wait_ge(y_ready, b * (2 * S) + q * 2 + 3)
                for half in range(2):
                    sp.dma_start(strips_of(y, b, q)[half], x_res[i][half * C:(half + 1) * C, :, :]
                                 ).then_inc(y_stored[i], 16)

            next_in(0, 0, 0)
            next_in(0, 1, 1)
            next_res(0, 0, 0)
            next_res(0, 1, 1)
            for q in range(2, LEAD + 2):
                next_in(0, q, q % 2)

            def step(b, q, i, last):
                store(b, q, i % 2)
                for fetch, ahead in ((next_res, 2), (next_in, LEAD + 2)):
                    if not isinstance(q, int) or q + ahead < S:
                        fetch(b, q + ahead, (i + ahead) % 2)
                    elif not last:
                        fetch(b + 1, q + ahead - S, (i + ahead) % 2)

            def image(b, last):
                tail = 2 * NB
                with sp.Fori(0, (S - tail) // NB) as j:
                    for i in range(NB):
                        step(b, j * NB + i, i, last)
                for q in range(S - tail, S):
                    step(b, q, q % NB, last)

            if B > 1:
                with sp.Fori(0, B - 1) as b:
                    image(b, False)
            image(B - 1, True)
            for i in range(2):
                sp.wait_ge(y_stored[i], 32 * (B * S // 2))

        @block.gpsimd
        def _(pool):
            for r in range(2):
                nc.gpsimd.memset(gated[r][:, :, :], 0.0)
            for i in range(NB):
                nc.gpsimd.memset(grid[i][:, :, :, 0:1], 0.0)
                nc.gpsimd.memset(grid[i][:, :, :, W + 1:W + 2], 0.0)
            nc.gpsimd.memset(zero[:, :, :], 0.0).then_inc(cleared, 1)

        @block.scalar
        def _(act):
            nc.scalar.sem_inc(grid_ready, 2)
            nc.scalar.sem_inc(wide_copied, 2)
            nc.scalar.sem_inc(taps_copied, 1)
            act.wait_ge(consts_loaded, 16 * (NSMALL + 2))

            def step(conv, idft, late, prev):
                if idft:
                    b, q, i = idft
                    n = b * S + q

                def normalise():
                    act.wait_ge(in_loaded[i % 2], b * (32 * S // 2) + q // 2 * 32 + 32)
                    if not (isinstance(n, int) and n == 0):
                        act.wait_ge(turned_done, n * 2)
                    nc.scalar.sem_inc(may_normalise, 1)
                    nc.scalar.activation(normed[:, :, :, :].rearrange("p j r c -> p r j c"),
                                         x_in[i % 2][:, :, :].rearrange("p r (j c) -> p r j c", j=NJ),
                                         ACT.Identity, scale=norm[:, b, 0:1], bias=norm[:, b, 1:2]
                                         ).then_inc(normed_ready, 1)

                def turn_copy(k):
                    act.wait_ge(turned_done, n * 2 + k + 1)
                    nc.scalar.activation(turned[:, :, :], ps_turn[:, :, :], ACT.Copy).then_inc(turned_ready, 1)

                def spectrum_copy(k):
                    act.wait_ge(spectrum_done, n * 2 + k + 1)
                    nc.scalar.activation(spectrum[:, :, :], ps_turn[:, :, :], ACT.Copy).then_inc(spectrum_ready, 1)

                def wide_copies(k, half):
                    for j in range(BJ):
                        m = half * BJ + j
                        act.wait_ge(wide_done, n * (4 * BJ) + k * 2 * BJ + m + 1)
                        nc.scalar.activation(wide[:, half, j, :], ps_wide[m % 2][:, 0:CIN], ACT.Copy
                                             ).then_inc(wide_copied, 1)

                def taps_copy(u):
                    cb, cq, _ = conv
                    at = cb * S + cq
                    r, ct = UNITS[u]
                    if ct == 1:
                        act.wait_ge(out_done, at * 2 + r + 1)
                    else:
                        gates = {0: 1, 2: 2, 3: 3, 4: 4}[u]
                        act.wait_ge(gate_ready, at * GATES + gates)
                    act.wait_ge(taps_done, at * NUN + u + 1)
                    nc.scalar.activation(acc[r][ct][:, :, :], ps_taps[:, :, :], ACT.Copy).then_inc(taps_copied, 1)

                def grid_copies(strip, k, half):
                    b, q, i = strip
                    n = b * S + q
                    if k == 0 and half == 0:
                        act.wait_ge(unit_ready, n * NUN + NUN)
                    for ct in range(CTS):
                        g = half * CTS + ct
                        act.wait_ge(grid_done, n * (4 * CTS) + k * 2 * CTS + g + 1)
                        c0 = 1 + half * HW_ + k * BJ * 2 * PATCH
                        dst = grid[i][:, ct, 1:PATCH + 1, c0:c0 + BJ * 2 * PATCH]
                        nc.scalar.activation(dst.rearrange("p r (j c) -> p r j c", j=BJ),
                                             ps_grid[g % 2][:, :, :, :].rearrange("p j r c -> p r j c"),
                                             ACT.Copy).then_inc(grid_ready, 1)

                def halo_copies(strip):
                    b, q, i = strip
                    act.wait_ge(grid_ready, (b * S + q) * (4 * CTS) + 4 * CTS + 2)
                    before = (i - 1) % NB

                    def rows(g, r):
                        return grid[g][:, :, r, 1:W + 1]

                    none = zero[:, :, :].broadcast_to([P, CTS, W])
                    if edge(q, 0):
                        last = nc.scalar.activation(rows(i, 0), none, ACT.Copy)
                    else:
                        nc.scalar.activation(rows(i, 0), rows(before, PATCH), ACT.Copy)
                        last = nc.scalar.activation(rows(before, PATCH + 1), rows(i, 1), ACT.Copy)
                    if edge(q, S - 1):
                        last = nc.scalar.activation(rows(i, PATCH + 1), none, ACT.Copy)
                    last.then_inc(halo_ready, 1)

                def gelu(u):
                    cb, cq, _ = conv
                    r, ct = UNITS[u]
                    act.wait_ge(unit_ready, cb * (S * NUN) + cq * NUN + u + 1 + UNIT0)
                    if ct == 0:
                        nc.scalar.activation(acc[r][0][:, :, :], acc[r][0][:, :, :], ACT.Gelu).then_inc(gelu_ready, 1)
                    else:
                        nc.scalar.activation(gated[r][C:P, :, :], acc[r][2][0:C, :, :], ACT.Gelu
                                             ).then_inc(gelu_ready, 1)

                if idft:
                    normalise()
                if conv:
                    taps_copy(0)
                if late:
                    grid_copies(late, 1, 0)
                if idft:
                    turn_copy(0)
                if conv:
                    taps_copy(1)
                if late:
                    grid_copies(late, 1, 1)
                    halo_copies(late)
                if idft:
                    spectrum_copy(0)
                if conv:
                    gelu(0)
                    taps_copy(2)
                if idft:
                    wide_copies(0, 0)
                    turn_copy(1)
                if conv:
                    taps_copy(3)
                if idft:
                    wide_copies(0, 1)
                    spectrum_copy(1)
                    grid_copies(idft, 0, 0)
                if conv:
                    gelu(2)
                    taps_copy(4)
                if idft:
                    wide_copies(1, 0)
                    grid_copies(idft, 0, 1)
                if conv:
                    gelu(3)
                    taps_copy(5)
                if idft:
                    wide_copies(1, 1)
                if conv:
                    gelu(4)

            steps(act, step)

        @block.tensor
        def _(pe):
            pe.wait_ge(consts_loaded, 16 * (NSMALL + 2))
            nc.tensor.matmul(ps_wide[0][:, 0:CIN], spread, filt_s.rearrange("p a b -> p (a b)"), start=True, stop=True
                             ).then_inc(gain_done, 1)
            nc.tensor.sem_inc(out_done, 2)
            pe.wait_ge(gain_ready, 1)

            def step(conv, idft, late, prev):
                if idft:
                    b, q, i = idft
                    n = b * S + q
                if conv:
                    cb, cq, ci = conv
                    at = cb * S + cq

                def turn(k):
                    pe.wait_ge(normed_ready, n + 1)
                    pe.wait_ge(spectrum_ready, n * 2 + k)
                    for j in range(BJ):
                        last = nc.tensor.matmul(ps_turn[:, j, :],
                                                normed[:, k * BJ + j, :, :].rearrange("p r c -> p (r c)"),
                                                ident[:, :], start=True, stop=True, is_transpose=True)
                    last.then_inc(turned_done, 1)

                def transform(k):
                    pe.wait_ge(turned_ready, n * 2 + k + 1)
                    for j in range(BJ):
                        last = nc.tensor.matmul(ps_turn[:, j, :], turned[:, j, :], to_freq[:, :],
                                                start=True, stop=True)
                    last.then_inc(spectrum_done, 1)

                def project(k, half):
                    pe.wait_ge(spectrum_ready, n * 2 + k + 1)
                    for j in range(BJ):
                        m = half * BJ + j
                        pe.wait_ge(wide_copied, n * (4 * BJ) + k * 2 * BJ + m + 1)
                        nc.tensor.matmul(ps_wide[m % 2][:, 0:CIN], spectrum[:, j, :], w_in_s[:, half, :],
                                         start=True, stop=True).then_inc(wide_done, 1)

                def invert(strip, k, half):
                    n = strip[0] * S + strip[1]
                    pe.wait_ge(wide_ready, n * 4 + k * 2 + half + 1)
                    for ct in range(CTS):
                        g = half * CTS + ct
                        pe.wait_ge(grid_ready, n * (4 * CTS) + k * 2 * CTS + g + 1)
                        for j in range(BJ):
                            last = nc.tensor.matmul(ps_grid[g % 2][:, j, :, :], wide[:, half, j, ct * P:(ct + 1) * P],
                                                    to_pixel[:, :], start=True, stop=True)
                        last.then_inc(grid_done, 1)

                def taps(u):
                    r, ct = UNITS[u]
                    if u == 0:
                        pe.wait_ge(halo_ready, at + (1 if edge(cq, S - 1) else 2))
                    pe.wait_ge(taps_copied, at * NUN + u + 1)
                    for h in range(RU // 2):
                        for m, (kh, kw) in enumerate(TAPS[:NPE]):
                            r0 = r * RU + 2 * h + kh
                            last = nc.tensor.matmul(ps_taps[:, 2 * h:2 * h + 2, :], diag[:, ct, m, :],
                                                    grid[ci][:, ct, r0:r0 + 2, kw:kw + W],
                                                    start=(m == 0), stop=(m == NPE - 1))
                    last.then_inc(taps_done, 1)

                def output(strip, r):
                    at = strip[0] * S + strip[1]
                    pe.wait_ge(gate_ready, at * GATES + 2 * r + 2 + GATES)
                    pe.wait_ge(y_ready, at * 2 + r + 1)
                    for half in range(2):
                        cols = slice(half * HW_, (half + 1) * HW_)
                        dst = ps_out[half * C:(half + 1) * C, :, :]
                        nc.tensor.matmul(dst, w_out_s[:, 1, :], gated[r][:, :, cols], start=True, stop=False)
                        last = nc.tensor.matmul(dst, w_out_s[:, 0, :], acc[r][1][:, :, cols], start=False, stop=True)
                    last.then_inc(out_done, 1)

                if conv:
                    taps(0)
                if late:
                    invert(late, 1, 0)
                if idft:
                    turn(0)
                if conv:
                    taps(1)
                if prev:
                    output(prev, 1)
                if late:
                    invert(late, 1, 1)
                if idft:
                    transform(0)
                if conv:
                    taps(2)
                if idft:
                    project(0, 0)
                    turn(1)
                if conv:
                    taps(3)
                if idft:
                    project(0, 1)
                    transform(1)
                    invert(idft, 0, 0)
                if conv:
                    taps(4)
                if idft:
                    project(1, 0)
                    invert(idft, 0, 1)
                if conv:
                    taps(5)
                    output(conv, 0)
                if idft:
                    project(1, 1)

            steps(pe, step)

        @block.vector
        def _(dve):
            nc.vector.memset(w_in_s[:, :, :], 0.0)
            nc.vector.memset(w_out_s[:, :, :], 0.0).then_inc(cleared, 1)
            dve.wait_ge(consts_loaded, 16 * (NSMALL + 2))
            for ct in range(CTS):
                for m, (kh, kw) in enumerate(TAPS[:NPE]):
                    k = kh * 3 + kw
                    nc.vector.tensor_scalar(diag[:, ct, m, :], ident[:, :], w_dw_s[:, ct, k:k + 1], None, ALU.mult)
            dve.wait_ge(gain_done, 1)
            nc.vector.tensor_copy(gain[:, :], ps_wide[0][:, 0:CIN]).then_inc(gain_ready, 1)
            nc.vector.sem_inc(gate_ready, GATES)
            nc.vector.sem_inc(unit_ready, UNIT0)
            nc.vector.sem_inc(y_ready, 1)
            dve.wait_ge(gain_ready, 1)

            def step(conv, idft, late, prev):
                if idft:
                    b, q, i = idft
                    n = b * S + q
                if conv:
                    cb, cq, ci = conv
                    at = cb * S + cq

                def scale(k, half):
                    dve.wait_ge(wide_copied, n * (4 * BJ) + k * 2 * BJ + (half + 1) * BJ + 2)
                    nc.vector.tensor_tensor(wide[:, half, :, :], wide[:, half, :, :],
                                            gain[:, :].unsqueeze(1).broadcast_to([P, BJ, CIN]), ALU.mult
                                            ).then_inc(wide_ready, 1)

                def unit(u, extras=()):
                    r, ct = UNITS[u]
                    extras = list(extras)
                    for t, (kh, kw) in enumerate(TAPS[NPE:]):
                        src = grid[ci][:, ct, r * RU + kh:r * RU + kh + RU, kw:kw + W]
                        w = w_dw_s[:, ct, kh * 3 + kw:kh * 3 + kw + 1]
                        if t == 0:
                            dve.wait_ge(taps_copied, at * NUN + u + 2)
                        nc.vector.scalar_tensor_tensor(acc[r][ct][:, :, :], src, w, acc[r][ct][:, :, :],
                                                       ALU.mult, ALU.add
                                                       ).then_inc(chain if t < NCHAIN else unit_ready, 1)
                        if t >= 1 and extras:
                            extras.pop(0)()
                        if t < NCHAIN:
                            dve.wait_ge(chain, (at * NUN + u) * NCHAIN + t + 1)
                    for extra in extras:
                        extra()

                def gate(k, u_b):
                    r, ct = UNITS[u_b]
                    dve.wait_ge(unit_ready, at * NUN + u_b + 1 + UNIT0)
                    dve.wait_ge(gelu_ready, at * GATES + k + 1)
                    if ct == 1:
                        a, dst = acc[r][0][:, :, :], acc[r][1][:, :, :]
                        last = nc.vector.tensor_tensor(dst, dst, a, ALU.mult)
                    else:
                        a, dst = acc[r][2][C:P, :, :], gated[r][C:P, :, :]
                        last = nc.vector.tensor_tensor(dst, dst, a, ALU.mult)
                    last.then_inc(gate_ready, 1)

                def add_x(strip, r):
                    b, q, i = strip
                    if r == 0:
                        dve.wait_ge(res_loaded[i % 2], b * (32 * S // 2) + q // 2 * 32 + 32)
                    dve.wait_ge(out_done, (b * S + q) * 2 + r + 1 + 2)
                    here = x_res[i % 2][:, r * RU:(r + 1) * RU, :]
                    nc.vector.tensor_tensor(here, ps_out[:, :, :], here, ALU.add).then_inc(y_ready, 1)

                def scaled(k, half):
                    return [lambda: scale(k, half)] if idft else []

                last_rows = [lambda: add_x(prev, 1)] if prev else []
                if not conv:
                    for extra in last_rows + [e for k in range(2) for h in range(2) for e in scaled(k, h)]:
                        extra()
                    return
                wait_a_tap = [lambda: None]
                unit(0)
                unit(1, last_rows)
                gate(0, 1)
                unit(2, scaled(0, 0))
                unit(3, scaled(0, 1))
                gate(1, 2)
                unit(4, scaled(1, 0))
                gate(2, 3)
                unit(5, wait_a_tap * 3 + [lambda: add_x(conv, 0)] + scaled(1, 1))
                gate(3, 5)

            steps(dve, step)


def patch_constants():
    n = PATCH
    r, c = np.meshgrid(np.arange(n), np.arange(n), indexing="ij")
    basis, spread = [], []
    for kx, ky in [(kx, ky) for ky in range(n // 2 + 1) for kx in range(n)]:
        own = ky in (0, n // 2)
        mirror = (-kx) % n
        if own and mirror < kx:
            continue
        ang = 2 * np.pi * (kx * r + ky * c) / n
        gain = np.zeros((n, n // 2 + 1))
        gain[kx, ky] += 0.5 if own else 1.0
        gain[mirror, ky] += 0.5 if own else 0.0
        for f in [np.cos(ang)] + ([] if own and mirror == kx else [np.sin(ang)]):
            basis.append((f / np.linalg.norm(f)).ravel())
            spread.append(gain.ravel())
    basis = np.array(basis)
    assert basis.shape == (n * n, n * n) and np.allclose(basis @ basis.T, np.eye(n * n))
    to_freq = np.zeros((n, 2, n, 2, n * n))
    for patch in range(2):
        to_freq[:, patch, :, patch, :] = basis.T.reshape(n, n, n * n)
    to_freq = to_freq.reshape(P, P)
    out = {"ident": np.eye(P), "to_freq": to_freq, "to_pixel": to_freq.T,
           "spread": np.tile(np.array(spread).T, (1, 2))}
    return {k: np.ascontiguousarray(v, dtype=np.float32) for k, v in out.items()}


def channel_order():
    h = CIN // 2
    return np.r_[0:P, h:h + P, P:h, h + P:CIN]


def projection_layouts(w_in, w_dw, filt, w_out):
    order = channel_order()
    w_in = np.ascontiguousarray(w_in[order].T)
    w_dw = np.ascontiguousarray(w_dw.reshape(CIN, 9)[order].reshape(CIN // P, P, 9).transpose(1, 0, 2))
    filt = np.ascontiguousarray(filt.reshape(CIN, 40)[order].T)
    return w_in, w_dw, filt, np.ascontiguousarray(w_out.T)


def build(nc, B, x, w_real, w_imag, dil_taps, dil_bias, kernel_all, kernel_halo, w_in, w_dw, filt, w_out, consts, y):
    def scratch(name, shape):
        return nc.dram_tensor(name, shape, FP32, kind="Internal").ap()

    shape = [B, C, H, W]
    x1, x2, x3 = (scratch(f"x{i}", shape) for i in (1, 2, 3))
    stats = [scratch(f"norm{i}", [B, C, 2]) for i in range(4)]
    modes_mixed = scratch("modes_mixed", [2 * B, MODES * MODES, C])
    with Stage(nc, "layer0a") as s:
        moments = s.sbuf("moments", [P, B * GROUPS, 2])
        modes_in = s.sbuf("modes_in", [P, MODES, MODES, 2 * B])
        spectral_forward(nc, x, consts, moments, modes_in, B)
        finish_statistics(nc, "norm0", moments, B * GROUPS, consts["average_all"], row_layout_stores(stats[0], B))
        spectral_mix(nc, w_real, w_imag, stats[0], modes_in, modes_mixed, B)
    with Stage(nc, "layer0b") as s:
        moments = s.sbuf("moments", [P, B * GROUPS, 2])
        spectral_inverse(nc, x, x1, consts, modes_mixed, moments, B)
        finish_statistics(nc, "norm1", moments, B * GROUPS, consts["average_all"], row_layout_stores(stats[1], B))
    with Stage(nc, "layer1") as s:
        moments = s.sbuf("moments", [P, NPARTS, B * len(DILATIONS), 2])
        dilated_conv(nc, x1, x2, dil_taps, dil_bias, stats[1], consts["slot_masks"], moments, B)
        finish_statistics(nc, "norm2", moments, B * len(DILATIONS), consts["sum_pairs"],
                          channel_layout_stores(stats[2], B), consts["part_weights"])
    with Stage(nc, "layer2") as s:
        moments = s.sbuf("moments", [P, B * GROUPS, 2])
        depthwise_mish(nc, x2, x3, consts, kernel_all, kernel_halo, stats[2], moments, B)
        finish_statistics(nc, "norm3", moments, B * GROUPS, consts["average_all"], row_layout_stores(stats[3], B))
    patch_filter_block(nc, x3, y, consts, w_in, w_dw, filt, w_out, stats[3], B)


def kernel(x, L0_conv_weight_real, L0_conv_weight_imag, L1_conv_weight, L1_conv_bias, L2_conv_kernel,
           L3_conv_w_in, L3_conv_w_dw, L3_conv_fft_filter, L3_conv_w_out):
    import concourse.bacc as bacc
    from concourse.bass_utils import run_bass_kernel_spmd

    B = x.shape[0]
    consts = {**constants(), **dilated_constants(), **mish_constants(), **patch_constants()}
    kernel_all, kernel_halo = mish_kernels(np.asarray(L2_conv_kernel))
    w_in, w_dw, filt, w_out = projection_layouts(*map(np.asarray, (L3_conv_w_in, L3_conv_w_dw, L3_conv_fft_filter,
                                                                  L3_conv_w_out)))
    arrays = {
        "x": np.asarray(x), "w_real": np.asarray(L0_conv_weight_real), "w_imag": np.asarray(L0_conv_weight_imag),
        "dil_taps": np.asarray(L1_conv_weight).reshape(4, 16, 16, 9).transpose(2, 0, 3, 1),
        "dil_bias": np.asarray(L1_conv_bias).reshape(4, 16).T,
        "kernel_all": kernel_all, "kernel_halo": kernel_halo,
        "w_in": w_in, "w_dw": w_dw, "filt": filt, "w_out": w_out,
    }
    arrays = {f"in_{k}": np.ascontiguousarray(v) for k, v in arrays.items()}
    tables = {f"const_{k}": v for k, v in consts.items()}
    nc = bacc.Bacc("TRN2", target_bir_lowering=False, num_devices=1)

    def declare(name, a):
        return nc.dram_tensor(name, a.shape, mybir.dt.from_np(a.dtype), kind="ExternalInput").ap()

    ins = {k[3:]: declare(k, v) for k, v in arrays.items()}
    const_aps = {k[6:]: declare(k, v) for k, v in tables.items()}
    y = nc.dram_tensor("out_y", [B, C, H, W], FP32, kind="ExternalOutput").ap()
    build(nc, B, consts=const_aps, y=y, **ins)
    r = run_bass_kernel_spmd(nc, [{**arrays, **tables}], core_ids=[0])
    return r.results[0]["out_y"]
```
